# Optimizing a Trainium2 kernel written in Bass

```python
import numpy as np
import jax
import jax.numpy as jnp

def _softmax(x, axis=-1):
    return jax.nn.softmax(x, axis=axis)

def _gelu(x):
    return jax.nn.gelu(x, approximate=True)

def _silu(x):
    return jax.nn.silu(x)

def _sigmoid(x):
    return jax.nn.sigmoid(x)

def _layernorm(x, axis=-1, eps=1e-05):
    m = jnp.mean(x, axis=axis, keepdims=True)
    v = jnp.var(x, axis=axis, keepdims=True)
    return (x - m) / jnp.sqrt(v + eps)

def _scatter_add(tgt, idx, src, axis=0):
    return tgt.at[idx].add(src)

def _segment_sum(src, seg, n):
    return jax.ops.segment_sum(src, seg, n)
kernel_name = 'mk_sandwich_d1_jaxref_r4_a225a8'

def setup_inputs(seed: int=0):
    np.random.seed(seed)
    _w = jnp.asarray

    def _L0_attn_setup():
        import jax, jax.numpy as jnp
        import numpy as np
        import math
        B, N, D, H = (8, 1024, 256, 16)
        DH = D // H
        key = jax.random.key(seed)
        k1, k2, k3, k4 = jax.random.split(key, 4)
        s = 1.0 / math.sqrt(D)
        return {'x': jax.random.normal(k1, (B, N, D), dtype=jnp.float32), 'Wqk': jax.random.normal(k2, (D, D), dtype=jnp.float32) * s, 'Wv': jax.random.normal(k3, (D, D), dtype=jnp.float32) * s, 'Wo': jax.random.normal(k4, (D, D), dtype=jnp.float32) * s, 'tau': jnp.ones((H, 1, 1), dtype=jnp.float32)}
    _L0_attn_in = _L0_attn_setup()

    def _L0_ffn_setup():
        import jax, jax.numpy as jnp
        import numpy as np
        import math
        D_MODEL = 256
        D_FF = 1024
        NUM_EXPERTS = 8
        NUM_SHARED = 1
        E_ROUTED = NUM_EXPERTS - NUM_SHARED
        TOP_K = 2
        CAP_FACTOR = 1.25
        B, S = (4, 512)
        T = B * S
        CAPACITY = math.ceil(CAP_FACTOR * T * TOP_K / E_ROUTED)
        SHARED_SCALE = 1.0

        def _layernorm(x, g, b, eps=1e-05):
            mu = jnp.mean(x, axis=-1, keepdims=True)
            var = jnp.mean((x - mu) ** 2, axis=-1, keepdims=True)
            return (x - mu) * jax.lax.rsqrt(var + eps) * g + b
        key = jax.random.key(seed)
        ks = jax.random.split(key, 10)
        s = 0.02
        return {'x': jax.random.normal(ks[0], (B, S, D_MODEL), dtype=jnp.float32), 'ln_g': jnp.ones((D_MODEL,), jnp.float32), 'ln_b': jnp.zeros((D_MODEL,), jnp.float32), 'Wr': jax.random.normal(ks[1], (D_MODEL, E_ROUTED), jnp.float32) * s, 'W1': jax.random.normal(ks[2], (E_ROUTED, D_MODEL, D_FF), jnp.float32) * s, 'W3': jax.random.normal(ks[3], (E_ROUTED, D_MODEL, D_FF), jnp.float32) * s, 'W2': jax.random.normal(ks[4], (E_ROUTED, D_FF, D_MODEL), jnp.float32) * s, 'W1s': jax.random.normal(ks[5], (D_MODEL, D_FF), jnp.float32) * s, 'W3s': jax.random.normal(ks[6], (D_MODEL, D_FF), jnp.float32) * s, 'W2s': jax.random.normal(ks[7], (D_FF, D_MODEL), jnp.float32) * s}
    _L0_ffn_in = _L0_ffn_setup()
    _d = {'L0_attn_x': _L0_attn_in['x'], 'L0_attn_Wqk': _L0_attn_in['Wqk'], 'L0_attn_Wv': _L0_attn_in['Wv'], 'L0_attn_Wo': _L0_attn_in['Wo'], 'L0_attn_tau': _L0_attn_in['tau'], 'L0_ffn_ln_g': _L0_ffn_in['ln_g'], 'L0_ffn_ln_b': _L0_ffn_in['ln_b'], 'L0_ffn_Wr': _L0_ffn_in['Wr'], 'L0_ffn_W1': _L0_ffn_in['W1'], 'L0_ffn_W3': _L0_ffn_in['W3'], 'L0_ffn_W2': _L0_ffn_in['W2'], 'L0_ffn_W1s': _L0_ffn_in['W1s'], 'L0_ffn_W3s': _L0_ffn_in['W3s'], 'L0_ffn_W2s': _L0_ffn_in['W2s']}
    _x0 = _d['L0_attn_x']
    _d['L0_attn_x'] = jax.random.normal(jax.random.fold_in(jax.random.key(seed), 1), (4, 2048, 256), dtype=_x0.dtype)
    del _x0
    return _d

def reference(L0_attn_x, L0_attn_Wqk, L0_attn_Wv, L0_attn_Wo, L0_attn_tau, L0_ffn_ln_g, L0_ffn_ln_b, L0_ffn_Wr, L0_ffn_W1, L0_ffn_W3, L0_ffn_W2, L0_ffn_W1s, L0_ffn_W3s, L0_ffn_W2s):

    def _L0_attn_ref(x, Wqk, Wv, Wo, tau):
        import jax, jax.numpy as jnp
        import numpy as np
        import math
        B, N, D, H = (8, 1024, 256, 16)
        DH = D // H
        Bb, Nn, Dd = x.shape
        qk = x @ Wqk
        v = x @ Wv
        qk = jnp.transpose(qk, (0, 2, 1)).reshape(Bb, H, DH, Nn)
        v = jnp.transpose(v, (0, 2, 1)).reshape(Bb, H, DH, Nn)
        dot = jnp.einsum('bhdn,bhen->bhde', qk, qk)
        q2 = jnp.sum(qk * qk, axis=-1)
        logits = 2.0 * dot - q2[..., :, None] - q2[..., None, :]
        logits = logits / jnp.sqrt(jnp.asarray(Nn, dtype=x.dtype))
        logits = logits * tau
        attn = jax.nn.softmax(logits, axis=-1)
        w = jnp.einsum('bhde,bhen->bhdn', attn, v)
        out = jnp.transpose(w.reshape(Bb, Dd, Nn), (0, 2, 1))
        return out @ Wo

    def _L0_ffn_ref(x, ln_g, ln_b, Wr, W1, W3, W2, W1s, W3s, W2s):
        import jax, jax.numpy as jnp
        import numpy as np
        import math
        D_MODEL = 256
        D_FF = 1024
        NUM_EXPERTS = 8
        NUM_SHARED = 1
        E_ROUTED = NUM_EXPERTS - NUM_SHARED
        TOP_K = 2
        CAP_FACTOR = 1.25
        B, S = (4, 512)
        T = B * S
        CAPACITY = math.ceil(CAP_FACTOR * T * TOP_K / E_ROUTED)
        SHARED_SCALE = 1.0

        def _layernorm(x, g, b, eps=1e-05):
            mu = jnp.mean(x, axis=-1, keepdims=True)
            var = jnp.mean((x - mu) ** 2, axis=-1, keepdims=True)
            return (x - mu) * jax.lax.rsqrt(var + eps) * g + b
        Bx, Sx, D = x.shape
        Tn = Bx * Sx
        h = _layernorm(x, ln_g, ln_b).reshape(Tn, D)
        logits = h @ Wr
        top_vals, top_idx = jax.lax.top_k(logits, TOP_K)
        gates = jax.nn.softmax(top_vals, axis=-1)
        idx = top_idx.T.reshape(-1)
        gat = gates.T.reshape(-1)
        tok = jnp.tile(jnp.arange(Tn), TOP_K)
        onehot = jax.nn.one_hot(idx, E_ROUTED, dtype=jnp.int32)
        pos = jnp.sum(jnp.cumsum(onehot, axis=0) * onehot, axis=-1) - 1
        keep = pos < CAPACITY
        pos_c = jnp.where(keep, pos, CAPACITY)
        xe = jnp.zeros((E_ROUTED, CAPACITY, D), h.dtype).at[idx, pos_c].set(h[tok], mode='drop')
        a = jnp.einsum('ecd,edf->ecf', xe, W1)
        b = jnp.einsum('ecd,edf->ecf', xe, W3)
        ye = jnp.einsum('ecf,efd->ecd', jax.nn.silu(a) * b, W2)
        out_slots = ye[jnp.clip(idx, 0, E_ROUTED - 1), jnp.clip(pos_c, 0, CAPACITY - 1)]
        out_slots = out_slots * (gat * keep.astype(gat.dtype))[:, None]
        routed = jnp.zeros((Tn, D), h.dtype).at[tok].add(out_slots)
        shared = jax.nn.silu(h @ W1s) * (h @ W3s) @ W2s
        out = routed + SHARED_SCALE * shared
        return out.reshape(Bx, Sx, D)
    x = L0_attn_x
    x = x + _layernorm(_L0_attn_ref(_layernorm(x, axis=-1), L0_attn_Wqk, L0_attn_Wv, L0_attn_Wo, L0_attn_tau), axis=-1)
    x = x + _layernorm(_L0_ffn_ref(_layernorm(x, axis=-1), L0_ffn_ln_g, L0_ffn_ln_b, L0_ffn_Wr, L0_ffn_W1, L0_ffn_W3, L0_ffn_W2, L0_ffn_W1s, L0_ffn_W3s, L0_ffn_W2s), axis=-1)
    return x

_drawn_inputs = setup_inputs


def setup_inputs(seed=0):
    import zlib

    import numpy as np

    out = dict(_drawn_inputs(seed))
    spreads = {'L0_attn_tau': (1.0, 0.2), 'L0_ffn_ln_g': (1.0, 0.2), 'L0_ffn_ln_b': (0.0, 0.1)}
    factors = {}
    for name, (base, spread) in spreads.items():
        noise = np.random.default_rng([zlib.crc32(name.encode()), seed]).standard_normal(out[name].shape)
        drawn = base * np.exp(spread * noise) if base else spread * noise
        out[name] = jnp.asarray(drawn.astype(out[name].dtype))
    for name, factor in factors.items():
        out[name] = (out[name] * factor).astype(out[name].dtype)
    return out
```

```python
from contextlib import ExitStack

import numpy as np

import concourse.bass as bass
from concourse import mybir

ALU = mybir.AluOpType
ACT = mybir.ActivationFunctionType
AX = mybir.AxisListType
F32 = mybir.dt.float32
F32R = mybir.dt.float32r
BF16 = mybir.dt.bfloat16
I32 = mybir.dt.int32
U32 = mybir.dt.uint32

P = 128
EPS = 1e-5
BIG = 3.0e38
OPEN = 1
TOP_K = 2
NOMINAL_TOKENS = 4 * 512


class Chain:

    def __init__(self, eng, sem, base):
        self.eng, self.sem, self.base, self.n = eng, sem, base, 0

    def step(self, ins):
        self.n += 1
        ins.then_inc(self.sem, 1)

    def settle(self):
        self.eng.wait_ge(self.sem, self.base + self.n)

    def link(self, ins):
        self.step(ins)
        self.settle()


def sandwich_kernel(nc, x_in, Wqk, Wv, Wo, tau, ln_g, ln_b, Wr, W1, W3, W2, W1s, W3s, W2s, out):
    B, N, D = x_in.shape
    T = B * N
    H = tau.shape[0]
    DH = D // H
    KC = D // P
    HB = P // DH
    F = W1s.shape[1]
    FM = F // P
    E = Wr.shape[1]
    CAP = -(-int(NOMINAL_TOKENS * TOP_K * 5) // (4 * E))
    GT = 4
    GW = GT * P
    NT = T // P
    NG = T // GW
    GB = N // GW
    TB = N // P
    ST = -(-CAP // P)
    LASTW = CAP - (ST - 1) * P
    HALF = ST // 2
    NC = E * ST
    assert D == KC * P and ST == 6 and E == 7 and GB == 4 and FM == 8

    x_t = x_in.rearrange("b n d -> (b n) d").rearrange("(g t p) d -> g p t d", p=P, t=GT)
    out_t = out.rearrange("b n d -> (b n) d").rearrange("(g t p) d -> g p t d", p=P, t=GT)
    x2_d = nc.dram_tensor("x2_scratch", (T, D), F32, kind="Internal").ap()
    u_d = nc.dram_tensor("u_scratch", (T, D), F32, kind="Internal").ap()
    y_d = nc.dram_tensor("y_scratch", (T + ST * P, D), F32, kind="Internal").ap()
    x2_t = x2_d.rearrange("(g t p) d -> g p t d", p=P, t=GT)
    u_t = u_d.rearrange("(g t p) d -> g p t d", p=P, t=GT)
    y_t = y_d[0:T, :].rearrange("(g t p) d -> g p t d", p=P, t=GT)
    y_spare = y_d[T:T + ST * P, :].rearrange("(t p) d -> t p d", p=P)

    with ExitStack() as ctx:
        def sb(name, shape, dt=F32):
            return ctx.enter_context(nc.sbuf_tensor("sb_" + name, shape, dt))

        def sem(name):
            return ctx.enter_context(nc.semaphore(name))

        bank = [ctx.enter_context(nc.psum_tensor(f"bank{i}", [P, 512], F32)) for i in range(8)]

        ident = sb("ident", [P, P])
        ones = sb("ones", [P, P])
        zrow = sb("zrow", [P, D])
        onesb = sb("onesb", [P, P], BF16)
        earlier = sb("earlier", [P, P], BF16)
        headmask = sb("headmask", [P, HB, DH])
        slot1 = sb("slot1", [P, P])
        colid = sb("colid", [P, NC])
        rank = sb("rank", [P, E])
        estep = sb("estep", [P, E])
        tokid = sb("tokid", [P, NT])
        spare = sb("spare", [P, E, ST])
        carry = sb("carry", [P, E, NT])
        mhalf = sb("mhalf", [P, GT])
        wqk = sb("wqk", [P, KC, D])
        wv = sb("wv", [P, KC, D])
        wvT = sb("wvT", [P, KC, D])
        wo = sb("wo", [P, KC, D])
        wr = sb("wr", [P, KC, E])
        gcol = sb("gcol", [P, KC])
        bcol = sb("bcol", [P, KC])
        taus = sb("taus", [P, KC])
        wup_hi = [sb(f"wup_hi{s}", [P, 2, KC, F], F32R) for s in range(2)]
        wup_lo = [sb(f"wup_lo{s}", [P, 2, KC, F], F32R) for s in range(2)]
        wdn_hi = [sb(f"wdn_hi{s}", [P, FM, D], F32R) for s in range(2)]
        wdn_lo = [sb(f"wdn_lo{s}", [P, FM, D], F32R) for s in range(2)]
        stage = sb("stage", [P, 3, F])
        xT_hi = wup_hi[1][:, :, :, :].rearrange("p a k f -> p (a k f)").rearrange("p (k n) -> p k n", k=KC)
        xT_lo = wup_lo[1][:, :, :, :].rearrange("p a k f -> p (a k f)").rearrange("p (k n) -> p k n", k=KC)
        rows = sb("rows", [P, 2, GT, D])
        xres = sb("xres", [P, GT, D])
        ln_o = sb("ln_o", [P, GT, D])
        x2 = sb("x2", [P, GT, D])
        ysb = sb("ysb", [P, 2, GT, D])
        hfull = sb("hfull", [P, KC, GW])
        h_hi = sb("h_hi", [P, 2, KC, GW], F32R)
        h_lo = sb("h_lo", [P, 2, KC, GW], F32R)
        gate = sb("gate", [P, 2, GW])
        act = sb("act", [P, 2, GW])
        act_hi = sb("act_hi", [P, 4, GW], F32R)
        act_lo = sb("act_lo", [P, 4, GW], F32R)
        res = [xres, ln_o]
        st = sb("st", [P, GT, 6])
        mv = sb("mv", [P, GT, 2])
        rstd = sb("rstd", [P, GT])
        nbias = sb("nbias", [P, GT])
        stB = sb("stB", [P, GT, 6])
        mvB = sb("mvB", [P, GT, 2])
        rstdB = sb("rstdB", [P, GT])
        nbiasB = sb("nbiasB", [P, GT])
        veB = sb("veB", [P, GT])
        st2 = sb("st2", [P, GT, 6])
        mv2 = sb("mv2", [P, GT, 2])
        ve2 = sb("ve2", [P, GT])
        rstd2 = sb("rstd2", [P, GT])
        veA = sb("veA", [P, GT])
        xn = ysb[:, 0, :, :]
        xx = act_hi[:, :, :].rearrange("p a (h d) -> p a h d", h=2)
        u = ysb[:, 1, :, :]
        gs = act[:, :, :]
        gf = gate[:, 0, :].rearrange("p (k d) -> p k d", k=KC)
        tsb = gate[:, 1, :].rearrange("p (k d) -> p k d", k=KC)
        sS = hfull[:, 0, 0:KC * P].rearrange("p (k j) -> p k j", k=KC)
        sD = hfull[:, 0, KC * P:2 * KC * P].rearrange("p (k j) -> p k j", k=KC)
        lc = sb("lc", [P, KC, DH])
        small = sb("small", [P, 8, KC])
        m_hi = sb("m_hi", [P, KC, D], F32R)
        m_lo = sb("m_lo", [P, KC, D], F32R)
        lg = sb("lg", [P, E, NT])
        oh = sb("oh", [P, 2, E, NT], BF16)
        slotcol = sb("slotcol", [P, 2, NT])
        slotm = sb("slotm", [P, 2, NT])
        gates = sb("gates", [P, 2, NT])
        table2 = sb("table2", [P, 2 * NC])
        tabe = sb("tabe", [P, NC])
        total = sb("total", [P, E])
        zmat = sb("zmat", [P, P])
        gidx = sb("gidx", [P, NC], U32)
        gcur = sb("gcur", [P, 2, HALF], U32)
        scur = sb("scur", [P, 2, HALF], U32)
        sidx = sb("sidx", [P, NC], U32)
        rt = [xn[:, :, :].rearrange("p t d -> p (t d)")[:, i * 512:i * 512 + E * NT].rearrange("p (e t) -> p e t", e=E)
              for i in range(2)]
        rt2 = ln_o[:, :, :].rearrange("p t d -> p (t d)")
        rincl = rt2[:, 0:E * NT]
        rsmall = rt2[:, 512:1024].rearrange("p (a t) -> p a t", t=2 * NT)
        RB = 4
        selA = x2[:, :, :].rearrange("p t d -> p (t d)")[:, 0:2 * RB * P].rearrange("p (s t m) -> p s t m", s=2, t=RB)
        selB = u[:, :, :].rearrange("p t d -> p (t d)")[:, 0:2 * RB * 2 * NC].rearrange(
            "p (s t a c) -> p s t a c", s=2, t=RB, a=2)
        selE = [xres[:, c, :].rearrange("p (t x) -> p t x", t=RB)[:, :, 0:NC] for c in range(2)]

        pool_go = sem("pool_go")
        dve_go = sem("dve_go")
        const_in = sem("const_in")
        const_ok = sem("const_ok")
        tau_ok = sem("tau_ok")
        wvT_ps = sem("wvT_ps")
        wvT_ok = sem("wvT_ok")
        x_in_s = [sem(f"x_in{i}") for i in range(2)]
        a_chain = sem("a_chain")
        a_var = sem("a_var")
        a_rstd = sem("a_rstd")
        xn_ok = sem("xn_ok")
        xhi_ok = sem("xhi_ok")
        xlo_ok = sem("xlo_ok")
        xt_ps = sem("xt_ps")
        xthi_ok = sem("xthi_ok")
        xtlo_ok = sem("xtlo_ok")
        g_done = sem("g_done")
        m_chain = sem("m_chain")
        m_pe = sem("m_pe")
        m_act = sem("m_act")
        m_dve = sem("m_dve")
        o_ok = sem("o_ok")
        b_chain = sem("b_chain")
        b_var = sem("b_var")
        b_rstd = sem("b_rstd")
        b_nb = sem("b_nb")
        lno_ok = sem("lno_ok")
        xres_in = sem("xres_in")
        x2_ok = sem("x2_ok")
        x2_out = sem("x2_out")
        b_var2 = sem("b_var2")
        b_rstd2 = sem("b_rstd2")
        u_ok = sem("u_ok")
        u_out = sem("u_out")
        ut_ps = sem("ut_ps")
        hT_ok = sem("hT_ok")
        lg_ps = sem("lg_ps")
        lg_ok = sem("lg_ok")
        r_chain = sem("r_chain")
        r_oh = sem("r_oh")
        r_d = sem("r_d")
        r_ex = sem("r_ex")
        r_cnt = sem("r_cnt")
        r_sel = sem("r_sel")
        r_selE = sem("r_selE")
        r_mm = sem("r_mm")
        r_tab = sem("r_tab")
        r_idx = sem("r_idx")
        stage_in = [sem(f"stage_in{i}") for i in range(3)]
        w_hi = sem("w_hi")
        w_lo = sem("w_lo")
        rows_in = [sem(f"rows_in{i}") for i in range(2)]
        gathered = [sem(f"gathered{i}") for i in range(2)]
        added = [sem(f"added{i}") for i in range(2)]
        ysb_free = [sem(f"ysb_free{i}") for i in range(2)]
        ht_ps = sem("ht_ps")
        hf_ok = sem("hf_ok")
        hhi_ok = sem("hhi_ok")
        hlo_ok = sem("hlo_ok")
        a_ps = sem("a_ps")
        b_ps = sem("b_ps")
        silu_ok = sem("silu_ok")
        act_ok = sem("act_ok")
        ahi_ok = sem("ahi_ok")
        alo_ok = sem("alo_ok")
        dn_done = sem("dn_done")
        y_sb = sem("y_sb")
        g_cur = sem("g_cur")
        s_cur = sem("s_cur")
        y_out = [sem(f"y_out{i}") for i in range(2)]
        spare_z = sem("spare_z")
        spare_out = sem("spare_out")
        t_y = [sem(f"t_y{i}") for i in range(2)]
        t_x = [sem(f"t_x{i}") for i in range(2)]
        t_chain = sem("t_chain")
        t_var = sem("t_var")
        t_rstd = sem("t_rstd")
        t_ok = sem("t_ok")
        t_out = [sem(f"t_out{i}") for i in range(2)]

        NCONST = 17
        NSMALL = 6 + HB
        MA, MP, MD = 6, 6, 5
        PIECES = 6

        class Chunk:
            def __init__(self, n, slot, wset, widths, landed, expert=None):
                self.n, self.slot, self.wset, self.widths = n, slot, wset, widths
                self.landed, self.expert, self.w = landed, expert, sum(widths)

        def shared_chunk(pair, slot):
            return Chunk(pair * 2 + slot, slot, 0, [P] * GT, pair * 16 + 16)

        def expert_chunk(e, part, wset):
            widths = [P] * HALF if part == 0 else [P] * (HALF - 1) + [LASTW]
            return Chunk(e * 2 + (NG + part), part, wset, widths, e * (16 * HALF) + 16 * HALF, e)

        def walk(eng, body):
            body(None, shared_chunk(0, 0), shared_chunk(0, 1))
            with eng.Fori(0, NG // 2 - 1) as i:
                body(shared_chunk(i, 0), shared_chunk(i, 1), shared_chunk(i + 1, 0))
                body(shared_chunk(i, 1), shared_chunk(i + 1, 0), shared_chunk(i + 1, 1))
            k = NG // 2 - 1
            body(shared_chunk(k, 0), shared_chunk(k, 1), expert_chunk(0, 0, 1))
            body(shared_chunk(k, 1), expert_chunk(0, 0, 1), expert_chunk(0, 1, 1))
            with eng.Fori(0, (E - 1) // 2) as i:
                seq = [expert_chunk(i * 2, 0, 1), expert_chunk(i * 2, 1, 1), expert_chunk(i * 2 + 1, 0, 0),
                       expert_chunk(i * 2 + 1, 1, 0), expert_chunk(i * 2 + 2, 0, 1), expert_chunk(i * 2 + 2, 1, 1)]
                for j in range(1, 5):
                    body(seq[j - 1], seq[j], seq[j + 1])
            body(expert_chunk(E - 1, 0, 1), expert_chunk(E - 1, 1, 1), None)

        NCH = NG + 2 * E
        TAIL = NCH

        block = ctx.enter_context(nc.Block())

        @block.sync
        def _(sp):
            def load_piece(w, j, ws):
                if not (isinstance(w, int) and w == 0 and j < 3):
                    sp.wait_ge(w_lo, w * PIECES + (j - 2))
                up, dn = ws
                if j < 4:
                    src = up[j // 2][(j % 2) * P:(j % 2 + 1) * P, :]
                    dst = stage[:, j % 3, :]
                else:
                    half = FM // 2
                    src = dn.rearrange("(m p) d -> p m d", p=P)[:, (j - 4) * half:(j - 3) * half, :]
                    dst = stage[:, j % 3, :].rearrange("p (m d) -> p m d", d=D)
                sp.dma_start(dst, src).then_inc(stage_in[j % 3], 16)

            def load_x(g, slot):
                sp.dma_start(rows[:, slot, :, :], x_t[g]).then_inc(x_in_s[slot], 16)

            for opened in (xtlo_ok, hT_ok, g_done, o_ok, m_act, lno_ok, x2_ok, x2_out, u_ok, u_out, ut_ps, lg_ps,
                           lg_ok, xhi_ok, xlo_ok, xt_ps, r_mm, *y_out, *t_out):
                sp.sem_inc(opened, OPEN)
            for s in range(2):
                load_x(s, s)
            for dst, src in ((wqk, Wqk), (wv, Wv), (wo, Wo), (wr, Wr)):
                sp.dma_start(dst[:, :, :], src.rearrange("(k p) n -> p k n", p=P)).then_inc(const_in, 16)
            with nc.allow_non_contiguous_dma(reason="vectors of 256 values"):
                for dst, src in ((gcol, ln_g), (bcol, ln_b)):
                    sp.dma_start(dst[:, :], src.rearrange("(k p) -> p k", p=P)).then_inc(const_in, 16)
                for h in range(HB):
                    src = tau.rearrange("(k h) a b -> (a b) h k", h=HB)[:, h, :]
                    sp.dma_start(taus[h * DH:(h + 1) * DH, :], src.broadcast_to([DH, KC])).then_inc(const_in, 16)
            for j in range(PIECES):
                load_piece(0, j, ([W1s, W3s], W2s))

            def batch_loads(b, last):
                for q in range(GB):
                    if not (last and q >= GB - 2):
                        sp.wait_ge(xn_ok, b * GB + (q + 1))
                        load_x(b * GB + (q + 2), q % 2)
                for q in range(GB):
                    g = b * GB + q
                    sp.wait_ge(x2_ok, OPEN + g)
                    sp.dma_start(xres[:, :, :], x_t[g]).then_inc(xres_in, 16)
                    sp.wait_ge(x2_ok, OPEN + g + 1)
                    sp.dma_start(x2_t[g], x2[:, :, :]).then_inc(x2_out, 16)
                    sp.wait_ge(u_ok, OPEN + g + 1)
                    sp.dma_start(u_t[g], u[:, :, :]).then_inc(u_out, 16)

            with sp.Fori(0, B - 1) as b:
                batch_loads(b, False)
            batch_loads(B - 1, True)

            sp.wait_ge(u_out, OPEN + 16 * NG)
            sp.wait_ge(x2_out, OPEN + 16 * NG)
            for j in range(ST):
                sp.dma_start(y_spare[j], zrow[:, :]).then_inc(spare_out, 16)
            for s in range(2):
                sp.dma_start(rows[:, s, :, :], u_t[s]).then_inc(rows_in[s], 16)
            for j in range(PIECES):
                load_piece(1, j, ([W1[0], W3[0]], W2[0]))

            def refill(n, slot):
                sp.wait_ge(ht_ps, n + 1)
                sp.dma_start(rows[:, slot, :, :], u_t[n + 2]).then_inc(rows_in[slot], 16)

            def store_y(n, slot):
                sp.wait_ge(y_sb, n + 1)
                sp.dma_start(y_t[n], ysb[:, slot, :, :]).then_inc(y_out[slot], 16)

            refill(0, 0)
            with sp.Fori(0, NG // 2 - 2) as i:
                for s in range(2):
                    refill(i * 2 + (1 + s), 1 - s)
                    store_y(i * 2 + s, s)
            refill(NG - 3, 1)
            for n in range(NG - 4, NG):
                store_y(n, n % 2)
            with sp.Fori(0, E - 1) as e:
                for j in range(PIECES):
                    load_piece(e + 2, j, ([W1[e + 1], W3[e + 1]], W2[e + 1]))
            for s in range(2):
                sp.wait_ge(added[s], 16 * HALF * E)
            with sp.Fori(0, NG // 2) as i:
                for s in range(2):
                    sp.wait_ge(t_out[s], OPEN + i * 16)
                    sp.dma_start(rows[:, s, :, :], y_t[i * 2 + s]).then_inc(t_y[s], 16)
                    sp.dma_start(res[s][:, :, :], x2_t[i * 2 + s]).then_inc(t_x[s], 16)
                for s in range(2):
                    sp.wait_ge(t_ok, i * 2 + (s + 1))
                    sp.dma_start(out_t[i * 2 + s], res[s][:, :, :]).then_inc(t_out[s], 16)
            for s in range(2):
                sp.wait_ge(t_out[s], OPEN + 16 * (NG // 2))

        @block.gpsimd
        def _(pool):
            v = nc.gpsimd
            n_const = [0]

            def made(ins, settle=False):
                n_const[0] += 1
                ins.then_inc(const_ok, 1)
                if settle:
                    pool.wait_ge(const_ok, n_const[0])
            made(v.memset(ones[:, :], 1.0))
            made(v.memset(onesb[:, :], 1.0))
            made(v.memset(zrow[:, :], 0.0))
            made(v.memset(mhalf[:, :], -0.5))
            made(v.memset(headmask[:, :, :], 1.0))
            made(v.memset(carry[:, :, :], 1.0))
            made(v.iota(slot1[:, :], [[1, P]], base=1, channel_multiplier=0, allow_small_or_imprecise_dtypes=True))
            made(v.iota(colid[:, :], [[1, NC]], base=0, channel_multiplier=0, allow_small_or_imprecise_dtypes=True))
            made(v.iota(rank[:, :], [[-1, E]], base=E, channel_multiplier=0, allow_small_or_imprecise_dtypes=True))
            made(v.iota(estep[:, :], [[ST, E]], base=0, channel_multiplier=0, allow_small_or_imprecise_dtypes=True))
            made(v.iota(tokid[:, :], [[P, NT]], base=1, channel_multiplier=1, allow_small_or_imprecise_dtypes=True))
            made(v.iota(spare[:, :, :], [[0, E], [P, ST]], base=T + 1, channel_multiplier=1,
                        allow_small_or_imprecise_dtypes=True), True)
            made(v.memset(carry[:, :, 0:1], 0.0))
            made(v.affine_select(out=ident[:, :], in_=ones[:, :], compare_op=ALU.is_equal, fill=0.0, base=0,
                                 pattern=[[-1, P]], channel_multiplier=1))
            made(v.affine_select(out=earlier[:, :], in_=onesb[:, :], compare_op=ALU.is_ge, fill=0.0, base=-1,
                                 pattern=[[1, P]], channel_multiplier=-1))
            made(v.affine_select(out=headmask[:, :, :], in_=headmask[:, :, :], compare_op=ALU.is_ge, fill=0.0,
                                 base=0, pattern=[[-DH, HB], [0, DH]], channel_multiplier=1), True)
            made(v.affine_select(out=headmask[:, :, :], in_=headmask[:, :, :], compare_op=ALU.is_ge, fill=0.0,
                                 base=DH - 1, pattern=[[DH, HB], [0, DH]], channel_multiplier=-1))
            assert n_const[0] == NCONST

            def split_piece(w, j):
                s = W_SET(w)
                if j == 0 and not (isinstance(w, int) and w == 0):
                    if isinstance(w, int) and w == 1:
                        pool.wait_ge(o_ok, OPEN + NG)
                    else:
                        pool.wait_ge(dn_done, w * (2 * FM) + FM * (NG - 4))
                pool.wait_ge(stage_in[j % 3], w * 32 + 16 * (j // 3 + 1))
                if j < 4:
                    hi, lo = wup_hi[s][:, j // 2, j % 2, :], wup_lo[s][:, j // 2, j % 2, :]
                    src = stage[:, j % 3, :]
                else:
                    m0 = (j - 4) * (FM // 2)
                    hi, lo = wdn_hi[s][:, m0:m0 + FM // 2, :], wdn_lo[s][:, m0:m0 + FM // 2, :]
                    src = stage[:, j % 3, :].rearrange("p (m d) -> p m d", d=D)
                pool.sem_inc(pool_go, 1)
                v.tensor_copy(hi, src).then_inc(w_hi, 1)
                pool.wait_ge(w_hi, w * PIECES + (j + 1))
                v.tensor_tensor(lo, src, hi.bitcast(F32), ALU.subtract).then_inc(w_lo, 1)

            def W_SET(w):
                return w % 2 if isinstance(w, int) else w_parity[0]
            w_parity = [0]

            for j in range(PIECES):
                split_piece(0, j)

            with pool.Fori(0, B) as b:
                for q in range(GB):
                    g = b * GB + q
                    pool.wait_ge(a_var, g + 1)
                    v.tensor_tensor(rstd[:, :], veA[:, :], mhalf[:, :], ALU.pow).then_inc(a_rstd, 1)
                    pool.wait_ge(xhi_ok, OPEN + g + 1)
                    v.tensor_tensor(xx[:, :, 1, :], xn[:, :, :], xx[:, :, 0, :].bitcast(F32),
                                    ALU.subtract).then_inc(xlo_ok, 1)
                for q in range(GB):
                    g = b * GB + q
                    pool.wait_ge(b_var, g + 1)
                    v.tensor_tensor(rstdB[:, :], veB[:, :], mhalf[:, :], ALU.pow).then_inc(b_rstd, 1)
                    pool.wait_ge(lno_ok, OPEN + g + 1)
                    pool.wait_ge(xres_in, g * 16 + 16)
                    pool.wait_ge(x2_out, OPEN + g * 16)
                    pool.wait_ge(u_ok, OPEN + g)
                    v.tensor_tensor(x2[:, :, :], ln_o[:, :, :], xres[:, :, :], ALU.add).then_inc(x2_ok, 1)
                    pool.wait_ge(b_var2, g + 1)
                    v.tensor_tensor(rstd2[:, :], ve2[:, :], mhalf[:, :], ALU.pow).then_inc(b_rstd2, 1)

            for j in range(PIECES):
                split_piece(1, j)

            def gather(e, part):
                n = e * 2 + (NG + part)
                pool.wait_ge(gathered[part], e * (16 * HALF))
                pool.sem_inc(pool_go, 1)
                v.tensor_copy(gcur[:, part, :], gidx[:, bass.ds(e * ST + part * HALF, HALF)]).then_inc(g_cur, 1)
                pool.wait_ge(g_cur, e * 2 + (part + 1))
                pool.wait_ge(ht_ps, n - 1)
                pool.sem_inc(pool_go, 1)
                for t in range(HALF):
                    w = LASTW if part * HALF + t == ST - 1 else P
                    pool.indirect_dma_start(rows[0:w, part, t, :], None, u_d,
                                            bass.IndirectOffsetOnAxis(ap=gcur[0:w, part, t:t + 1], axis=0)
                                            ).then_inc(gathered[part], 16)

            def release(e, part):
                pool.wait_ge(added[part], e * (16 * HALF))
                pool.sem_inc(ysb_free[part], 1)

            def scatter(e, part):
                n = e * 2 + (NG + part)
                v.tensor_copy(scur[:, part, :], sidx[:, bass.ds(e * ST + part * HALF, HALF)]).then_inc(s_cur, 1)
                pool.wait_ge(s_cur, e * 2 + (part + 1))
                pool.wait_ge(y_sb, n + 1)
                for s in range(2):
                    pool.wait_ge(y_out[s], OPEN + 16 * (NG // 2))
                    pool.wait_ge(added[s], e * (16 * HALF))
                pool.sem_inc(pool_go, 1)
                for t in range(HALF):
                    w = LASTW if part * HALF + t == ST - 1 else P
                    pool.indirect_dma_start(y_d, bass.IndirectOffsetOnAxis(ap=scur[0:w, part, t:t + 1], axis=0),
                                            ysb[0:w, part, t, :], None, compute_op=ALU.add
                                            ).then_inc(added[part], 16)

            pool.wait_ge(r_idx, 1)
            gather(0, 0)
            gather(0, 1)
            pool.wait_ge(spare_out, 16 * ST)
            release(0, 0)
            release(0, 1)
            gather(1, 0)
            for j in range(PIECES):
                split_piece(2, j)
            gather(1, 1)
            scatter(0, 0)

            def during(e):
                release(e, 0)
                gather(e + 1, 0)
                scatter(e - 1, 1)
                for j in range(PIECES):
                    split_piece(e + 2, j)
                gather(e + 1, 1)
                release(e, 1)
                scatter(e, 0)

            w_parity[0] = 1
            during(1)
            with pool.Fori(1, (E - 1) // 2) as i:
                for s in range(2):
                    w_parity[0] = s
                    during(i * 2 + s)
            release(E - 1, 0)
            scatter(E - 2, 1)
            release(E - 1, 1)
            scatter(E - 1, 0)
            scatter(E - 1, 1)
            with pool.Fori(0, NG) as g:
                pool.wait_ge(t_var, g + 1)
                v.tensor_tensor(rstd[:, :], veA[:, :], mhalf[:, :], ALU.pow).then_inc(t_rstd, 1)

        @block.scalar
        def _(act_e):
            s = nc.scalar
            act_e.wait_ge(wvT_ps, 1)
            s.activation(wvT[:, :, :].rearrange("p k d -> p (k d)"), bank[6][:, :], ACT.Copy).then_inc(wvT_ok, 1)

            def stage_a(g, b, q):
                act_e.wait_ge(xn_ok, g + 1)
                act_e.wait_ge(g_done, OPEN + g)
                s.activation(xx[:, :, 0, :], xn[:, :, :], ACT.Copy).then_inc(xhi_ok, 1)
                act_e.wait_ge(xt_ps, OPEN + g + 1)
                if q == 0:
                    act_e.wait_ge(o_ok, OPEN + b * GB)
                for k in range(KC):
                    ins = s.activation(xT_hi[:, k, q * GW:(q + 1) * GW], bank[2 + k][:, :], ACT.Copy)
                ins.then_inc(xthi_ok, 1)

            def stage_m(b):
                def out_step(k, dst, src, func=ACT.Copy):
                    s.activation(dst, src, func).then_inc(m_act, 1)
                flat = lambda t: t.rearrange("p k d -> p (k d)")
                act_e.wait_ge(g_done, OPEN + b * GB + GB)
                for k in range(KC):
                    ins = s.activation(gs[:, k, :], bank[k][:, :], ACT.Copy)
                ins.then_inc(m_act, 1)
                act_e.wait_ge(m_pe, b * MP + 2)
                out_step(2, gate[:, 1, :], bank[7][:, :])
                act_e.wait_ge(m_pe, b * MP + 3)
                out_step(3, hfull[:, 0, 0:KC * P], bank[6][:, 0:KC * P])
                act_e.wait_ge(m_dve, b * MD + 3)
                out_step(4, lc[:, :, :], lc[:, :, :], ACT.Exp)
                act_e.wait_ge(m_pe, b * MP + 5)
                out_step(5, gate[:, 1, :], bank[6][:, :])
                act_e.wait_ge(m_pe, b * MP + 6)
                out_step(6, flat(m_hi[:, :, :]), bank[7][:, :])

            def stage_b(g):
                act_e.wait_ge(b_nb, g + 1)
                act_e.wait_ge(x2_ok, OPEN + g)
                for t in range(GT):
                    ins = s.activation(ln_o[:, t, :], bank[4 + t // 2][:, (t % 2) * D:(t % 2 + 1) * D],
                                       ACT.Identity, scale=rstdB[:, t:t + 1], bias=nbiasB[:, t:t + 1])
                ins.then_inc(lno_ok, 1)
                act_e.wait_ge(ut_ps, OPEN + g + 1)
                act_e.wait_ge(lg_ps, OPEN + g)
                for k in range(KC):
                    ins = s.activation(hfull[:, k, :], bank[2 + k][:, :], ACT.Identity,
                                       scale=gcol[:, k:k + 1], bias=bcol[:, k:k + 1])
                ins.then_inc(hT_ok, 1)

            act_e.wait_ge(const_in, 16 * NSMALL)
            with act_e.Fori(0, B) as b:
                for q in range(GB):
                    stage_a(b * GB + q, b, q)
                stage_m(b)
                for q in range(GB):
                    stage_b(b * GB + q)
            act_e.wait_ge(r_d, 1)
            s.activation(rsmall[:, 1, 0:NT], rsmall[:, 0, 0:NT], ACT.Exp).then_inc(r_ex, 1)

            def prep(c, before):
                act_e.wait_ge(ht_ps, c.n + 1)
                if before:
                    act_e.wait_ge(hlo_ok, c.n)
                else:
                    act_e.wait_ge(lg_ps, OPEN + NG)
                for k in range(KC):
                    ins = s.activation(hfull[:, k, 0:c.w], bank[6 + k][:, 0:c.w], ACT.Identity,
                                       scale=gcol[:, k:k + 1], bias=bcol[:, k:k + 1])
                ins.then_inc(hf_ok, 1)
                act_e.wait_ge(hf_ok, c.n + 1)
                if before:
                    act_e.wait_ge(b_ps, (c.n - 1) * FM)
                s.activation(h_hi[:, c.slot, :, 0:c.w], hfull[:, :, 0:c.w], ACT.Copy).then_inc(hhi_ok, 1)

            def high(c, m):
                act_e.wait_ge(act_ok, c.n * FM + (m + 1))
                if not (isinstance(c.n, int) and c.n * FM + m - 3 <= 0):
                    act_e.wait_ge(dn_done, c.n * FM + (m - 3))
                s.activation(act_hi[:, m % 4, 0:c.w], act[:, m % 2, 0:c.w], ACT.Copy).then_inc(ahi_ok, 1)

            def take_y(c):
                act_e.wait_ge(dn_done, c.n * FM + FM)
                if c.expert is None:
                    act_e.wait_ge(y_out[c.slot], OPEN + c.landed - 16)
                    for t2 in range(2):
                        ins = s.activation(ysb[:, c.slot, 2 * t2:2 * t2 + 2, :].rearrange("p t d -> p (t d)"),
                                           bank[4 + t2][:, :], ACT.Copy)
                else:
                    act_e.wait_ge(y_out[c.slot], OPEN + 16 * (NG // 2))
                    act_e.wait_ge(ysb_free[c.slot], c.expert + 1)
                    for t, w in enumerate(c.widths):
                        col = c.expert * ST + (c.slot * HALF + t + NC)
                        ins = s.activation(ysb[0:w, c.slot, t, :], bank[4 + t // 2][0:w, (t % 2) * D:(t % 2 + 1) * D],
                                           ACT.Copy, scale=table2[0:w, bass.ds(col, 1)])
                ins.then_inc(y_sb, 1)

            def body(prev, c, nxt):
                for m in range(FM):
                    if m == 2 and prev is not None:
                        take_y(prev)
                    act_e.wait_ge(a_ps, c.n * FM + (m + 1))
                    if not (isinstance(c.n, int) and c.n * FM + m - 1 <= 0):
                        act_e.wait_ge(act_ok, c.n * FM + (m - 1))
                    s.activation(gate[:, m % 2, 0:c.w], bank[2 * (m % 2)][:, 0:c.w], ACT.Silu).then_inc(silu_ok, 1)
                    if m > 0:
                        high(c, m - 1)
                    elif prev is not None:
                        high(prev, FM - 1)
                    if m == 5 and nxt is not None:
                        prep(nxt, True)

            prep(shared_chunk(0, 0), False)
            walk(act_e, body)
            last = expert_chunk(E - 1, 1, 1)
            high(last, FM - 1)
            take_y(last)

        @block.tensor
        def _(pe):
            t_ = nc.tensor
            pe.wait_ge(const_ok, NCONST)
            pe.wait_ge(const_in, 16 * NSMALL)
            for k in range(KC):
                for c in range(KC):
                    ins = t_.transpose(bank[6][:, k * D + c * P:k * D + (c + 1) * P], wv[:, c, k * P:(k + 1) * P],
                                       ident[:, :])
            ins.then_inc(wvT_ps, 1)

            def three(o, a_hi, a_lo, b_hi, b_lo, start, stop):
                t_.matmul(o, a_lo, b_hi, start=start, stop=False, skip_group_check=True)
                t_.matmul(o, a_hi, b_lo, start=False, stop=False, skip_group_check=True)
                return t_.matmul(o, a_hi, b_hi, start=False, stop=stop, skip_group_check=True)

            def stage_a(g, b, q):
                pe.wait_ge(xn_ok, g + 1)
                pe.wait_ge(xtlo_ok, OPEN + g)
                if q == 0:
                    pe.wait_ge(hT_ok, OPEN + b * GB)
                for t in range(GT):
                    for k in range(KC):
                        ins = t_.transpose(bank[2 + k][:, t * P:(t + 1) * P], xn[:, t, k * P:(k + 1) * P], ident[:, :])
                ins.then_inc(xt_ps, 1)
                pe.wait_ge(xlo_ok, OPEN + g + 1)
                if q == 0:
                    pe.wait_ge(m_act, OPEN + b * MA)
                for t in range(GT):
                    for k in range(KC):
                        ins = t_.matmul(bank[k][:, :], xx[:, t, 0, k * P:(k + 1) * P],
                                        xx[:, t, :, :].rearrange("p h d -> p (h d)"),
                                        start=(q == 0 and t == 0), stop=(q == GB - 1 and t == GT - 1))
                ins.then_inc(g_done, 1)

            def stage_m(b):
                pe.wait_ge(m_act, OPEN + b * MA + 1)
                for k in range(KC):
                    for c in range(KC):
                        ins = t_.transpose(bank[6][:, k * D + c * P:k * D + (c + 1) * P],
                                           gs[:, c, D + k * P:D + (k + 1) * P], ident[:, :])
                ins.then_inc(m_pe, 1)
                pe.wait_ge(m_dve, b * MD + 1)
                pe.wait_ge(lg_ok, OPEN + b * GB)
                for c in range(KC):
                    for k in range(KC):
                        ins = t_.matmul(bank[7][:, c * D:(c + 1) * D], gf[:, k, c * P:(c + 1) * P], wqk[:, k, :],
                                        start=(k == 0), stop=(k == KC - 1))
                ins.then_inc(m_pe, 1)
                pe.wait_ge(m_act, OPEN + b * MA + 2)
                for c in range(KC):
                    for k in range(KC):
                        ins = t_.matmul(bank[6][:, c * P:(c + 1) * P], wqk[:, k, c * P:(c + 1) * P],
                                        tsb[:, k, c * P:(c + 1) * P], start=(k == 0), stop=(k == KC - 1))
                ins.then_inc(m_pe, 1)
                pe.wait_ge(m_dve, b * MD + 2)
                t_.matmul(bank[7][:, 0:KC * P], ones[:, :], hfull[:, 0, KC * P:2 * KC * P],
                          start=True, stop=True).then_inc(m_pe, 1)
                pe.wait_ge(m_dve, b * MD + 4)
                for c in range(KC):
                    ins = t_.matmul(bank[6][:, c * D:(c + 1) * D], sD[:, c, :], wo[:, c, :], start=True, stop=True)
                ins.then_inc(m_pe, 1)
                pe.wait_ge(m_act, OPEN + b * MA + 5)
                pe.wait_ge(wvT_ok, 1)
                for c in range(KC):
                    for k in range(KC):
                        ins = t_.matmul(bank[7][:, c * D:(c + 1) * D], wvT[:, k, c * P:(c + 1) * P], tsb[:, k, :],
                                        start=(k == 0), stop=(k == KC - 1))
                ins.then_inc(m_pe, 1)

            def stage_b(g, b, q):
                if q == 0:
                    pe.wait_ge(m_dve, b * MD + MD)
                    pe.wait_ge(xtlo_ok, OPEN + b * GB + GB)
                pe.wait_ge(lno_ok, OPEN + g)
                for t in range(GT):
                    o = bank[4 + t // 2][:, (t % 2) * D:(t % 2 + 1) * D]
                    cols = slice(q * GW + t * P, q * GW + (t + 1) * P)
                    for k in range(KC):
                        ins = three(o, xT_hi[:, k, cols], xT_lo[:, k, cols], m_hi[:, k, :], m_lo[:, k, :],
                                    k == 0, k == KC - 1)
                ins.then_inc(o_ok, 1)
                pe.wait_ge(u_ok, OPEN + g + 1)
                pe.wait_ge(hT_ok, OPEN + g)
                for t in range(GT):
                    for k in range(KC):
                        ins = t_.transpose(bank[2 + k][:, t * P:(t + 1) * P], u[:, t, k * P:(k + 1) * P], ident[:, :])
                ins.then_inc(ut_ps, 1)
                pe.wait_ge(hT_ok, OPEN + g + 1)
                pe.wait_ge(lg_ok, OPEN + g)
                for t in range(GT):
                    for k in range(KC):
                        ins = t_.matmul(bank[7][:, t * 8:t * 8 + E], hfull[:, k, t * P:(t + 1) * P], wr[:, k, :],
                                        start=(k == 0), stop=(k == KC - 1))
                ins.then_inc(lg_ps, 1)

            with pe.Fori(0, B) as b:
                for q in range(GB):
                    stage_a(b * GB + q, b, q)
                stage_m(b)
                for q in range(GB):
                    stage_b(b * GB + q, b, q)

            for c in range(2):
                pe.wait_ge(r_oh, c + 1)
                if c == 0:
                    pe.wait_ge(hT_ok, OPEN + NG)
                rhs = oh[:, c, :, :].rearrange("p e t -> p (e t)")
                t_.matmul(bank[2 * c][:, 0:E * NT], earlier[:, :], rhs, start=True, stop=True)
                t_.matmul(bank[2 * c + 1][:, 0:E * NT], onesb[:, :], rhs, start=True, stop=True).then_inc(r_cnt, 1)
            t_.matmul(bank[4][:, 0:2 * NC], zmat[:, :], wo[:, 0, 0:2 * NC], start=True, stop=False,
                      skip_group_check=True)
            with pe.Fori(0, NT // RB) as i:
                for c in range(2):
                    pe.wait_ge(r_sel, i * 2 + (c + 1))
                    for t in range(RB):
                        ins = t_.matmul(bank[4][:, 0:2 * NC], selA[:, c, t, :],
                                        selB[:, c, t, :, :].rearrange("p a c -> p (a c)"),
                                        start=False, stop=False, skip_group_check=True)
                    ins.then_inc(r_mm, 1)

            def turn(c, first):
                pe.wait_ge((rows_in if c.expert is None else gathered)[c.slot], c.landed)
                if not first:
                    pe.wait_ge(hf_ok, c.n)
                for t, w in enumerate(c.widths):
                    for k in range(KC):
                        ins = t_.transpose(bank[6 + k][:, t * P:t * P + w], rows[0:w, c.slot, t, k * P:(k + 1) * P],
                                           ident[0:w, 0:w])
                ins.then_inc(ht_ps, 1)

            def up(c, m, opening):
                if m == 0:
                    pe.wait_ge(hlo_ok, c.n + 1)
                    if opening is not None:
                        pe.wait_ge(w_lo, opening)
                for which, freed, full in ((0, silu_ok, a_ps), (1, act_ok, b_ps)):
                    o = bank[2 * (m % 2) + which][:, 0:c.w]
                    if not (isinstance(c.n, int) and c.n * FM + m - 1 <= 0):
                        pe.wait_ge(freed, c.n * FM + (m - 1))
                    for k in range(KC):
                        wh = wup_hi[c.wset][:, which, k, m * P:(m + 1) * P]
                        wl = wup_lo[c.wset][:, which, k, m * P:(m + 1) * P]
                        ins = three(o, wh, wl, h_hi[:, c.slot, k, 0:c.w], h_lo[:, c.slot, k, 0:c.w],
                                    k == 0, k == KC - 1)
                    ins.then_inc(full, 1)

            def down(c, m):
                pe.wait_ge(alo_ok, c.n * FM + (m + 1))
                if m == 0:
                    pe.wait_ge(y_sb, c.n)
                for t, w in enumerate(c.widths):
                    cols = slice(t * P, t * P + w)
                    ins = three(bank[4 + t // 2][0:w, (t % 2) * D:(t % 2 + 1) * D],
                                act_hi[:, m % 4, cols], act_lo[:, m % 4, cols],
                                wdn_hi[c.wset][:, m, :], wdn_lo[c.wset][:, m, :],
                                m == 0 and t % 2 == 0, m == FM - 1)
                ins.then_inc(dn_done, 1)

            def body(prev, c, nxt):
                if c.expert is None:
                    opening = PIECES if prev is None else None
                else:
                    opening = c.expert * PIECES + 2 * PIECES if c.slot == 0 else None
                for m in range(FM):
                    up(c, m, opening)
                    if m == 4 and nxt is not None:
                        turn(nxt, False)
                    if m >= 2:
                        down(c, m - 2)
                    elif prev is not None:
                        down(prev, m + FM - 2)

            turn(shared_chunk(0, 0), True)
            walk(pe, body)
            last = expert_chunk(E - 1, 1, 1)
            down(last, FM - 2)
            down(last, FM - 1)

        @block.vector
        def _(dve):
            v = nc.vector
            SQ = float(np.sqrt(np.float32(N)))
            nc.vector.memset(zmat[:, :], 0.0).then_inc(tau_ok, 1)
            dve.wait_ge(const_in, 16 * NSMALL)
            v.tensor_scalar(taus[:, :], taus[:, :], 1.0 / SQ, None, ALU.mult).then_inc(tau_ok, 1)
            dve.wait_ge(tau_ok, 2)
            dve.wait_ge(const_ok, NCONST)

            def stats(ch, src, st_, mv_):
                for t in range(GT):
                    ins = v.bn_stats(st_[:, t, :], src(t))
                ch.link(ins)
                dve.sem_inc(dve_go, 1)
                for t in range(GT):
                    ins = v.bn_aggr(mv_[:, t, :], st_[:, t, :])
                ch.link(ins)

            A_STEPS = 2

            def stage_a(g, b, q):
                dve.wait_ge(x_in_s[q % 2], b * (8 * GB) + 16 * (q // 2 + 1))
                ch = Chain(dve, a_chain, g * A_STEPS)
                stats(ch, lambda t: rows[:, q % 2, t, :], st, mv)
                v.tensor_scalar(veA[:, :], mv[:, :, 1], EPS, None, ALU.add).then_inc(a_var, 1)
                dve.wait_ge(a_rstd, g + 1)
                dve.wait_ge(xhi_ok, OPEN + g)
                dve.wait_ge(xlo_ok, OPEN + g)
                dve.wait_ge(xt_ps, OPEN + g)
                for t in range(GT):
                    ins = v.tensor_scalar(xn[:, t, :], rows[:, q % 2, t, :], mv[:, t, 0:1], rstd[:, t:t + 1],
                                          ALU.subtract, ALU.mult)
                ins.then_inc(xn_ok, 1)
                dve.wait_ge(xthi_ok, g + 1)
                for k in range(KC):
                    ins = v.tensor_tensor(xT_lo[:, k, q * GW:(q + 1) * GW], bank[2 + k][:, :],
                                          xT_hi[:, k, q * GW:(q + 1) * GW].bitcast(F32), ALU.subtract)
                ins.then_inc(xtlo_ok, 1)

            M_STEPS = 9

            def stage_m(b):
                ch = Chain(dve, m_chain, b * M_STEPS)
                flat = lambda t: t.rearrange("p k d -> p (k d)")
                dve.wait_ge(m_act, OPEN + b * MA + 1)
                ch.link(v.tensor_tensor(gf[:, :, :], gs[:, :, 0:D], gs[:, :, D:2 * D], ALU.add))
                dve.wait_ge(m_pe, b * MP + 1)
                v.tensor_tensor(gate[:, 0, :], gate[:, 0, :], bank[6][:, :], ALU.add).then_inc(m_dve, 1)
                dve.wait_ge(m_act, OPEN + b * MA + 3)
                v.tensor_tensor(sD[:, :, :], sS[:, :, :], ident[:, :].rearrange("p (a j) -> p a j", a=1)
                                .broadcast_to([P, KC, P]), ALU.mult).then_inc(m_dve, 1)
                dve.wait_ge(m_dve, b * MD + 2)
                v.tensor_reduce(small[:, 0, :], sD[:, :, :], AX.X, ALU.add)
                dve.wait_ge(m_pe, b * MP + 4)
                ch.link(v.scalar_tensor_tensor(out=hfull[:, 0, 0:KC * P], in0=hfull[:, 0, 0:KC * P], scalar=2.0,
                                               in1=bank[7][:, 0:KC * P], op0=ALU.mult, op1=ALU.subtract))
                hm = headmask[:, :, :].rearrange("p h e -> p (h e)").rearrange("p (a j) -> p a j", a=1)
                ch.link(v.tensor_tensor(sS[:, :, :], sS[:, :, :], hm.broadcast_to([P, KC, P]), ALU.mult))
                ch.link(v.tensor_reduce(lc[:, :, :], sS[:, :, :].rearrange("p k (h e) -> p k e h", e=DH),
                                        AX.X, ALU.add))
                for k in range(KC):
                    ins = v.tensor_scalar(lc[:, k, :], lc[:, k, :], small[:, 0, k:k + 1], taus[:, k:k + 1],
                                          ALU.subtract, ALU.mult)
                ch.link(ins)
                ch.link(v.tensor_reduce(small[:, 1, :], lc[:, :, :], AX.X, ALU.max))
                for k in range(KC):
                    ins = v.tensor_scalar(lc[:, k, :], lc[:, k, :], small[:, 1, k:k + 1], None, ALU.subtract)
                ins.then_inc(m_dve, 1)
                dve.wait_ge(m_act, OPEN + b * MA + 4)
                ch.link(v.tensor_reduce(small[:, 2, :], lc[:, :, :], AX.X, ALU.add))
                ch.link(v.reciprocal(small[:, 3, :], small[:, 2, :]))
                for k in range(KC):
                    ins = v.tensor_scalar(lc[:, k, :], lc[:, k, :], small[:, 3, k:k + 1], None, ALU.mult)
                ch.link(ins)
                for k in range(KC):
                    own = lc[:, k, :].rearrange("p (a e) -> p a e", a=1).broadcast_to([P, HB, DH])
                    ins = v.tensor_tensor(sD[:, k, :].rearrange("p (h e) -> p h e", e=DH), headmask[:, :, :],
                                          own, ALU.mult)
                ins.then_inc(m_dve, 1)
                dve.wait_ge(m_act, OPEN + b * MA + 6)
                v.tensor_tensor(flat(m_lo[:, :, :]), bank[7][:, :], flat(m_hi[:, :, :]).bitcast(F32),
                                ALU.subtract).then_inc(m_dve, 1)
                assert ch.n == M_STEPS, ch.n

            B_STEPS = 4

            def stage_b(g):
                ch = Chain(dve, b_chain, g * B_STEPS)
                dve.wait_ge(o_ok, OPEN + g + 1)
                stats(ch, lambda t: bank[4 + t // 2][:, (t % 2) * D:(t % 2 + 1) * D], stB, mvB)
                v.tensor_scalar(veB[:, :], mvB[:, :, 1], EPS, None, ALU.add).then_inc(b_var, 1)
                dve.wait_ge(b_rstd, g + 1)
                v.scalar_tensor_tensor(out=nbiasB[:, :], in0=mvB[:, :, 0], scalar=-1.0, in1=rstdB[:, :],
                                       op0=ALU.mult, op1=ALU.mult).then_inc(b_nb, 1)
                dve.wait_ge(x2_ok, OPEN + g + 1)
                stats(ch, lambda t: x2[:, t, :], st2, mv2)
                v.tensor_scalar(ve2[:, :], mv2[:, :, 1], 1.0 + EPS, EPS * EPS, ALU.mult, ALU.add).then_inc(b_var2, 1)
                dve.wait_ge(b_rstd2, g + 1)
                dve.wait_ge(u_out, OPEN + g * 16)
                dve.wait_ge(ut_ps, OPEN + g)
                for t in range(GT):
                    ins = v.tensor_scalar(u[:, t, :], x2[:, t, :], mv2[:, t, 0:1], rstd2[:, t:t + 1],
                                          ALU.subtract, ALU.mult)
                ins.then_inc(u_ok, 1)
                dve.wait_ge(lg_ps, OPEN + g + 1)
                v.tensor_copy(lg[:, :, bass.ds(g * GT, GT)],
                              bank[7][:, 0:GT * 8].rearrange("p (t e) -> p e t", e=8)[:, 0:E, :]).then_inc(lg_ok, 1)
                assert ch.n == B_STEPS

            with dve.Fori(0, B) as b:
                for q in range(GB):
                    stage_a(b * GB + q, b, q)
                stage_m(b)
                for q in range(GB):
                    stage_b(b * GB + q)

            ch = Chain(dve, r_chain, 0)
            dve.wait_ge(lg_ok, OPEN + NG)
            dve.wait_ge(x2_ok, OPEN + NG)
            dve.wait_ge(xlo_ok, OPEN + NG)
            over_e = lambda a: a.rearrange("p (a t) -> p a t", a=1).broadcast_to([P, E, NT])
            over_t = lambda a: a.rearrange("p (e a) -> p e a", a=1).broadcast_to([P, E, NT])
            by_t = lambda a: a.rearrange("p e t -> p t e")
            best = rsmall[:, 3, :].rearrange("p (c t) -> p c t", c=2)
            scores = lg
            for c in range(2):
                ch.link(v.tensor_reduce(best[:, c, :], by_t(scores[:, :, :]), AX.X, ALU.max))
                ch.link(v.tensor_tensor(rt[0], scores[:, :, :], over_e(best[:, c, :]), ALU.is_equal))
                ch.link(v.tensor_tensor(rt[0], rt[0], over_t(rank[:, :]), ALU.mult))
                ch.link(v.tensor_reduce(rsmall[:, 2, 0:NT], by_t(rt[0]), AX.X, ALU.max))
                v.tensor_tensor(oh[:, c, :, :], rt[0], over_e(rsmall[:, 2, 0:NT]), ALU.is_equal).then_inc(r_oh, 1)
                dve.wait_ge(r_oh, c + 1)
                if c == 0:
                    ch.link(v.scalar_tensor_tensor(out=lg[:, :, :], in0=oh[:, 0, :, :], scalar=-BIG,
                                                   in1=lg[:, :, :], op0=ALU.mult, op1=ALU.add))
            v.tensor_tensor(rsmall[:, 0, 0:NT], best[:, 1, :], best[:, 0, :], ALU.subtract).then_inc(r_d, 1)
            dve.wait_ge(r_ex, 1)
            ch.link(v.tensor_scalar(rsmall[:, 0, 0:NT], rsmall[:, 1, 0:NT], 1.0, None, ALU.add))
            ch.link(v.reciprocal(gates[:, 0, :], rsmall[:, 0, 0:NT]))
            ch.link(v.tensor_tensor(gates[:, 1, :], gates[:, 0, :], rsmall[:, 1, 0:NT], ALU.mult))
            flat = lambda a: a.rearrange("p e t -> p (e t)")
            pos = rsmall[:, 0, :].rearrange("p (c t) -> p c t", c=2)
            first = rsmall[:, 2, :].rearrange("p (c t) -> p c t", c=2)
            for c in range(2):
                dve.wait_ge(r_cnt, c + 1)
                ch.link(v.tensor_tensor_scan(rincl, flat(carry[:, :, :]), bank[2 * c + 1][:, 0:E * NT], 0.0,
                                             ALU.mult, ALU.add))
                if c == 0:
                    ch.link(v.tensor_copy(total[:, :], rincl.rearrange("p (e t) -> p e t", e=E)[:, :, NT - 1]))
                ch.link(v.tensor_tensor(flat(rt[0]), rincl, bank[2 * c + 1][:, 0:E * NT], ALU.subtract))
                ch.link(v.tensor_tensor(flat(rt[0]), flat(rt[0]), bank[2 * c][:, 0:E * NT], ALU.add))
                if c == 1:
                    ch.link(v.tensor_tensor(rt[0], rt[0], over_t(total[:, :]), ALU.add))
                ch.link(v.tensor_tensor(rt[0], rt[0], oh[:, c, :, :], ALU.mult))
                ch.link(v.tensor_reduce(pos[:, c, :], by_t(rt[0]), AX.X, ALU.add))
                ch.link(v.tensor_tensor(rt[0], over_t(estep[:, :]), oh[:, c, :, :], ALU.mult))
                ch.link(v.tensor_reduce(first[:, c, :], by_t(rt[0]), AX.X, ALU.add))
            ch.link(v.tensor_scalar(slotcol[:, :, :], pos, float(P), None, ALU.is_ge))
            for j in range(2, ST):
                ch.link(v.scalar_tensor_tensor(out=slotcol[:, :, :], in0=pos, scalar=float(P * j),
                                               in1=slotcol[:, :, :], op0=ALU.is_ge, op1=ALU.add))
            ch.link(v.scalar_tensor_tensor(out=slotm[:, :, :], in0=slotcol[:, :, :], scalar=-float(P), in1=pos,
                                           op0=ALU.mult, op1=ALU.add))
            ch.link(v.tensor_scalar(best, pos, float(CAP), None, ALU.is_lt))
            ch.link(v.scalar_tensor_tensor(out=slotm[:, :, :], in0=slotm[:, :, :], scalar=1.0, in1=best,
                                           op0=ALU.add, op1=ALU.mult))
            ch.link(v.tensor_tensor(slotcol[:, :, :], slotcol[:, :, :], first, ALU.add))
            dve.wait_ge(u_out, OPEN + 16 * NG)
            dve.wait_ge(x2_out, OPEN + 16 * NG)
            with dve.Fori(0, NT // RB) as i:
                for c in range(2):
                    cut = bass.ds(i * RB, RB)
                    wide = lambda a, n: a.rearrange("p (t a) -> p t a", a=1).broadcast_to([P, RB, n])
                    row = lambda a, n: a.rearrange("p (a m) -> p a m", a=1).broadcast_to([P, RB, n])
                    dve.wait_ge(r_mm, OPEN + i * 2)
                    v.tensor_tensor(selA[:, c, :, :], row(slot1[:, :], P), wide(slotm[:, c, cut], P), ALU.is_equal)
                    v.tensor_tensor(selE[c], row(colid[:, :], NC), wide(slotcol[:, c, cut], NC),
                                    ALU.is_equal).then_inc(r_selE, 1)
                    dve.wait_ge(r_selE, i * 2 + (c + 1))
                    v.tensor_tensor(selB[:, c, :, 0, :], selE[c], wide(tokid[:, cut], NC), ALU.mult)
                    v.tensor_tensor(selB[:, c, :, 1, :], selE[c], wide(gates[:, c, cut], NC), ALU.mult).then_inc(r_sel, 1)
            dve.wait_ge(r_mm, OPEN + 2 * NT // RB)
            ch = Chain(dve, r_tab, 0)
            ch.link(v.tensor_copy(table2[:, :], bank[4][:, 0:2 * NC]))
            v.tensor_scalar(gidx[:, :], table2[:, 0:NC], -1.0, 0.0, ALU.add, ALU.max)
            ch.link(v.tensor_scalar(tabe[:, :], table2[:, 0:NC], 0.0, None, ALU.is_equal))
            ch.link(v.tensor_tensor(tabe[:, :], tabe[:, :], spare[:, :, :].rearrange("p e s -> p (e s)"), ALU.mult))
            ch.link(v.tensor_tensor(tabe[:, :], tabe[:, :], table2[:, 0:NC], ALU.add))
            v.tensor_scalar(sidx[:, :], tabe[:, :], -1.0, None, ALU.add).then_inc(r_idx, 1)

            def prep(c, before):
                dve.wait_ge(hhi_ok, c.n + 1)
                if before:
                    dve.wait_ge(b_ps, (c.n - 1) * FM)
                v.tensor_tensor(h_lo[:, c.slot, :, 0:c.w], hfull[:, :, 0:c.w],
                                h_hi[:, c.slot, :, 0:c.w].bitcast(F32), ALU.subtract).then_inc(hlo_ok, 1)

            def low(c, m):
                dve.wait_ge(ahi_ok, c.n * FM + (m + 1))
                if not (isinstance(c.n, int) and c.n * FM + m - 3 <= 0):
                    dve.wait_ge(dn_done, c.n * FM + (m - 3))
                v.tensor_tensor(act_lo[:, m % 4, 0:c.w], act[:, m % 2, 0:c.w],
                                act_hi[:, m % 4, 0:c.w].bitcast(F32), ALU.subtract).then_inc(alo_ok, 1)

            def body(prev, c, nxt):
                for m in range(FM):
                    dve.wait_ge(silu_ok, c.n * FM + (m + 1))
                    dve.wait_ge(b_ps, c.n * FM + (m + 1))
                    if not (isinstance(c.n, int) and c.n * FM + m - 1 <= 0):
                        dve.wait_ge(alo_ok, c.n * FM + (m - 1))
                    v.tensor_tensor(act[:, m % 2, 0:c.w], bank[2 * (m % 2) + 1][:, 0:c.w], gate[:, m % 2, 0:c.w],
                                    ALU.mult).then_inc(act_ok, 1)
                    if m > 0:
                        low(c, m - 1)
                    elif prev is not None:
                        low(prev, FM - 1)
                    if m == 6 and nxt is not None:
                        prep(nxt, True)

            prep(shared_chunk(0, 0), False)
            walk(dve, body)
            low(expert_chunk(E - 1, 1, 1), FM - 1)

            with dve.Fori(0, NG // 2) as i:
                for s in range(2):
                    g = i * 2 + s
                    ch = Chain(dve, t_chain, g * 3)
                    dve.wait_ge(t_y[s], i * 16 + 16)
                    stats(ch, lambda t: rows[:, s, t, :], st, mv)
                    v.tensor_scalar(veA[:, :], mv[:, :, 1], EPS, None, ALU.add).then_inc(t_var, 1)
                    dve.wait_ge(t_rstd, g + 1)
                    for t in range(GT):
                        ins = v.tensor_scalar(rows[:, s, t, :], rows[:, s, t, :], mv[:, t, 0:1], rstd[:, t:t + 1],
                                              ALU.subtract, ALU.mult)
                    ch.link(ins)
                    dve.wait_ge(t_x[s], i * 16 + 16)
                    v.tensor_tensor(res[s][:, :, :], res[s][:, :, :], rows[:, s, :, :], ALU.add).then_inc(t_ok, 1)


_INS = ['L0_attn_x', 'L0_attn_Wqk', 'L0_attn_Wv', 'L0_attn_Wo', 'L0_attn_tau', 'L0_ffn_ln_g', 'L0_ffn_ln_b',
        'L0_ffn_Wr', 'L0_ffn_W1', 'L0_ffn_W3', 'L0_ffn_W2', 'L0_ffn_W1s', 'L0_ffn_W3s', 'L0_ffn_W2s']


def kernel(**inputs):
    import numpy as _np
    import concourse.bacc as _bacc
    from concourse import mybir as _mybir
    from concourse.bass_utils import run_bass_kernel_spmd as _run

    nc = _bacc.Bacc("TRN2", target_bir_lowering=False, num_devices=1)
    arrays, args = {}, []
    for name in _INS:
        a = _np.ascontiguousarray(inputs[name])
        arrays[f"in_{name}_dram"] = a
        args.append(nc.dram_tensor(f"in_{name}_dram", a.shape, _mybir.dt.from_np(a.dtype), kind="ExternalInput").ap())
    shape = arrays["in_L0_attn_x_dram"].shape
    args.append(nc.dram_tensor("out_0_dram", shape, _mybir.dt.float32, kind="ExternalOutput").ap())
    sandwich_kernel(nc, *args)
    r = _run(nc, [arrays], core_ids=[0])
    return r.results[0]["out_0_dram"]
```

```python
from contextlib import ExitStack

import numpy as np

import concourse.bass as bass
from concourse import mybir

ALU = mybir.AluOpType
ACT = mybir.ActivationFunctionType
AX = mybir.AxisListType
F32 = mybir.dt.float32
F32R = mybir.dt.float32r
BF16 = mybir.dt.bfloat16
I32 = mybir.dt.int32
U32 = mybir.dt.uint32

P = 128
EPS = 1e-5
BIG = 3.0e38
OPEN = 4
TOP_K = 2
NOMINAL_TOKENS = 4 * 512


class Chain:

    def __init__(self, eng, sem, base):
        self.eng, self.sem, self.base, self.n = eng, sem, base, 0

    def step(self, ins):
        self.n += 1
        ins.then_inc(self.sem, 1)

    def settle(self):
        self.eng.wait_ge(self.sem, self.base + self.n)

    def link(self, ins):
        self.step(ins)
        self.settle()


def sandwich_kernel(nc, x_in, Wqk, Wv, Wo, tau, ln_g, ln_b, Wr, W1, W3, W2, W1s, W3s, W2s, out):
    B, N, D = x_in.shape
    T = B * N
    H = tau.shape[0]
    DH = D // H
    KC = D // P
    HB = P // DH
    F = W1s.shape[1]
    FM = F // P
    E = Wr.shape[1]
    CAP = -(-int(NOMINAL_TOKENS * TOP_K * 5) // (4 * E))
    GT = 4
    GW = GT * P
    NT = T // P
    NG = T // GW
    GB = N // GW
    TB = N // P
    ST = -(-CAP // P)
    LASTW = CAP - (ST - 1) * P
    HALF = ST // 2
    NC = E * ST
    assert D == KC * P and ST == 6 and E == 7 and GB == 4 and FM == 8

    x_t = x_in.rearrange("b n d -> (b n) d").rearrange("(g t p) d -> g p t d", p=P, t=GT)
    out_t = out.rearrange("b n d -> (b n) d").rearrange("(g t p) d -> g p t d", p=P, t=GT)
    x2_d = nc.dram_tensor("x2_scratch", (T, D), F32, kind="Internal").ap()
    u_d = nc.dram_tensor("u_scratch", (T, D), F32, kind="Internal").ap()
    y_d = nc.dram_tensor("y_scratch", (T + ST * P, D), F32, kind="Internal").ap()
    x2_t = x2_d.rearrange("(g t p) d -> g p t d", p=P, t=GT)
    u_t = u_d.rearrange("(g t p) d -> g p t d", p=P, t=GT)
    y_t = y_d[0:T, :].rearrange("(g t p) d -> g p t d", p=P, t=GT)
    y_spare = y_d[T:T + ST * P, :].rearrange("(t p) d -> t p d", p=P)

    with ExitStack() as ctx:
        def sb(name, shape, dt=F32):
            return ctx.enter_context(nc.sbuf_tensor("sb_" + name, shape, dt))

        def sem(name):
            return ctx.enter_context(nc.semaphore(name))

        bank = [ctx.enter_context(nc.psum_tensor(f"bank{i}", [P, 512], F32)) for i in range(8)]

        ident = sb("ident", [P, P])
        ones = sb("ones", [P, P])
        zrow = sb("zrow", [P, D])
        onesb = sb("onesb", [P, P], BF16)
        earlier = sb("earlier", [P, P], BF16)
        headmask = sb("headmask", [P, HB, DH])
        slot1 = sb("slot1", [P, P])
        colid = sb("colid", [P, NC])
        rank = sb("rank", [P, E])
        estep = sb("estep", [P, E])
        tokid = sb("tokid", [P, NT])
        spare = sb("spare", [P, E, ST])
        carry = sb("carry", [P, E, NT])
        mhalf = sb("mhalf", [P, GT])
        wqk = sb("wqk", [P, KC, D])
        wvT = sb("wvT", [P, KC, D])
        wo = sb("wo", [P, KC, D])
        wr = sb("wr", [P, KC, E])
        gcol = sb("gcol", [P, KC])
        bcol = sb("bcol", [P, KC])
        taus = sb("taus", [P, KC])
        wup_hi = [sb(f"wup_hi{s}", [P, 2, KC, F], F32R) for s in range(2)]
        wup_lo = [sb(f"wup_lo{s}", [P, 2, KC, F], F32R) for s in range(2)]
        wdn_hi = [sb(f"wdn_hi{s}", [P, FM, D], F32R) for s in range(2)]
        wdn_lo = [sb(f"wdn_lo{s}", [P, FM, D], F32R) for s in range(2)]
        xT_hi = wup_hi[1][:, :, :, :].rearrange("p a k f -> p (a k f)").rearrange("p (k n) -> p k n", k=KC)
        xT_lo = wup_lo[1][:, :, :, :].rearrange("p a k f -> p (a k f)").rearrange("p (k n) -> p k n", k=KC)
        xx = wdn_hi[1][:, :, :].rearrange("p m d -> p (m d)").rearrange("p (t h d) -> p t h d", h=2, d=D)
        xin = sb("xin", [P, 2, GT, D])
        xn = sb("xn", [P, GT, D])
        ln_o = sb("ln_o", [P, GT, D])
        x2 = sb("x2", [P, 2, GT, D])
        u = sb("u", [P, GT, D])
        hr = sb("hr", [P, KC, GW])
        rows = sb("rows", [P, 2, GT, D])
        ysb = sb("ysb", [P, 2, GT, D])
        hfull = sb("hfull", [P, KC, GW])
        h_hi = sb("h_hi", [P, 2, KC, GW], F32R)
        h_lo = sb("h_lo", [P, 2, KC, GW], F32R)
        act = sb("act", [P, 2, GW])
        act_hi = sb("act_hi", [P, 4, GW], F32R)
        act_lo = sb("act_lo", [P, 4, GW], F32R)
        flat4 = lambda a: a.rearrange("p t d -> p (t d)")
        stage_first = [flat4(rows[:, 0, :, :]), flat4(rows[:, 1, :, :]), flat4(ysb[:, 0, :, :])]
        stage_later = [flat4(xin[:, 0, :, :]), flat4(xin[:, 1, :, :]), flat4(xn[:, :, :])]
        TR, TY = 8, 4
        as_rows = lambda a: a.rearrange("p k (t d) -> p (k t) d", d=D)
        last_x = [x2[:, 0, :, :], x2[:, 1, :, :], ln_o[:, :, :], u[:, :, :],
                  xin[:, 0, :, :], xin[:, 1, :, :], xn[:, :, :], as_rows(hr[:, :, :])]
        last_y = [rows[:, 0, :, :], rows[:, 1, :, :], ysb[:, 0, :, :], ysb[:, 1, :, :]]
        st = sb("st", [P, GT, 6])
        mv = sb("mv", [P, GT, 2])
        rstd = sb("rstd", [P, GT])
        nbias = sb("nbias", [P, GT])
        t_scale = [sb(f"t_scale{k}", [P, GT])[:, :] for k in range(2)]
        stB = sb("stB", [P, GT, 6])
        mvB = sb("mvB", [P, GT, 2])
        rstdB = sb("rstdB", [P, GT])
        nbiasB = sb("nbiasB", [P, GT])
        veB = sb("veB", [P, GT])
        st2 = sb("st2", [P, GT, 6])
        mv2 = sb("mv2", [P, GT, 2])
        ve2 = sb("ve2", [P, GT])
        rstd2 = sb("rstd2", [P, GT])
        veA = sb("veA", [P, GT])
        gs = flat4(ln_o[:, :, :]).rearrange("p (k j) -> p k j", k=KC)
        gf, tsb = u[:, 0:KC, :], u[:, KC:2 * KC, :]
        sS = hr[:, 0, 0:KC * P].rearrange("p (k j) -> p k j", k=KC)
        sD = hr[:, 0, KC * P:2 * KC * P].rearrange("p (k j) -> p k j", k=KC)
        lc = sb("lc", [P, KC, DH])
        small = sb("small", [P, 8, KC])
        m_hi = sb("m_hi", [P, KC, D], F32R)
        m_lo = sb("m_lo", [P, KC, D], F32R)
        lg = sb("lg", [P, E, NT])
        oh = sb("oh", [P, 2, E, NT], BF16)
        slotcol = sb("slotcol", [P, 2, NT])
        slotm = sb("slotm", [P, 2, NT])
        gates = sb("gates", [P, 2, NT])
        table2 = sb("table2", [P, 2 * NC])
        tabe = sb("tabe", [P, NC])
        total = sb("total", [P, E])
        gidx = sb("gidx", [P, NC], U32)
        gcur = sb("gcur", [P, 2, HALF], U32)
        scur = sb("scur", [P, 2, HALF], U32)
        sidx = sb("sidx", [P, NC], U32)
        rt = flat4(u[:, :, :])[:, 0:E * NT].rearrange("p (e t) -> p e t", e=E)
        rincl = hr[:, 0, 0:E * NT]
        rsmall = hr[:, 1, :].rearrange("p (a t) -> p a t", t=2 * NT)
        RB = 4
        selA = flat4(x2[:, 0, :, :]).rearrange("p (s t m) -> p s t m", s=2, t=RB)
        selB = flat4(x2[:, 1, :, :])[:, 0:2 * RB * 2 * NC].rearrange("p (s t a c) -> p s t a c", s=2, t=RB, a=2)
        selE = flat4(ln_o[:, :, :])[:, 0:2 * RB * NC].rearrange("p (s t c) -> p s t c", s=2, t=RB)

        pool_go = sem("pool_go")
        dve_go = sem("dve_go")
        sp_go = sem("sp_go")
        const_in = sem("const_in")
        const_ok = sem("const_ok")
        tau_ok = sem("tau_ok")
        wvT_ps = sem("wvT_ps")
        wvT_ok = sem("wvT_ok")
        x_in_s = [sem(f"x_in{i}") for i in range(2)]
        a_chain = sem("a_chain")
        a_var = sem("a_var")
        a_rstd = sem("a_rstd")
        xn_ok = sem("xn_ok")
        xhi_ok = sem("xhi_ok")
        xlo_ok = sem("xlo_ok")
        xt_ps = sem("xt_ps")
        xthi_ok = sem("xthi_ok")
        xtlo_ok = sem("xtlo_ok")
        g_done = sem("g_done")
        m_chain = sem("m_chain")
        m_pe = sem("m_pe")
        m_act = sem("m_act")
        m_dve = sem("m_dve")
        o_ok = sem("o_ok")
        b_chain = sem("b_chain")
        u_chain = sem("u_chain")
        b_var = sem("b_var")
        b_rstd = sem("b_rstd")
        b_nb = sem("b_nb")
        lno_ok = sem("lno_ok")
        xres_in = [sem(f"xres_in{i}") for i in range(2)]
        x2_ok = sem("x2_ok")
        x2_out = [sem(f"x2_out{i}") for i in range(2)]
        b_var2 = sem("b_var2")
        b_rstd2 = sem("b_rstd2")
        u_ok = sem("u_ok")
        u_out = sem("u_out")
        ut_ps = sem("ut_ps")
        hT_ok = sem("hT_ok")
        lg_ps = sem("lg_ps")
        lg_ok = sem("lg_ok")
        r_chain = sem("r_chain")
        r_oh = sem("r_oh")
        r_d = sem("r_d")
        r_ex = sem("r_ex")
        r_cnt = sem("r_cnt")
        r_sel = sem("r_sel")
        r_selE = sem("r_selE")
        r_scan = sem("r_scan")
        r_mm = sem("r_mm")
        r_tab = sem("r_tab")
        r_idx = sem("r_idx")
        stage_in = [sem(f"stage_in{i}") for i in range(3)]
        w_hi = sem("w_hi")
        w_lo = sem("w_lo")
        rows_in = [sem(f"rows_in{i}") for i in range(2)]
        gathered = [sem(f"gathered{i}") for i in range(2)]
        added = [sem(f"added{i}") for i in range(2)]
        ysb_free = [sem(f"ysb_free{i}") for i in range(2)]
        ht_ps = sem("ht_ps")
        hf_ok = sem("hf_ok")
        hhi_ok = sem("hhi_ok")
        hlo_ok = sem("hlo_ok")
        a_ps = sem("a_ps")
        b_ps = sem("b_ps")
        silu_ok = sem("silu_ok")
        act_ok = sem("act_ok")
        ahi_ok = sem("ahi_ok")
        alo_ok = sem("alo_ok")
        dn_done = sem("dn_done")
        y_sb = sem("y_sb")
        g_cur = sem("g_cur")
        s_cur = sem("s_cur")
        y_out = [sem(f"y_out{i}") for i in range(2)]
        spare_z = sem("spare_z")
        spare_out = sem("spare_out")
        t_y = [sem(f"t_y{i}") for i in range(TY)]
        t_x = [sem(f"t_x{i}") for i in range(TR)]
        t_chain = sem("t_chain")
        t_nb = sem("t_nb")
        t_act = sem("t_act")
        t_var = sem("t_var")
        t_rstd = sem("t_rstd")
        t_ok = sem("t_ok")
        t_okp = sem("t_okp")
        t_out = [sem(f"t_out{i}") for i in range(TR)]

        NCONST = 17
        NSMALL = 6 + HB
        MA, MP, MD = 6, 6, 5
        PIECES = 6

        class Chunk:
            def __init__(self, n, slot, wset, widths, landed, expert=None, wide=False):
                self.n, self.slot, self.wset, self.widths = n, slot, wset, widths
                self.landed, self.expert, self.w = landed, expert, sum(widths)
                self.wide = wide

        def shared_chunk(b, j, wide=False):
            return Chunk(b * GB + j, j % 2, 0, [P] * GT, b * (8 * GB) + 16 * (j // 2 + 1), wide=wide)

        def expert_chunk(e, part, wset):
            widths = [P] * HALF if part == 0 else [P] * (HALF - 1) + [LASTW]
            return Chunk(e * 2 + (NG + part), part, wset, widths, e * (16 * HALF) + 16 * HALF, e, True)

        def last_chunks():
            return [shared_chunk(B - 1, j, j > 0) for j in range(GB)] + [expert_chunk(0, 0, 1)]

        def routed_chunks(eng, body):
            body(shared_chunk(B - 1, GB - 1, True), expert_chunk(0, 0, 1), expert_chunk(0, 1, 1))
            with eng.Fori(0, (E - 1) // 2) as i:
                seq = [expert_chunk(i * 2, 0, 1), expert_chunk(i * 2, 1, 1), expert_chunk(i * 2 + 1, 0, 0),
                       expert_chunk(i * 2 + 1, 1, 0), expert_chunk(i * 2 + 2, 0, 1), expert_chunk(i * 2 + 2, 1, 1)]
                for j in range(1, 5):
                    body(seq[j - 1], seq[j], seq[j + 1])
            body(expert_chunk(E - 1, 0, 1), expert_chunk(E - 1, 1, 1), None)

        NCH = NG + 2 * E

        def piece(j, wset, stage):
            if j < 4:
                return wup_hi[wset][:, j // 2, j % 2, :], wup_lo[wset][:, j // 2, j % 2, :], stage[j % 3]
            m0 = (j - 4) * (FM // 2)
            return (wdn_hi[wset][:, m0:m0 + FM // 2, :], wdn_lo[wset][:, m0:m0 + FM // 2, :],
                    stage[j % 3].rearrange("p (m d) -> p m d", d=D))

        PLACES = 2 * FM * GB
        timetable = [[] for _ in range(PLACES)]
        for q in range(GB):
            for name, at in (("x_stats", 0), ("x_norm", 3), ("x_turn0", 4), ("x_low0", 5), ("x_turn1", 6),
                             ("x_gram", 7)):
                timetable[4 * q + at].append((name, q))
        for name, at in (("m_gram", 20), ("m_turn", 22), ("m_sym", 23), ("m_times_wqk", 24), ("m_keep_t", 25),
                         ("m_dots", 26), ("m_keep_s", 27), ("m_diag", 28), ("m_rowdiag", 30), ("m_logits", 31),
                         ("m_exp", 32), ("m_softmax", 33), ("m_times_wo", 34), ("m_keep_n", 35),
                         ("m_times_wv", 36), ("m_high", 36), ("m_low", 37)):
            timetable[at].append((name, 0))
        for q in range(GB):
            for name, at in (("o_mix", 0), ("o_stats", 1), ("o_norm", 3), ("o_add", 4), ("u_stats", 6),
                             ("u_norm", 9), ("u_turn0", 10), ("u_turn1", 11), ("u_route", 12)):
                timetable[38 + 4 * q + at].append((name, q))

        def o_bank(b, q):
            return 2 if isinstance(b, int) and b == 0 and q % 2 else 4

        shared_at = {9: 0, 13: 1, 17: 2, 20: 3, 24: 4, 28: 5}

        WEIGHTS_AT = (1, 3, 5, 7, 9, 11)

        def attend(steps, place, b):
            for name, q in timetable[place]:
                if name in steps:
                    steps[name](b, q)

        NR = 18
        NBLK = 2 * (NT // RB)
        R_IDX = NR + NBLK + 1

        def last_add(v, eng, i, k, go, tiles, done):
            eng.wait_ge(t_x[k], i * 16 + 16)
            eng.wait_ge(t_act, i * TR + (k + 1))
            eng.sem_inc(go, 1)
            v.tensor_tensor(flat4(last_x[k][:, tiles, :]), flat4(last_x[k][:, tiles, :]),
                            flat4(last_y[k % TY][:, tiles, :]), ALU.add).then_inc(done, 1)

        block = ctx.enter_context(nc.Block())

        @block.sync
        def _(sp):
            for opened in (xtlo_ok, hT_ok, g_done, o_ok, m_act, lno_ok, x2_ok, *x2_out, u_ok, u_out, ut_ps, lg_ps,
                           lg_ok, xhi_ok, xlo_ok, xt_ps, xn_ok, b_ps, ht_ps, act_ok, silu_ok, alo_ok, dn_done,
                           y_sb, *y_out):
                sp.sem_inc(opened, OPEN)

            def load_piece(w, j, up, dn, stage):
                if not (isinstance(w, int) and w == 0 and j < 3):
                    sp.wait_ge(w_lo, w * PIECES + (j - 2))
                    sp.sem_inc(sp_go, 1)
                if j < 4:
                    src = up[j // 2][(j % 2) * P:(j % 2 + 1) * P, :]
                    dst = stage[j % 3]
                else:
                    half = FM // 2
                    src = dn.rearrange("(m p) d -> p m d", p=P)[:, (j - 4) * half:(j - 3) * half, :]
                    dst = stage[j % 3].rearrange("p (m d) -> p m d", d=D)
                sp.dma_start(dst, src).then_inc(stage_in[j % 3], 16)

            def load_x(b, q):
                sp.dma_start(xin[:, q % 2, :, :], x_t[b * GB + q]).then_inc(x_in_s[q % 2], 16)

            def first_x(b, q):
                if q == 0:
                    for k in range(2):
                        sp.wait_ge(xn_ok, OPEN + b * GB + (k - 1 if k else 0))
                        sp.sem_inc(sp_go, 1)
                        load_x(b, k)

            def next_x(b, q):
                if q < 2:
                    sp.wait_ge(xn_ok, OPEN + b * GB + (q + 1))
                    sp.sem_inc(sp_go, 1)
                    load_x(b, q + 2)

            def load_res(b, q):
                sp.wait_ge(u_ok, OPEN + b * GB + (q - 1 if q >= 2 else 0))
                sp.sem_inc(sp_go, 1)
                sp.wait_ge(x2_out[q % 2], OPEN + b * (16 * (GB // 2)) + 16 * (q // 2))
                sp.sem_inc(sp_go, 1)
                sp.dma_start(x2[:, q % 2, :, :], x_t[b * GB + q]).then_inc(xres_in[q % 2], 16)

            def first_res(b, q):
                for k in range(2):
                    load_res(b, k)

            def store_x2(b, q):
                sp.wait_ge(x2_ok, OPEN + b * GB + (q + 1))
                sp.sem_inc(sp_go, 1)
                sp.dma_start(x2_t[b * GB + q], x2[:, q % 2, :, :]).then_inc(x2_out[q % 2], 16)

            def store_u(b, q):
                sp.wait_ge(u_ok, OPEN + b * GB + (q + 1))
                sp.sem_inc(sp_go, 1)
                sp.dma_start(u_t[b * GB + q], u[:, :, :]).then_inc(u_out, 16)
                if q < 2:
                    load_res(b, q + 2)

            steps = {"x_norm": next_x, "m_dots": first_res, "u_stats": store_x2, "u_turn0": store_u}

            def load_rows(b, j):
                n = b * GB + j
                sp.wait_ge(u_out, OPEN + n * 16 + 16)
                sp.sem_inc(sp_go, 1)
                if not (isinstance(n, int) and n < 2):
                    sp.wait_ge(ht_ps, OPEN + n * 2 - 2)
                sp.sem_inc(sp_go, 1)
                sp.sem_inc(sp_go, 1)
                sp.dma_start(rows[:, j % 2, :, :], u_t[n]).then_inc(rows_in[j % 2], 16)

            def store_y(b, j):
                sp.wait_ge(y_sb, OPEN + b * GB + (j + 1))
                sp.sem_inc(sp_go, 1)
                sp.dma_start(y_t[b * GB + j], ysb[:, j % 2, :, :]).then_inc(y_out[j % 2], 16)

            first_x(0, 0)
            for dst, src in ((wqk, Wqk), (tsb, Wv), (wo, Wo), (wr, Wr)):
                sp.dma_start(dst if dst is tsb else dst[:, :, :],
                             src.rearrange("(k p) n -> p k n", p=P)).then_inc(const_in, 16)
            with nc.allow_non_contiguous_dma(reason="vectors of 256 values"):
                for dst, src in ((gcol, ln_g), (bcol, ln_b)):
                    sp.dma_start(dst[:, :], src.rearrange("(k p) -> p k", p=P)).then_inc(const_in, 16)
                for h in range(HB):
                    src = tau.rearrange("(k h) a b -> (a b) h k", h=HB)[:, h, :]
                    sp.dma_start(taus[h * DH:(h + 1) * DH, :], src.broadcast_to([DH, KC])).then_inc(const_in, 16)
            for j in range(ST):
                sp.wait_ge(const_ok, NCONST)
                sp.sem_inc(sp_go, 1)
                sp.dma_start(y_spare[j], zrow[:, :]).then_inc(spare_out, 16)
            for place in range(PLACES):
                attend(steps, place, 0)
                if place in (2, 10):
                    for j in ((0, 1, 2) if place == 2 else (3, 4, 5)):
                        load_piece(0, j, [W1s, W3s], W2s, stage_first)
            sp.wait_ge(w_lo, PIECES)
            sp.sem_inc(sp_go, 1)
            load_rows(0, 0)

            with sp.Fori(1, B) as b:
                first_x(b, 0)
                for place in range(PLACES):
                    j, step = place // (2 * FM), place % (2 * FM)
                    if step == 2:
                        if j < GB - 1:
                            load_rows(b - 1, j + 1)
                        else:
                            load_rows(b, 0)
                    if step == 6 and j > 0:
                        store_y(b - 1, j - 1)
                    attend(steps, place, b)
                store_y(b - 1, GB - 1)
            b = B - 1
            load_rows(b, 1)
            for k in range(4):
                sp.wait_ge((xn_ok, xlo_ok, xt_ps, xt_ps)[k], OPEN + NG * (1, 1, 2, 2)[k])
                sp.sem_inc(sp_go, 1)
            for j in range(PIECES):
                load_piece(1, j, [W1[0], W3[0]], W2[0], stage_later)
            for j in range(GB):
                if 1 <= j < GB - 1:
                    load_rows(b, j + 1)
                if j > 0:
                    store_y(b, j - 1)
            store_y(b, GB - 1)
            with sp.Fori(0, E - 1) as e:
                for j in range(PIECES):
                    load_piece(e + 2, j, [W1[e + 1], W3[e + 1]], W2[e + 1], stage_later)
            sp.wait_ge(r_idx, 1)
            for k in range(2):
                sp.wait_ge(x2_out[k], OPEN + 16 * (NG // 2))
            for k in range(TR):
                if k == 4:
                    sp.wait_ge(w_lo, PIECES * (E + 1))
                sp.dma_start(last_x[k], x2_t[k]).then_inc(t_x[k], 16)
            sp.wait_ge(ht_ps, OPEN + 2 * NCH)
            for k in range(2):
                sp.wait_ge(added[k], 16 * HALF * E)
            for k in range(TY):
                sp.dma_start(last_y[k], y_t[k]).then_inc(t_y[k], 16)

            def last_round(i, more):
                for k in range(TR):
                    sp.wait_ge(t_ok, i * TR + (k + 1))
                    sp.sem_inc(sp_go, 1)
                    sp.wait_ge(t_okp, i * TR + (k + 1))
                    sp.sem_inc(sp_go, 1)
                    sp.dma_start(out_t[i * TR + k], last_x[k]).then_inc(t_out[k], 16)
                    if more or k < TR - TY:
                        sp.dma_start(last_y[k % TY], y_t[i * TR + (k + TY)]).then_inc(t_y[k % TY], 16)
                    if more and k >= 2:
                        refill(i, k - 2)
                if more:
                    refill(i, TR - 2)
                    refill(i, TR - 1)

            def refill(i, k):
                sp.wait_ge(t_out[k], i * 16 + 16)
                sp.sem_inc(sp_go, 1)
                sp.dma_start(last_x[k], x2_t[i * TR + (k + TR)]).then_inc(t_x[k], 16)
            with sp.Fori(0, NG // TR - 1) as i:
                last_round(i, True)
            last_round(NG // TR - 1, False)
            for k in range(TR):
                sp.wait_ge(t_out[k], 16 * (NG // TR))

        @block.gpsimd
        def _(pool):
            v = nc.gpsimd
            n_const = [0]

            def made(ins, settle=False):
                n_const[0] += 1
                ins.then_inc(const_ok, 1)
                if settle:
                    pool.wait_ge(const_ok, n_const[0])
            made(v.memset(mhalf[:, :], -0.5))
            made(v.memset(ones[:, :], 1.0))
            made(v.memset(onesb[:, :], 1.0))
            made(v.memset(zrow[:, :], 0.0))
            made(v.memset(headmask[:, :, :], 1.0))
            made(v.memset(carry[:, :, :], 1.0))
            made(v.iota(slot1[:, :], [[1, P]], base=1, channel_multiplier=0, allow_small_or_imprecise_dtypes=True))
            made(v.iota(colid[:, :], [[1, NC]], base=0, channel_multiplier=0, allow_small_or_imprecise_dtypes=True))
            made(v.iota(rank[:, :], [[-1, E]], base=E, channel_multiplier=0, allow_small_or_imprecise_dtypes=True))
            made(v.iota(estep[:, :], [[ST, E]], base=0, channel_multiplier=0, allow_small_or_imprecise_dtypes=True))
            made(v.iota(tokid[:, :], [[P, NT]], base=1, channel_multiplier=1, allow_small_or_imprecise_dtypes=True))
            made(v.iota(spare[:, :, :], [[0, E], [P, ST]], base=T + 1, channel_multiplier=1,
                        allow_small_or_imprecise_dtypes=True), True)
            made(v.memset(carry[:, :, 0:1], 0.0))
            made(v.affine_select(out=ident[:, :], in_=ones[:, :], compare_op=ALU.is_equal, fill=0.0, base=0,
                                 pattern=[[-1, P]], channel_multiplier=1))
            made(v.affine_select(out=earlier[:, :], in_=onesb[:, :], compare_op=ALU.is_ge, fill=0.0, base=-1,
                                 pattern=[[1, P]], channel_multiplier=-1))
            made(v.affine_select(out=headmask[:, :, :], in_=headmask[:, :, :], compare_op=ALU.is_ge, fill=0.0,
                                 base=0, pattern=[[-DH, HB], [0, DH]], channel_multiplier=1), True)
            made(v.affine_select(out=headmask[:, :, :], in_=headmask[:, :, :], compare_op=ALU.is_ge, fill=0.0,
                                 base=DH - 1, pattern=[[DH, HB], [0, DH]], channel_multiplier=-1))
            assert n_const[0] == NCONST

            def low_piece(w, j, wset, stage):
                hi, lo, src = piece(j, wset, stage)
                pool.wait_ge(w_hi, w * PIECES + (j + 1))
                v.tensor_tensor(lo, src, hi.bitcast(F32), ALU.subtract).then_inc(w_lo, 1)

            def x_rstd(b, q):
                pool.wait_ge(a_var, b * GB + (q + 1))
                v.tensor_tensor(rstd[:, :], veA[:, :], mhalf[:, :], ALU.pow).then_inc(a_rstd, 1)

            def x_part(b, q):
                pool.wait_ge(xhi_ok, OPEN + b * GB + (q + 1))
                v.tensor_tensor(xx[:, :, 1, :], xn[:, :, :], xx[:, :, 0, :].bitcast(F32),
                                ALU.subtract).then_inc(xlo_ok, 1)

            def o_rstd(b, q):
                pool.wait_ge(b_var, b * GB + (q + 1))
                v.tensor_tensor(rstdB[:, :], veB[:, :], mhalf[:, :], ALU.pow).then_inc(b_rstd, 1)

            def o_add(b, q):
                pool.wait_ge(lno_ok, OPEN + b * GB + (q + 1))
                pool.wait_ge(xres_in[q % 2], b * (16 * (GB // 2)) + 16 * (q // 2 + 1))
                v.tensor_tensor(x2[:, q % 2, :, :], ln_o[:, :, :], x2[:, q % 2, :, :], ALU.add).then_inc(x2_ok, 1)

            def u_rstd(b, q):
                pool.wait_ge(b_var2, b * GB + (q + 1))
                v.tensor_tensor(rstd2[:, :], ve2[:, :], mhalf[:, :], ALU.pow).then_inc(b_rstd2, 1)

            steps = {"x_stats": x_rstd, "x_low0": x_part, "o_stats": o_rstd, "o_add": o_add, "u_stats": u_rstd}

            for place in range(PLACES):
                attend(steps, place, 0)
                if place in shared_at:
                    low_piece(0, shared_at[place], 0, stage_first)
            with pool.Fori(1, B) as b:
                for place in range(PLACES):
                    attend(steps, place, b)
            for j in range(PIECES):
                low_piece(1, j, 1, stage_later)

            def gather(e, part):
                n = e * 2 + (NG + part)
                if not (isinstance(e, int) and e == 0):
                    pool.wait_ge(gathered[part], e * (16 * HALF))
                pool.sem_inc(pool_go, 1)
                v.tensor_copy(gcur[:, part, :], gidx[:, bass.ds(e * ST + part * HALF, HALF)]).then_inc(g_cur, 1)
                pool.wait_ge(g_cur, e * 2 + (part + 1))
                pool.wait_ge(ht_ps, OPEN + n * 2 - 2)
                pool.sem_inc(pool_go, 1)
                for t in range(HALF):
                    w = LASTW if part * HALF + t == ST - 1 else P
                    pool.indirect_dma_start(rows[0:w, part, t, :], None, u_d,
                                            bass.IndirectOffsetOnAxis(ap=gcur[0:w, part, t:t + 1], axis=0)
                                            ).then_inc(gathered[part], 16)

            def release(e, part):
                if not (isinstance(e, int) and e == 0):
                    pool.wait_ge(added[part], e * (16 * HALF))
                pool.sem_inc(ysb_free[part], 1)

            def scatter(e, part):
                n = e * 2 + (NG + part)
                v.tensor_copy(scur[:, part, :], sidx[:, bass.ds(e * ST + part * HALF, HALF)]).then_inc(s_cur, 1)
                pool.wait_ge(s_cur, e * 2 + (part + 1))
                pool.wait_ge(y_sb, OPEN + n + 1)
                for s in range(2):
                    pool.wait_ge(y_out[s], OPEN + 16 * (NG // 2))
                    if not (isinstance(e, int) and e == 0):
                        pool.wait_ge(added[s], e * (16 * HALF))
                pool.wait_ge(spare_out, 16 * ST)
                pool.sem_inc(pool_go, 1)
                for t in range(HALF):
                    w = LASTW if part * HALF + t == ST - 1 else P
                    pool.indirect_dma_start(y_d, bass.IndirectOffsetOnAxis(ap=scur[0:w, part, t:t + 1], axis=0),
                                            ysb[0:w, part, t, :], None, compute_op=ALU.add
                                            ).then_inc(added[part], 16)

            pool.wait_ge(r_idx, 1)
            gather(0, 0)
            gather(0, 1)
            release(0, 0)
            release(0, 1)
            gather(1, 0)
            gather(1, 1)
            for j in range(PIECES):
                if j == 2:
                    scatter(0, 0)
                low_piece(2, j, 0, stage_later)

            def during(e, other):
                release(e, 0)
                gather(e + 1, 0)
                scatter(e - 1, 1)
                gather(e + 1, 1)
                release(e, 1)
                for j in range(PIECES):
                    if j == 2:
                        scatter(e, 0)
                    low_piece(e + 2, j, other, stage_later)

            during(1, 1)
            with pool.Fori(1, (E - 1) // 2) as i:
                for s in range(2):
                    during(i * 2 + s, s)
            release(E - 1, 0)
            scatter(E - 2, 1)
            release(E - 1, 1)
            scatter(E - 1, 0)
            scatter(E - 1, 1)
            with pool.Fori(0, NG // TR) as i:
                for k in range(TR):
                    pool.wait_ge(t_var, i * TR + (k + 1))
                    v.tensor_tensor(t_scale[k % 2], veA[:, :], mhalf[:, :], ALU.pow).then_inc(t_rstd, 1)
                    if k > 0:
                        last_add(v, pool, i, k - 1, pool_go, slice(GT // 2, GT), t_okp)
                last_add(v, pool, i, TR - 1, pool_go, slice(GT // 2, GT), t_okp)

        @block.scalar
        def _(act_e):
            s = nc.scalar

            def x_high(b, q):
                act_e.wait_ge(xn_ok, OPEN + b * GB + (q + 1))
                act_e.wait_ge(g_done, OPEN + b * GB + q)
                s.activation(xx[:, :, 0, :], xn[:, :, :], ACT.Copy).then_inc(xhi_ok, 1)

            def x_keep(k):
                def step(b, q):
                    act_e.wait_ge(xt_ps, OPEN + b * (2 * GB) + (2 * q + k + 1))
                    if q == 0 and k == 0:
                        act_e.wait_ge(o_ok, OPEN + b * GB)
                    s.activation(xT_hi[:, k, q * GW:(q + 1) * GW], bank[6][:, :], ACT.Copy).then_inc(xthi_ok, 1)
                return step

            def m_step(dst, src, ready, count, func=ACT.Copy):
                def step(b, q):
                    act_e.wait_ge(ready, b * (MP if ready is m_pe else MD) + count)
                    s.activation(dst, src, func).then_inc(m_act, 1)
                return step

            def m_gram(b, q):
                act_e.wait_ge(g_done, OPEN + b * GB + GB)
                act_e.wait_ge(x2_ok, OPEN + b * GB)
                for k in range(KC):
                    ins = s.activation(gs[:, k, :], bank[4 + k][:, :], ACT.Copy)
                ins.then_inc(m_act, 1)

            def keep_s(b, q):
                act_e.wait_ge(lg_ps, OPEN + b * GB)
                m_step(hr[:, 0, 0:KC * P], bank[6][:, 0:KC * P], m_pe, 3)(b, q)

            def o_norm(b, q):
                act_e.wait_ge(b_nb, b * GB + (q + 1))
                act_e.wait_ge(x2_ok, OPEN + b * GB + q)
                for t in range(GT):
                    ins = s.activation(ln_o[:, t, :], bank[o_bank(b, q) + t // 2][:, (t % 2) * D:(t % 2 + 1) * D],
                                       ACT.Identity, scale=rstdB[:, t:t + 1], bias=nbiasB[:, t:t + 1])
                ins.then_inc(lno_ok, 1)

            def u_keep(k):
                def step(b, q):
                    act_e.wait_ge(ut_ps, OPEN + b * (2 * GB) + (2 * q + k + 1))
                    act_e.wait_ge(lg_ps, OPEN + b * GB + q)
                    s.activation(hr[:, k, :], bank[6][:, :], ACT.Identity,
                                 scale=gcol[:, k:k + 1], bias=bcol[:, k:k + 1]).then_inc(hT_ok, 1)
                return step

            tflat = flat4(tsb)
            steps = {"x_turn0": x_high, "x_low0": x_keep(0), "x_gram": x_keep(1), "m_gram": m_gram,
                     "m_keep_t": m_step(tflat, bank[4][:, :], m_pe, 2), "m_keep_s": keep_s,
                     "m_exp": m_step(lc[:, :, :], lc[:, :, :], m_dve, 3, ACT.Exp),
                     "m_keep_n": m_step(tflat, bank[6][:, :], m_pe, 5),
                     "m_high": m_step(m_hi[:, :, :].rearrange("p k d -> p (k d)"), bank[4][:, :], m_pe, 6),
                     "o_norm": o_norm, "u_turn0": u_keep(0), "u_turn1": u_keep(1)}

            def prep(c, k):
                act_e.wait_ge(ht_ps, OPEN + c.n * 2 + (k + 1))
                if not (isinstance(c.n, int) and c.n == 0):
                    act_e.wait_ge(hlo_ok, c.n)
                s.activation(hfull[:, k, 0:c.w], bank[7][:, 0:c.w], ACT.Identity,
                             scale=gcol[:, k:k + 1], bias=bcol[:, k:k + 1]).then_inc(hf_ok, 1)
                if k == KC - 1:
                    act_e.wait_ge(hf_ok, c.n * 2 + 2)
                    if not (isinstance(c.n, int) and c.n == 0):
                        act_e.wait_ge(b_ps, OPEN + (c.n - 1) * FM)
                    s.activation(h_hi[:, c.slot, :, 0:c.w], hfull[:, :, 0:c.w], ACT.Copy).then_inc(hhi_ok, 1)

            def high_piece(w, j, wset, stage):
                if j == 0:
                    if isinstance(w, int) and w == 1:
                        act_e.wait_ge(o_ok, OPEN + NG)
                        act_e.wait_ge(g_done, OPEN + NG)
                    elif not (isinstance(w, int) and w == 0):
                        act_e.wait_ge(dn_done, OPEN + w * (2 * FM) + FM * (NG - 4))
                hi, lo, src = piece(j, wset, stage)
                act_e.wait_ge(stage_in[j % 3], w * 32 + 16 * (j // 3 + 1))
                s.activation(hi, src, ACT.Copy).then_inc(w_hi, 1)

            def high(c, m):
                act_e.wait_ge(act_ok, OPEN + c.n * FM + (m + 1))
                act_e.wait_ge(dn_done, OPEN + c.n * FM + (m - 3))
                s.activation(act_hi[:, m % 4, 0:c.w], act[:, m % 2, 0:c.w], ACT.Copy).then_inc(ahi_ok, 1)

            def take_y(c):
                act_e.wait_ge(dn_done, OPEN + c.n * FM + FM)
                if c.expert is None:
                    act_e.wait_ge(y_out[c.slot], OPEN + c.landed - 16)
                    for h in range(2):
                        ins = s.activation(flat4(ysb[:, c.slot, 2 * h:2 * h + 2, :]), bank[2 + h][:, :], ACT.Copy)
                else:
                    act_e.wait_ge(y_out[c.slot], OPEN + 16 * (NG // 2))
                    act_e.wait_ge(ysb_free[c.slot], c.expert + 1)
                    for t, w in enumerate(c.widths):
                        col = c.expert * ST + (c.slot * HALF + t + NC)
                        ins = s.activation(ysb[0:w, c.slot, t, :], bank[2 + t // 2][0:w, (t % 2) * D:(t % 2 + 1) * D],
                                           ACT.Copy, scale=table2[0:w, bass.ds(col, 1)])
                ins.then_inc(y_sb, 1)

            def body(prev, c, nxt, between=lambda place: None):
                for m in range(FM):
                    if m == 2 and prev is not None:
                        take_y(prev)
                    act_e.wait_ge(a_ps, c.n * FM + (m + 1))
                    act_e.wait_ge(alo_ok, OPEN + c.n * FM + (m - 1))
                    a = bank[4 if c.wide and m % 2 else 0]
                    s.activation(act[:, m % 2, 0:c.w], a[:, 0:c.w], ACT.Silu).then_inc(silu_ok, 1)
                    between(2 * m)
                    if m > 0:
                        high(c, m - 1)
                    elif prev is not None:
                        high(prev, FM - 1)
                    if m in (4, 5) and nxt is not None:
                        prep(nxt, m - 4)
                    between(2 * m + 1)

            act_e.wait_ge(wvT_ps, 1)
            s.activation(wvT[:, :, :].rearrange("p k d -> p (k d)"), bank[6][:, :], ACT.Copy).then_inc(wvT_ok, 1)
            act_e.wait_ge(const_in, 16 * NSMALL)
            for place in range(PLACES):
                attend(steps, place, 0)
                if place in shared_at:
                    high_piece(0, shared_at[place], 0, stage_first)
            for k in range(KC):
                prep(shared_chunk(0, 0), k)
            with act_e.Fori(1, B) as b:
                cs = [shared_chunk(b - 1, j) for j in range(GB)] + [shared_chunk(b, 0)]
                for j in range(GB):
                    body(cs[j - 1] if j else None, cs[j], cs[j + 1],
                         lambda place: attend(steps, 2 * FM * j + place, b))
                high(cs[GB - 1], FM - 1)
                take_y(cs[GB - 1])

            def route(place):
                if place == 8:
                    act_e.wait_ge(r_d, 1)
                    s.activation(rsmall[:, 1, 0:NT], rsmall[:, 0, 0:NT], ACT.Exp).then_inc(r_ex, 1)
                elif 2 * FM < place < 4 * FM and place % 2:
                    if (place - 2 * FM) // 2 < PIECES:
                        high_piece(1, (place - 2 * FM) // 2, 1, stage_later)

            cs = last_chunks()
            for j in range(GB):
                body(cs[j - 1] if j else None, cs[j], cs[j + 1], lambda place: route(2 * FM * j + place))
            def body_and_weights(prev, c, nxt):
                def weights(place):
                    if place in WEIGHTS_AT and c.slot == 1 and nxt is not None:
                        high_piece(c.expert + 2, WEIGHTS_AT.index(place), 1 - c.wset, stage_later)
                body(prev, c, nxt, weights)
            routed_chunks(act_e, body_and_weights)
            last = expert_chunk(E - 1, 1, 1)
            high(last, FM - 1)
            take_y(last)
            with act_e.Fori(0, NG // TR) as i:
                for k in range(TR):
                    act_e.wait_ge(t_nb, i * TR + (k + 1))
                    y = last_y[k % TY]
                    for t in range(GT):
                        ins = s.activation(y[:, t, :], y[:, t, :], ACT.Identity,
                                           scale=t_scale[k % 2][:, t:t + 1], bias=nbias[:, t:t + 1])
                    ins.then_inc(t_act, 1)

        @block.tensor
        def _(pe):
            t_ = nc.tensor

            def three(o, a_hi, a_lo, b_hi, b_lo, start, stop):
                t_.matmul(o, a_lo, b_hi, start=start, stop=False, skip_group_check=True)
                t_.matmul(o, a_hi, b_lo, start=False, stop=False, skip_group_check=True)
                return t_.matmul(o, a_hi, b_hi, start=False, stop=stop, skip_group_check=True)

            def x_turn(k):
                def step(b, q):
                    if k == 0:
                        pe.wait_ge(xn_ok, OPEN + b * GB + (q + 1))
                    pe.wait_ge(xtlo_ok, OPEN + b * (2 * GB) + (2 * q + k))
                    if q == 0 and k == 0:
                        pe.wait_ge(lg_ok, OPEN + b * GB)
                    for t in range(GT):
                        ins = t_.transpose(bank[6][:, t * P:(t + 1) * P], xn[:, t, k * P:(k + 1) * P], ident[:, :])
                    ins.then_inc(xt_ps, 1)
                return step

            def x_gram(b, q):
                pe.wait_ge(xlo_ok, OPEN + b * GB + (q + 1))
                if q == 0:
                    pe.wait_ge(lno_ok, OPEN + b * GB)
                for t in range(GT):
                    for k in range(KC):
                        ins = t_.matmul(bank[4 + k][:, :], xx[:, t, 0, k * P:(k + 1) * P],
                                        xx[:, t, :, :].rearrange("p h d -> p (h d)"),
                                        start=(q == 0 and t == 0), stop=(q == GB - 1 and t == GT - 1))
                ins.then_inc(g_done, 1)

            def m_turn(b, q):
                pe.wait_ge(m_act, OPEN + b * MA + 1)
                pe.wait_ge(xtlo_ok, OPEN + b * (2 * GB) + 2 * GB)
                for k in range(KC):
                    for c in range(KC):
                        ins = t_.transpose(bank[6][:, k * D + c * P:k * D + (c + 1) * P],
                                           gs[:, c, D + k * P:D + (k + 1) * P], ident[:, :])
                ins.then_inc(m_pe, 1)

            def m_times_wqk(b, q):
                pe.wait_ge(m_dve, b * MD + 1)
                for c in range(KC):
                    for k in range(KC):
                        ins = t_.matmul(bank[4][:, c * D:(c + 1) * D], gf[:, k, c * P:(c + 1) * P], wqk[:, k, :],
                                        start=(k == 0), stop=(k == KC - 1))
                ins.then_inc(m_pe, 1)

            def m_dots(b, q):
                pe.wait_ge(m_act, OPEN + b * MA + 2)
                for c in range(KC):
                    for k in range(KC):
                        ins = t_.matmul(bank[6][:, c * P:(c + 1) * P], wqk[:, k, c * P:(c + 1) * P],
                                        tsb[:, k, c * P:(c + 1) * P], start=(k == 0), stop=(k == KC - 1))
                ins.then_inc(m_pe, 1)

            def m_rowdiag(b, q):
                pe.wait_ge(m_dve, b * MD + 2)
                t_.matmul(bank[5][:, 0:KC * P], ones[:, :], hr[:, 0, KC * P:2 * KC * P],
                          start=True, stop=True).then_inc(m_pe, 1)

            def m_times_wo(b, q):
                pe.wait_ge(m_dve, b * MD + 4)
                for c in range(KC):
                    ins = t_.matmul(bank[6][:, c * D:(c + 1) * D], sD[:, c, :], wo[:, c, :], start=True, stop=True)
                ins.then_inc(m_pe, 1)

            def m_times_wv(b, q):
                pe.wait_ge(m_act, OPEN + b * MA + 5)
                pe.wait_ge(wvT_ok, 1)
                for c in range(KC):
                    for k in range(KC):
                        ins = t_.matmul(bank[4][:, c * D:(c + 1) * D], wvT[:, k, c * P:(c + 1) * P], tsb[:, k, :],
                                        start=(k == 0), stop=(k == KC - 1))
                ins.then_inc(m_pe, 1)

            def o_mix(b, q):
                if q == 0:
                    pe.wait_ge(m_dve, b * MD + MD)
                if not (isinstance(b, int) and b == 0):
                    pe.wait_ge(lno_ok, OPEN + b * GB + q)
                elif q > 1:
                    pe.wait_ge(lno_ok, OPEN + (q - 1))
                for t in range(GT):
                    o = bank[o_bank(b, q) + t // 2][:, (t % 2) * D:(t % 2 + 1) * D]
                    cols = slice(q * GW + t * P, q * GW + (t + 1) * P)
                    for k in range(KC):
                        ins = three(o, xT_hi[:, k, cols], xT_lo[:, k, cols], m_hi[:, k, :], m_lo[:, k, :],
                                    k == 0, k == KC - 1)
                ins.then_inc(o_ok, 1)

            def u_turn(k):
                def step(b, q):
                    if k == 0:
                        pe.wait_ge(u_ok, OPEN + b * GB + (q + 1))
                        pe.wait_ge(lg_ok, OPEN + b * GB + q)
                    else:
                        pe.wait_ge(hT_ok, OPEN + b * (2 * GB) + (2 * q + 1))
                    for t in range(GT):
                        ins = t_.transpose(bank[6][:, t * P:(t + 1) * P], u[:, t, k * P:(k + 1) * P], ident[:, :])
                    ins.then_inc(ut_ps, 1)
                return step

            def u_route(b, q):
                pe.wait_ge(hT_ok, OPEN + b * (2 * GB) + (2 * q + 2))
                for t in range(GT):
                    for k in range(KC):
                        ins = t_.matmul(bank[6][:, t * 8:t * 8 + E], hr[:, k, t * P:(t + 1) * P], wr[:, k, :],
                                        start=(k == 0), stop=(k == KC - 1))
                ins.then_inc(lg_ps, 1)

            steps = {"x_turn0": x_turn(0), "x_turn1": x_turn(1), "x_gram": x_gram, "m_turn": m_turn,
                     "m_times_wqk": m_times_wqk, "m_dots": m_dots, "m_rowdiag": m_rowdiag,
                     "m_times_wo": m_times_wo, "m_times_wv": m_times_wv, "o_mix": o_mix,
                     "u_turn0": u_turn(0), "u_turn1": u_turn(1), "u_route": u_route}

            def turn(c, k):
                if k == 0:
                    pe.wait_ge((rows_in if c.expert is None else gathered)[c.slot], c.landed)
                if not (isinstance(c.n, int) and c.n == 0 and k == 0):
                    pe.wait_ge(hf_ok, c.n * 2 + k)
                for t, w in enumerate(c.widths):
                    ins = t_.transpose(bank[7][:, t * P:t * P + w], rows[0:w, c.slot, t, k * P:(k + 1) * P],
                                       ident[0:w, 0:w])
                ins.then_inc(ht_ps, 1)

            def up(c, m, opening, first_wide):
                if m == 0:
                    pe.wait_ge(hlo_ok, c.n + 1)
                    if opening is not None:
                        pe.wait_ge(w_lo, opening)
                back = 1 if c.wide and not (first_wide and m == 0) else 0
                for which, freed, full in ((0, silu_ok, a_ps), (1, act_ok, b_ps)):
                    o = bank[(4 if c.wide and m % 2 else 0) + which][:, 0:c.w]
                    pe.wait_ge(freed, OPEN + c.n * FM + (m - back))
                    for k in range(KC):
                        wh = wup_hi[c.wset][:, which, k, m * P:(m + 1) * P]
                        wl = wup_lo[c.wset][:, which, k, m * P:(m + 1) * P]
                        ins = three(o, wh, wl, h_hi[:, c.slot, k, 0:c.w], h_lo[:, c.slot, k, 0:c.w],
                                    k == 0, k == KC - 1)
                    ins.then_inc(full, 1)

            def down(c, m):
                pe.wait_ge(alo_ok, OPEN + c.n * FM + (m + 1))
                if m == 0:
                    pe.wait_ge(y_sb, OPEN + c.n)
                for t, w in enumerate(c.widths):
                    cols = slice(t * P, t * P + w)
                    ins = three(bank[2 + t // 2][0:w, (t % 2) * D:(t % 2 + 1) * D],
                                act_hi[:, m % 4, cols], act_lo[:, m % 4, cols],
                                wdn_hi[c.wset][:, m, :], wdn_lo[c.wset][:, m, :],
                                m == 0 and t % 2 == 0, m == FM - 1)
                ins.then_inc(dn_done, 1)

            def body(prev, c, nxt, between=lambda place: None):
                first_wide = c.wide and prev is not None and not prev.wide
                if c.expert is None:
                    opening = PIECES
                else:
                    opening = c.expert * PIECES + 2 * PIECES if c.slot == 0 else None
                for m in range(FM):
                    up(c, m, opening, first_wide)
                    between(2 * m)
                    if m in (4, 5) and nxt is not None:
                        turn(nxt, m - 4)
                    if m >= 2:
                        down(c, m - 2)
                    elif prev is not None:
                        down(prev, m + FM - 2)
                    between(2 * m + 1)

            pe.wait_ge(const_ok, NCONST)
            pe.wait_ge(const_in, 16 * NSMALL)
            for k in range(KC):
                for c in range(KC):
                    ins = t_.transpose(bank[6][:, k * D + c * P:k * D + (c + 1) * P], tsb[:, c, k * P:(k + 1) * P],
                                       ident[:, :])
            ins.then_inc(wvT_ps, 1)
            pe.wait_ge(wvT_ok, 1)
            for place in range(PLACES):
                attend(steps, place, 0)
            for k in range(KC):
                turn(shared_chunk(0, 0), k)
            with pe.Fori(1, B) as b:
                cs = [shared_chunk(b - 1, j) for j in range(GB)] + [shared_chunk(b, 0)]
                for j in range(GB):
                    body(cs[j - 1] if j else None, cs[j], cs[j + 1],
                         lambda place: attend(steps, 2 * FM * j + place, b))
                for m in (FM - 2, FM - 1):
                    down(cs[GB - 1], m)

            def count(c, which, to):
                pe.wait_ge(r_oh, c + 1)
                t_.matmul(bank[to][:, 0:E * NT], (earlier, onesb)[which][:, :],
                          oh[:, c, :, :].rearrange("p e t -> p (e t)"), start=True, stop=True).then_inc(r_cnt, 1)

            def route(place):
                if place == 4:
                    count(0, 1, 4)
                    count(0, 0, 5)
                elif place == 7:
                    count(1, 0, 6)
                elif place == 10:
                    pe.wait_ge(r_scan, 1)
                    count(1, 1, 4)
                elif place == 15:
                    pe.wait_ge(r_scan, 3)
                elif NR < place <= NR + NBLK:
                    n = place - NR - 1
                    pe.wait_ge(r_sel, n + 1)
                    for t in range(RB):
                        ins = t_.matmul(bank[6][:, 0:2 * NC], selA[:, n % 2, t, :],
                                        selB[:, n % 2, t, :, :].rearrange("p a c -> p (a c)"),
                                        start=(n == 0 and t == 0), stop=(n == NBLK - 1 and t == RB - 1))
                    ins.then_inc(r_mm, 1)

            cs = last_chunks()
            for j in range(GB):
                body(cs[j - 1] if j else None, cs[j], cs[j + 1], lambda place: route(2 * FM * j + place))
            routed_chunks(pe, body)
            last = expert_chunk(E - 1, 1, 1)
            down(last, FM - 2)
            down(last, FM - 1)

        @block.vector
        def _(dve):
            v = nc.vector
            SQ = float(np.sqrt(np.float32(N)))

            def stats(ch, src, st_, mv_):
                for t in range(GT):
                    ins = v.bn_stats(st_[:, t, :], src(t))
                ch.link(ins)
                dve.sem_inc(dve_go, 1)
                for t in range(GT):
                    ins = v.bn_aggr(mv_[:, t, :], st_[:, t, :])
                ch.link(ins)

            def x_stats(b, q):
                dve.wait_ge(x_in_s[q % 2], b * (8 * GB) + 16 * (q // 2 + 1))
                ch = Chain(dve, a_chain, (b * GB + q) * 2)
                stats(ch, lambda t: xin[:, q % 2, t, :], st, mv)
                v.tensor_scalar(veA[:, :], mv[:, :, 1], EPS, None, ALU.add).then_inc(a_var, 1)

            def x_norm(b, q):
                g = b * GB + q
                dve.wait_ge(a_rstd, g + 1)
                dve.wait_ge(xhi_ok, OPEN + g)
                dve.wait_ge(xlo_ok, OPEN + g)
                dve.wait_ge(xt_ps, OPEN + g * 2)
                for t in range(GT):
                    ins = v.tensor_scalar(xn[:, t, :], xin[:, q % 2, t, :], mv[:, t, 0:1], rstd[:, t:t + 1],
                                          ALU.subtract, ALU.mult)
                ins.then_inc(xn_ok, 1)

            def x_low(k):
                def step(b, q):
                    dve.wait_ge(xthi_ok, b * (2 * GB) + (2 * q + k + 1))
                    v.tensor_tensor(xT_lo[:, k, q * GW:(q + 1) * GW], bank[6][:, :],
                                    xT_hi[:, k, q * GW:(q + 1) * GW].bitcast(F32), ALU.subtract).then_inc(xtlo_ok, 1)
                return step

            M_AT = {"turn": 0, "logits": 1, "softmax": 6}
            M_STEPS = 9
            gflat = flat4(gf)

            def m_sum(b, q):
                dve.wait_ge(m_act, OPEN + b * MA + 1)
                dve.wait_ge(u_out, OPEN + b * (16 * GB))
                dve.wait_ge(ut_ps, OPEN + b * (2 * GB))
                ch = Chain(dve, m_chain, b * M_STEPS + M_AT["turn"])
                ch.step(v.tensor_tensor(gf, gs[:, :, 0:D], gs[:, :, D:2 * D], ALU.add))

            def m_sym(b, q):
                dve.wait_ge(m_chain, b * M_STEPS + 1)
                dve.wait_ge(m_pe, b * MP + 1)
                v.tensor_tensor(gflat, gflat, bank[6][:, :], ALU.add).then_inc(m_dve, 1)

            def m_diag(b, q):
                dve.wait_ge(m_act, OPEN + b * MA + 3)
                v.tensor_tensor(sD, sS, ident[:, :].rearrange("p (a j) -> p a j", a=1).broadcast_to([P, KC, P]),
                                ALU.mult).then_inc(m_dve, 1)
                dve.wait_ge(m_dve, b * MD + 2)
                v.tensor_reduce(small[:, 0, :], sD, AX.X, ALU.add)

            def m_logits(b, q):
                ch = Chain(dve, m_chain, b * M_STEPS + M_AT["logits"])
                dve.wait_ge(m_pe, b * MP + 4)
                ch.link(v.scalar_tensor_tensor(out=hr[:, 0, 0:KC * P], in0=hr[:, 0, 0:KC * P], scalar=2.0,
                                               in1=bank[5][:, 0:KC * P], op0=ALU.mult, op1=ALU.subtract))
                hm = headmask[:, :, :].rearrange("p h e -> p (h e)").rearrange("p (a j) -> p a j", a=1)
                ch.link(v.tensor_tensor(sS, sS, hm.broadcast_to([P, KC, P]), ALU.mult))
                ch.link(v.tensor_reduce(lc[:, :, :], sS.rearrange("p k (h e) -> p k e h", e=DH), AX.X, ALU.add))
                for k in range(KC):
                    ins = v.tensor_scalar(lc[:, k, :], lc[:, k, :], small[:, 0, k:k + 1], taus[:, k:k + 1],
                                          ALU.subtract, ALU.mult)
                ch.link(ins)
                ch.link(v.tensor_reduce(small[:, 1, :], lc[:, :, :], AX.X, ALU.max))
                for k in range(KC):
                    ins = v.tensor_scalar(lc[:, k, :], lc[:, k, :], small[:, 1, k:k + 1], None, ALU.subtract)
                ins.then_inc(m_dve, 1)

            def m_softmax(b, q):
                ch = Chain(dve, m_chain, b * M_STEPS + M_AT["softmax"])
                dve.wait_ge(m_act, OPEN + b * MA + 4)
                ch.link(v.tensor_reduce(small[:, 2, :], lc[:, :, :], AX.X, ALU.add))
                ch.link(v.reciprocal(small[:, 3, :], small[:, 2, :]))
                for k in range(KC):
                    ins = v.tensor_scalar(lc[:, k, :], lc[:, k, :], small[:, 3, k:k + 1], None, ALU.mult)
                ch.link(ins)
                for k in range(KC):
                    own = lc[:, k, :].rearrange("p (a e) -> p a e", a=1).broadcast_to([P, HB, DH])
                    ins = v.tensor_tensor(sD[:, k, :].rearrange("p (h e) -> p h e", e=DH), headmask[:, :, :],
                                          own, ALU.mult)
                ins.then_inc(m_dve, 1)

            def m_low(b, q):
                flat = lambda t: t.rearrange("p k d -> p (k d)")
                dve.wait_ge(m_act, OPEN + b * MA + 6)
                v.tensor_tensor(flat(m_lo[:, :, :]), bank[4][:, :], flat(m_hi[:, :, :]).bitcast(F32),
                                ALU.subtract).then_inc(m_dve, 1)

            def o_stats(b, q):
                ch = Chain(dve, b_chain, (b * GB + q) * 2)
                dve.wait_ge(o_ok, OPEN + b * GB + (q + 1))
                stats(ch, lambda t: bank[o_bank(b, q) + t // 2][:, (t % 2) * D:(t % 2 + 1) * D], stB, mvB)
                v.tensor_scalar(veB[:, :], mvB[:, :, 1], EPS, None, ALU.add).then_inc(b_var, 1)

            def o_norm(b, q):
                dve.wait_ge(b_rstd, b * GB + (q + 1))
                v.scalar_tensor_tensor(out=nbiasB[:, :], in0=mvB[:, :, 0], scalar=-1.0, in1=rstdB[:, :],
                                       op0=ALU.mult, op1=ALU.mult).then_inc(b_nb, 1)

            def u_stats(b, q):
                ch = Chain(dve, u_chain, (b * GB + q) * 2)
                dve.wait_ge(x2_ok, OPEN + b * GB + (q + 1))
                stats(ch, lambda t: x2[:, q % 2, t, :], st2, mv2)
                v.tensor_scalar(ve2[:, :], mv2[:, :, 1], 1.0 + EPS, EPS * EPS, ALU.mult, ALU.add).then_inc(b_var2, 1)

            def u_norm(b, q):
                g = b * GB + q
                dve.wait_ge(b_rstd2, g + 1)
                dve.wait_ge(u_out, OPEN + g * 16)
                dve.wait_ge(ut_ps, OPEN + g * 2)
                for t in range(GT):
                    ins = v.tensor_scalar(u[:, t, :], x2[:, q % 2, t, :], mv2[:, t, 0:1], rstd2[:, t:t + 1],
                                          ALU.subtract, ALU.mult)
                ins.then_inc(u_ok, 1)

            def u_route(b, q):
                g = b * GB + q
                dve.wait_ge(lg_ps, OPEN + g + 1)
                v.tensor_copy(lg[:, :, bass.ds(g * GT, GT)],
                              bank[6][:, 0:GT * 8].rearrange("p (t e) -> p e t", e=8)[:, 0:E, :]).then_inc(lg_ok, 1)

            steps = {"x_stats": x_stats, "x_norm": x_norm, "x_low0": x_low(0), "x_gram": x_low(1),
                     "m_turn": m_sum, "m_sym": m_sym, "m_diag": m_diag, "m_logits": m_logits,
                     "m_softmax": m_softmax, "m_low": m_low, "o_stats": o_stats, "o_norm": o_norm,
                     "u_stats": u_stats, "u_norm": u_norm, "u_route": u_route}

            def prep(c):
                dve.wait_ge(hhi_ok, c.n + 1)
                if not (isinstance(c.n, int) and c.n == 0):
                    dve.wait_ge(b_ps, OPEN + (c.n - 1) * FM)
                v.tensor_tensor(h_lo[:, c.slot, :, 0:c.w], hfull[:, :, 0:c.w],
                                h_hi[:, c.slot, :, 0:c.w].bitcast(F32), ALU.subtract).then_inc(hlo_ok, 1)

            def low(c, m):
                dve.wait_ge(ahi_ok, c.n * FM + (m + 1))
                dve.wait_ge(dn_done, OPEN + c.n * FM + (m - 3))
                v.tensor_tensor(act_lo[:, m % 4, 0:c.w], act[:, m % 2, 0:c.w],
                                act_hi[:, m % 4, 0:c.w].bitcast(F32), ALU.subtract).then_inc(alo_ok, 1)

            def body(prev, c, nxt, between=lambda place: None):
                for m in range(FM):
                    dve.wait_ge(silu_ok, OPEN + c.n * FM + (m + 1))
                    dve.wait_ge(b_ps, OPEN + c.n * FM + (m + 1))
                    v.tensor_tensor(act[:, m % 2, 0:c.w], bank[(4 if c.wide and m % 2 else 0) + 1][:, 0:c.w],
                                    act[:, m % 2, 0:c.w], ALU.mult).then_inc(act_ok, 1)
                    between(2 * m)
                    if m > 0:
                        low(c, m - 1)
                    elif prev is not None:
                        low(prev, FM - 1)
                    if m == 6 and nxt is not None:
                        prep(nxt)
                    between(2 * m + 1)

            dve.wait_ge(const_in, 16 * NSMALL)
            v.tensor_scalar(taus[:, :], taus[:, :], 1.0 / SQ, None, ALU.mult).then_inc(tau_ok, 1)
            dve.wait_ge(tau_ok, 1)
            dve.wait_ge(const_ok, NCONST)
            for place in range(PLACES):
                attend(steps, place, 0)
            prep(shared_chunk(0, 0))
            with dve.Fori(1, B) as b:
                cs = [shared_chunk(b - 1, j) for j in range(GB)] + [shared_chunk(b, 0)]
                for j in range(GB):
                    body(cs[j - 1] if j else None, cs[j], cs[j + 1],
                         lambda place: attend(steps, 2 * FM * j + place, b))
                low(cs[GB - 1], FM - 1)

            ch = Chain(dve, r_chain, 0)
            over_e = lambda a: a.rearrange("p (a t) -> p a t", a=1).broadcast_to([P, E, NT])
            over_t = lambda a: a.rearrange("p (e a) -> p e a", a=1).broadcast_to([P, E, NT])
            by_t = lambda a: a.rearrange("p e t -> p t e")
            flat = lambda a: a.rearrange("p e t -> p (e t)")
            best = rsmall[:, 3, :].rearrange("p (c t) -> p c t", c=2)
            pos = rsmall[:, 0, :].rearrange("p (c t) -> p c t", c=2)
            first = rsmall[:, 2, :].rearrange("p (c t) -> p c t", c=2)

            def pick_best(c):
                if c == 0:
                    dve.wait_ge(lg_ok, OPEN + NG)
                    dve.wait_ge(u_out, OPEN + 16 * NG)
                ch.link(v.tensor_reduce(best[:, c, :], by_t(lg[:, :, :]), AX.X, ALU.max))
                ch.link(v.tensor_tensor(rt, lg[:, :, :], over_e(best[:, c, :]), ALU.is_equal))

            def pick_first(c):
                ch.link(v.tensor_tensor(rt, rt, over_t(rank[:, :]), ALU.mult))
                ch.link(v.tensor_reduce(rsmall[:, 2, 0:NT], by_t(rt), AX.X, ALU.max))

            def mark(c):
                v.tensor_tensor(oh[:, c, :, :], rt, over_e(rsmall[:, 2, 0:NT]), ALU.is_equal).then_inc(r_oh, 1)
                dve.wait_ge(r_oh, c + 1)
                if c == 0:
                    ch.link(v.scalar_tensor_tensor(out=lg[:, :, :], in0=oh[:, 0, :, :], scalar=-BIG,
                                                   in1=lg[:, :, :], op0=ALU.mult, op1=ALU.add))
                else:
                    v.tensor_tensor(rsmall[:, 0, 0:NT], best[:, 1, :], best[:, 0, :], ALU.subtract).then_inc(r_d, 1)

            def gates_of(c):
                dve.wait_ge(r_ex, 1)
                ch.link(v.tensor_scalar(rsmall[:, 0, 0:NT], rsmall[:, 1, 0:NT], 1.0, None, ALU.add))
                ch.link(v.reciprocal(gates[:, 0, :], rsmall[:, 0, 0:NT]))
                ch.link(v.tensor_tensor(gates[:, 1, :], gates[:, 0, :], rsmall[:, 1, 0:NT], ALU.mult))

            def scan(c):
                dve.wait_ge(r_cnt, (2, 4)[c])
                ch.link(v.tensor_tensor_scan(rincl, flat(carry[:, :, :]), bank[4][:, 0:E * NT], 0.0,
                                             ALU.mult, ALU.add))
                v.tensor_tensor(flat(rt), rincl, bank[4][:, 0:E * NT], ALU.subtract).then_inc(r_scan, 1)
                dve.wait_ge(r_scan, c + 1)

            def within(c):
                if c == 0:
                    ch.link(v.tensor_copy(total[:, :], rincl.rearrange("p (e t) -> p e t", e=E)[:, :, NT - 1]))
                    ch.link(v.tensor_tensor(flat(rt), flat(rt), bank[5][:, 0:E * NT], ALU.add))
                else:
                    ch.link(v.tensor_tensor(rt, rt, over_t(total[:, :]), ALU.add))
                    v.tensor_tensor(flat(rt), flat(rt), bank[6][:, 0:E * NT], ALU.add).then_inc(r_scan, 1)
                    dve.wait_ge(r_scan, 3)

            def queue(c):
                ch.link(v.tensor_tensor(rt, rt, oh[:, c, :, :], ALU.mult))
                ch.link(v.tensor_reduce(pos[:, c, :], by_t(rt), AX.X, ALU.add))

            def column(c):
                ch.link(v.tensor_tensor(rt, over_t(estep[:, :]), oh[:, c, :, :], ALU.mult))
                ch.link(v.tensor_reduce(first[:, c, :], by_t(rt), AX.X, ALU.add))

            def tile_of(_):
                ch.link(v.tensor_scalar(slotcol[:, :, :], pos, float(P), None, ALU.is_ge))
                for j in range(2, ST):
                    ch.link(v.scalar_tensor_tensor(out=slotcol[:, :, :], in0=pos, scalar=float(P * j),
                                                   in1=slotcol[:, :, :], op0=ALU.is_ge, op1=ALU.add))

            def slot_of(_):
                ch.link(v.scalar_tensor_tensor(out=slotm[:, :, :], in0=slotcol[:, :, :], scalar=-float(P), in1=pos,
                                               op0=ALU.mult, op1=ALU.add))
                ch.link(v.tensor_scalar(best, pos, float(CAP), None, ALU.is_lt))
                ch.link(v.scalar_tensor_tensor(out=slotm[:, :, :], in0=slotm[:, :, :], scalar=1.0, in1=best,
                                               op0=ALU.add, op1=ALU.mult))
                ch.link(v.tensor_tensor(slotcol[:, :, :], slotcol[:, :, :], first, ALU.add))

            routing = {0: (pick_best, 0), 1: (pick_first, 0), 2: (mark, 0), 3: (pick_best, 1), 4: (pick_first, 1),
                       5: (mark, 1), 6: (scan, 0), 7: (within, 0), 9: (gates_of, 0), 10: (queue, 0), 11: (column, 0),
                       12: (scan, 1), 13: (within, 1), 14: (queue, 1), 15: (column, 1), 16: (tile_of, 0),
                       17: (slot_of, 0)}

            def select(n):
                c, cut = n % 2, slice(n // 2 * RB, (n // 2 + 1) * RB)
                wide = lambda a, k: a.rearrange("p (t a) -> p t a", a=1).broadcast_to([P, RB, k])
                row = lambda a, k: a.rearrange("p (a m) -> p a m", a=1).broadcast_to([P, RB, k])
                if n >= 2:
                    dve.wait_ge(r_mm, n - 1)
                v.tensor_tensor(selE[:, c, :, :], row(colid[:, :], NC), wide(slotcol[:, c, cut], NC),
                                ALU.is_equal).then_inc(r_selE, 1)
                v.tensor_tensor(selA[:, c, :, :], row(slot1[:, :], P), wide(slotm[:, c, cut], P), ALU.is_equal)
                dve.wait_ge(r_selE, n + 1)
                v.tensor_tensor(selB[:, c, :, 0, :], selE[:, c, :, :], wide(tokid[:, cut], NC), ALU.mult)
                v.tensor_tensor(selB[:, c, :, 1, :], selE[:, c, :, :], wide(gates[:, c, cut], NC),
                                ALU.mult).then_inc(r_sel, 1)

            def indices():
                dve.wait_ge(r_mm, NBLK)
                ch.link(v.tensor_copy(table2[:, :], bank[6][:, 0:2 * NC]))
                v.tensor_scalar(gidx[:, :], table2[:, 0:NC], -1.0, 0.0, ALU.add, ALU.max)
                ch.link(v.tensor_scalar(tabe[:, :], table2[:, 0:NC], 0.0, None, ALU.is_equal))
                ch.link(v.tensor_tensor(tabe[:, :], tabe[:, :], spare[:, :, :].rearrange("p e s -> p (e s)"),
                                        ALU.mult))
                ch.link(v.tensor_tensor(tabe[:, :], tabe[:, :], table2[:, 0:NC], ALU.add))
                v.tensor_scalar(sidx[:, :], tabe[:, :], -1.0, None, ALU.add).then_inc(r_idx, 1)

            def route(place):
                if place in routing:
                    step, c = routing[place]
                    step(c)
                elif NR <= place < NR + NBLK:
                    if place == NR:
                        for s in range(2):
                            dve.wait_ge(x2_out[s], OPEN + 16 * (NG // 2))
                    select(place - NR)
                elif place == R_IDX:
                    indices()

            cs = last_chunks()
            for j in range(GB):
                body(cs[j - 1] if j else None, cs[j], cs[j + 1], lambda place: route(2 * FM * j + place))
            routed_chunks(dve, body)
            low(expert_chunk(E - 1, 1, 1), FM - 1)

            with dve.Fori(0, NG // TR) as i:
                for k in range(TR):
                    ch = Chain(dve, t_chain, i * (2 * TR) + 2 * k)
                    dve.wait_ge(t_y[k % TY], i * (16 * TR // TY) + 16 * (k // TY + 1))
                    stats(ch, lambda t: last_y[k % TY][:, t, :], st, mv)
                    v.tensor_scalar(veA[:, :], mv[:, :, 1], EPS, None, ALU.add).then_inc(t_var, 1)
                    if k > 0:
                        last_add(v, dve, i, k - 1, dve_go, slice(0, GT // 2), t_ok)
                    dve.wait_ge(t_rstd, i * TR + (k + 1))
                    v.scalar_tensor_tensor(out=nbias[:, :], in0=mv[:, :, 0], scalar=-1.0, in1=t_scale[k % 2],
                                           op0=ALU.mult, op1=ALU.mult).then_inc(t_nb, 1)
                last_add(v, dve, i, TR - 1, dve_go, slice(0, GT // 2), t_ok)


_INS = ['L0_attn_x', 'L0_attn_Wqk', 'L0_attn_Wv', 'L0_attn_Wo', 'L0_attn_tau', 'L0_ffn_ln_g', 'L0_ffn_ln_b',
        'L0_ffn_Wr', 'L0_ffn_W1', 'L0_ffn_W3', 'L0_ffn_W2', 'L0_ffn_W1s', 'L0_ffn_W3s', 'L0_ffn_W2s']


def kernel(**inputs):
    import numpy as _np
    import concourse.bacc as _bacc
    from concourse import mybir as _mybir
    from concourse.bass_utils import run_bass_kernel_spmd as _run

    nc = _bacc.Bacc("TRN2", target_bir_lowering=False, num_devices=1)
    arrays, args = {}, []
    for name in _INS:
        a = _np.ascontiguousarray(inputs[name])
        arrays[f"in_{name}_dram"] = a
        args.append(nc.dram_tensor(f"in_{name}_dram", a.shape, _mybir.dt.from_np(a.dtype), kind="ExternalInput").ap())
    shape = arrays["in_L0_attn_x_dram"].shape
    args.append(nc.dram_tensor("out_0_dram", shape, _mybir.dt.float32, kind="ExternalOutput").ap())
    sandwich_kernel(nc, *args)
    r = _run(nc, [arrays], core_ids=[0])
    return r.results[0]["out_0_dram"]
```

```python
from contextlib import ExitStack

import numpy as np

import concourse.bass as bass
from concourse import mybir

ALU = mybir.AluOpType
ACT = mybir.ActivationFunctionType
AX = mybir.AxisListType
F32 = mybir.dt.float32
F32R = mybir.dt.float32r
BF16 = mybir.dt.bfloat16
I32 = mybir.dt.int32
U32 = mybir.dt.uint32

P = 128
EPS = 1e-5
BIG = 3.0e38
OPEN = 4
TOP_K = 2
NOMINAL_TOKENS = 4 * 512


class Chain:

    def __init__(self, eng, sem, base):
        self.eng, self.sem, self.base, self.n = eng, sem, base, 0

    def step(self, ins):
        self.n += 1
        ins.then_inc(self.sem, 1)

    def settle(self):
        self.eng.wait_ge(self.sem, self.base + self.n)

    def link(self, ins):
        self.step(ins)
        self.settle()


def sandwich_kernel(nc, x_in, Wqk, Wv, Wo, tau, ln_g, ln_b, Wr, W1, W3, W2, W1s, W3s, W2s, out):
    B, N, D = x_in.shape
    T = B * N
    H = tau.shape[0]
    DH = D // H
    KC = D // P
    HB = P // DH
    F = W1s.shape[1]
    FM = F // P
    E = Wr.shape[1]
    CAP = -(-int(NOMINAL_TOKENS * TOP_K * 5) // (4 * E))
    GT = 4
    GW = GT * P
    NT = T // P
    NG = T // GW
    GB = N // GW
    ST = -(-CAP // P)
    LASTW = CAP - (ST - 1) * P
    HELD = 2
    FIRST = NG - HELD
    HALF = ST // 2
    NC = E * ST
    assert D == KC * P and ST == 6 and E == 7 and GB == 4 and FM == 8

    x_t = x_in.rearrange("b n d -> (b n) d").rearrange("(g t p) d -> g p t d", p=P, t=GT)
    x2_d = nc.dram_tensor("x2_scratch", (T, D), F32, kind="Internal").ap()
    u_d = nc.dram_tensor("u_scratch", (T, D), F32, kind="Internal").ap()
    y_d = nc.dram_tensor("y_scratch", (T + ST * P, D), F32, kind="Internal").ap()
    x2_t = x2_d.rearrange("(g t p) d -> g p t d", p=P, t=GT)
    u_t = u_d.rearrange("(g t p) d -> g p t d", p=P, t=GT)
    y_t = y_d[0:T, :].rearrange("(g t p) d -> g p t d", p=P, t=GT)
    hT_d = nc.dram_tensor("hT_scratch", (NG, P, KC * GW), F32, kind="Internal").ap()
    near = lambda a: a.rearrange("(g p t) d -> g p t d", p=P, t=GT)
    apart = lambda a: a.rearrange("(g t p) d -> g p t d", p=P, t=GT)
    last_view = lambda a, g: (near if g < FIRST else apart)(a)[g]
    out_d = out.rearrange("b n d -> (b n) d")
    NZERO = HELD * GT + ST
    y_zero = y_d[FIRST * GW:T + ST * P, :].rearrange("(t p) d -> t p d", p=P)

    with ExitStack() as ctx:
        def sb(name, shape, dt=F32):
            return ctx.enter_context(nc.sbuf_tensor("sb_" + name, shape, dt))

        def sem(name):
            return ctx.enter_context(nc.semaphore(name))

        bank = [ctx.enter_context(nc.psum_tensor(f"bank{i}", [P, 512], F32)) for i in range(8)]

        ident = sb("ident", [P, P])
        ones = sb("ones", [P, P])
        zrow = sb("zrow", [P, D])
        onesb = sb("onesb", [P, P], BF16)
        earlier = sb("earlier", [P, P], BF16)
        headmask = sb("headmask", [P, HB, DH])
        slot1 = sb("slot1", [P, P])
        colid = sb("colid", [P, NC])
        rank = sb("rank", [P, E])
        estep = sb("estep", [P, E])
        tokid = sb("tokid", [P, NT])
        spare = sb("spare", [P, E, ST])
        carry = sb("carry", [P, E, NT])
        mhalf = sb("mhalf", [P, GT])
        wqk = sb("wqk", [P, KC, D])
        wvT = sb("wvT", [P, KC, D])
        wo = sb("wo", [P, KC, D])
        wr = sb("wr", [P, KC, E])
        gcol = sb("gcol", [P, KC])
        bcol = sb("bcol", [P, KC])
        taus = sb("taus", [P, KC])
        wup_hi = [sb(f"wup_hi{s}", [P, 2, KC, F], F32R) for s in range(2)]
        wup_lo = [sb(f"wup_lo{s}", [P, 2, KC, F], F32R) for s in range(2)]
        wdn_hi = [sb(f"wdn_hi{s}", [P, FM, D], F32R) for s in range(2)]
        wdn_lo = [sb(f"wdn_lo{s}", [P, FM, D], F32R) for s in range(2)]
        xT_hi = wup_hi[1][:, :, :, :].rearrange("p a k f -> p (a k f)").rearrange("p (k n) -> p k n", k=KC)
        xT_lo = wup_lo[1][:, :, :, :].rearrange("p a k f -> p (a k f)").rearrange("p (k n) -> p k n", k=KC)
        xx = wdn_hi[1][:, :, :].rearrange("p m d -> p (m d)").rearrange("p (t h d) -> p t h d", h=2, d=D)
        xin = sb("xin", [P, 2, GT, D])
        xn = sb("xn", [P, GT, D])
        ln_o = sb("ln_o", [P, GT, D])
        x2 = sb("x2", [P, 2, GT, D])
        u = sb("u", [P, GT, D])
        hr = sb("hr", [P, KC, GW])
        rows = sb("rows", [P, 2, GT, D])
        ysb = sb("ysb", [P, 2, GT, D])
        hfull = sb("hfull", [P, KC, GW])
        h_hi = sb("h_hi", [P, 2, KC, GW], F32R)
        h_lo = sb("h_lo", [P, 2, KC, GW], F32R)
        act = sb("act", [P, 2, GW])
        act_hi = sb("act_hi", [P, 4, GW], F32R)
        act_lo = sb("act_lo", [P, 4, GW], F32R)
        flat4 = lambda a: a.rearrange("p t d -> p (t d)")
        flat_h = lambda a: a[:, :, :].rearrange("p k n -> p (k n)")
        stage_first = [flat4(rows[:, 0, :, :]), flat4(rows[:, 1, :, :]), flat4(ysb[:, 0, :, :])]
        stage_later = [flat4(xin[:, 0, :, :]), flat4(xin[:, 1, :, :]), flat4(xn[:, :, :])]
        TX, TY = 6, 4
        last_x = [x2[:, 0, :, :], x2[:, 1, :, :], ln_o[:, :, :], u[:, :, :], rows[:, 0, :, :], rows[:, 1, :, :]]
        last_y = [xin[:, 0, :, :], xin[:, 1, :, :], xn[:, :, :], hr[:, :, :].rearrange("p k (t d) -> p (k t) d", d=D)]
        st = sb("st", [P, GT, 6])
        mv = sb("mv", [P, GT, 2])
        rstd = sb("rstd", [P, GT])
        nbias = sb("nbias", [P, GT])
        t_scale = [sb(f"t_scale{k}", [P, GT])[:, :] for k in range(2)]
        stB = sb("stB", [P, GT, 6])
        mvB = sb("mvB", [P, GT, 2])
        rstdB = sb("rstdB", [P, GT])
        nbiasB = sb("nbiasB", [P, GT])
        veB = sb("veB", [P, GT])
        st2 = sb("st2", [P, GT, 6])
        mv2 = sb("mv2", [P, GT, 2])
        ve2 = sb("ve2", [P, GT])
        rstd2 = sb("rstd2", [P, GT])
        veA = sb("veA", [P, GT])
        gs = flat4(ln_o[:, :, :]).rearrange("p (k j) -> p k j", k=KC)
        gf, tsb = u[:, 0:KC, :], u[:, KC:2 * KC, :]
        sS = hr[:, 0, 0:KC * P].rearrange("p (k j) -> p k j", k=KC)
        sD = hr[:, 0, KC * P:2 * KC * P].rearrange("p (k j) -> p k j", k=KC)
        lc = sb("lc", [P, KC, DH])
        small = sb("small", [P, 8, KC])
        m_hi = sb("m_hi", [P, KC, D], F32R)
        m_lo = sb("m_lo", [P, KC, D], F32R)
        lg = sb("lg", [P, E, NT])
        oh = sb("oh", [P, 2, E, NT], BF16)
        slotcol = sb("slotcol", [P, 2, NT])
        slotm = sb("slotm", [P, 2, NT])
        gates = sb("gates", [P, 2, NT])
        table2 = sb("table2", [P, 2 * NC])
        tabe = sb("tabe", [P, NC])
        total = sb("total", [P, E])
        gidx = sb("gidx", [P, NC], U32)
        gcur = sb("gcur", [P, 2, HALF], U32)
        scur = sb("scur", [P, 2, HALF], U32)
        sidx = sb("sidx", [P, NC], U32)
        rt = flat4(u[:, :, :])[:, 0:E * NT].rearrange("p (e t) -> p e t", e=E)
        rincl = hr[:, 0, 0:E * NT]
        rsmall = hr[:, 1, :].rearrange("p (a t) -> p a t", t=2 * NT)
        RB = 4
        SR = 4
        selA = x2[:, :, :, :].rearrange("p s t d -> p (s t d)")[:, 0:SR * RB * P].rearrange(
            "p (s t m) -> p s t m", s=SR, t=RB)
        selB = rows[:, :, :, :].rearrange("p s t d -> p (s t d)")[:, 0:SR * RB * 2 * NC].rearrange(
            "p (s t a c) -> p s t a c", s=SR, t=RB, a=2)
        along = lambda a, k: a.rearrange("p (t a) -> p t a", a=1).broadcast_to([P, RB, k])
        across = lambda a, k: a.rearrange("p (a m) -> p a m", a=1).broadcast_to([P, RB, k])
        selE = flat4(ln_o[:, :, :])[:, 0:SR * RB * NC].rearrange("p (s t c) -> p s t c", s=SR, t=RB)

        pool_go = sem("pool_go")
        dve_go = sem("dve_go")
        sp_go = sem("sp_go")
        const_in = sem("const_in")
        const_ok = sem("const_ok")
        tau_ok = sem("tau_ok")
        wvT_ps = sem("wvT_ps")
        wvT_ok = sem("wvT_ok")
        x_in_s = [sem(f"x_in{i}") for i in range(2)]
        a_chain = sem("a_chain")
        a_var = sem("a_var")
        a_rstd = sem("a_rstd")
        xn_ok = sem("xn_ok")
        xhi_ok = sem("xhi_ok")
        xlo_ok = sem("xlo_ok")
        xt_ps = sem("xt_ps")
        xthi_ok = sem("xthi_ok")
        xtlo_ok = sem("xtlo_ok")
        g_done = sem("g_done")
        m_chain = sem("m_chain")
        m_pe = sem("m_pe")
        m_act = sem("m_act")
        m_dve = sem("m_dve")
        o_ok = sem("o_ok")
        b_chain = sem("b_chain")
        u_chain = sem("u_chain")
        b_var = sem("b_var")
        b_rstd = sem("b_rstd")
        b_nb = sem("b_nb")
        lno_ok = sem("lno_ok")
        xres_in = [sem(f"xres_in{i}") for i in range(2)]
        x2_ok = sem("x2_ok")
        x2_out = [sem(f"x2_out{i}") for i in range(2)]
        b_var2 = sem("b_var2")
        b_rstd2 = sem("b_rstd2")
        u_ok = sem("u_ok")
        u_out = sem("u_out")
        ut_ps = sem("ut_ps")
        hT_ok = sem("hT_ok")
        lg_ps = sem("lg_ps")
        lg_ok = sem("lg_ok")
        r_chain = sem("r_chain")
        r_oh = sem("r_oh")
        r_d = sem("r_d")
        r_ex = sem("r_ex")
        r_cnt = sem("r_cnt")
        r_sel = sem("r_sel")
        r_selE = sem("r_selE")
        r_scan = sem("r_scan")
        r_mm = sem("r_mm")
        r_idx = sem("r_idx")
        stage_in = [sem(f"stage_in{i}") for i in range(3)]
        w_hi = sem("w_hi")
        w_lo = sem("w_lo")
        h_out = sem("h_out")
        h_in = sem("h_in")
        gathered = [sem(f"gathered{i}") for i in range(2)]
        added = [sem(f"added{i}") for i in range(2)]
        ysb_free = [sem(f"ysb_free{i}") for i in range(2)]
        ht_ps = sem("ht_ps")
        hf_ok = sem("hf_ok")
        hhi_ok = sem("hhi_ok")
        hlo_ok = sem("hlo_ok")
        a_ps = sem("a_ps")
        b_ps = sem("b_ps")
        silu_ok = sem("silu_ok")
        act_ok = sem("act_ok")
        ahi_ok = sem("ahi_ok")
        alo_ok = sem("alo_ok")
        dn_done = sem("dn_done")
        y_sb = sem("y_sb")
        g_cur = sem("g_cur")
        s_cur = sem("s_cur")
        y_out = [sem(f"y_out{i}") for i in range(2)]
        spare_out = sem("spare_out")
        t_y = [sem(f"t_y{i}") for i in range(TY)]
        t_x = [sem(f"t_x{i}") for i in range(TX)]
        t_chain = sem("t_chain")
        t_nb = sem("t_nb")
        t_act = sem("t_act")
        t_var = sem("t_var")
        t_rstd = sem("t_rstd")
        t_ok = sem("t_ok")
        t_okp = sem("t_okp")
        t_sum = sem("t_sum")
        r_slots = sem("r_slots")
        r_selA = sem("r_selA")
        t_out = [sem(f"t_out{i}") for i in range(TX)]

        NCONST = 17
        NSMALL = 6 + HB
        MA, MP, MD = 6, 6, 5
        PIECES = 6

        class Chunk:
            def __init__(self, n, slot, wset, widths, landed, opening, expert=None, wide=False):
                self.n, self.slot, self.wset, self.widths = n, slot, wset, widths
                self.landed, self.expert, self.w = landed, expert, sum(widths)
                self.wide = wide
                self.opening = opening

        def shared_chunk(b, j, wide=False):
            c = Chunk(b * GB + j, j % 2, 0, [P] * GT, b * (16 * GB) + 16 * (j + 1), PIECES, wide=wide)
            c.stored = b * (8 * GB) + 16 * (j // 2)
            return c

        def expert_chunk(e, part, wset):
            widths = [P] * HALF if part == 0 else [P] * (HALF - 1) + [LASTW]
            c = Chunk(e * 2 + (FIRST + part), part, wset, widths, e * (16 * HALF) + 16 * HALF,
                      e * PIECES + 2 * PIECES, e, True)
            c.x = e * 2 + part
            return c

        def held_chunk(h):
            return Chunk(FIRST + 2 * E + h, h, 0, [P] * GT, 16 * (FIRST + h + 1), (E + 2) * PIECES, wide=True)

        def last_chunks():
            return [shared_chunk(B - 1, j, j > 0) for j in range(GB - HELD)]

        def routed_chunks(eng, body):
            body(None, expert_chunk(0, 0, 1), expert_chunk(0, 1, 1))
            with eng.Fori(0, (E - 1) // 2) as i:
                seq = [expert_chunk(i * 2, 0, 1), expert_chunk(i * 2, 1, 1), expert_chunk(i * 2 + 1, 0, 0),
                       expert_chunk(i * 2 + 1, 1, 0), expert_chunk(i * 2 + 2, 0, 1), expert_chunk(i * 2 + 2, 1, 1)]
                for j in range(1, 5):
                    body(seq[j - 1], seq[j], seq[j + 1])
            body(expert_chunk(E - 1, 0, 1), expert_chunk(E - 1, 1, 1), held_chunk(0))

        def held_chunks(body, between=lambda place: None):
            body(expert_chunk(E - 1, 1, 1), held_chunk(0), held_chunk(1), between)
            body(held_chunk(0), held_chunk(1), None, lambda place: between(2 * FM + place))

        NCH = NG + 2 * E

        def piece(j, wset, stage):
            if j < 4:
                return wup_hi[wset][:, j // 2, j % 2, :], wup_lo[wset][:, j // 2, j % 2, :], stage[j % 3]
            m0 = (j - 4) * (FM // 2)
            return (wdn_hi[wset][:, m0:m0 + FM // 2, :], wdn_lo[wset][:, m0:m0 + FM // 2, :],
                    stage[j % 3].rearrange("p (m d) -> p m d", d=D))

        LAST0 = 8
        IN_HELD = (2 * FM * HELD - LAST0) // 2

        PLACES = 2 * FM * GB
        timetable = [[] for _ in range(PLACES)]
        for q in range(GB):
            for name, at in (("x_stats", 1), ("x_norm", 3), ("x_turn0", 4), ("x_low0", 5), ("x_turn1", 6),
                             ("x_gram", 7)):
                timetable[4 * q + at].append((name, q))
        for name, at in (("m_gram", 20), ("m_turn", 22), ("m_sym", 23), ("m_times_wqk", 24), ("m_keep_t", 25),
                         ("m_dots", 26), ("m_keep_s", 27), ("m_diag", 28), ("m_rowdiag", 30), ("m_logits", 31),
                         ("m_exp", 32), ("m_softmax", 33), ("m_times_wo", 34), ("m_keep_n", 35),
                         ("m_times_wv", 36), ("m_high", 36), ("m_low", 37)):
            timetable[at].append((name, 0))
        for q in range(GB):
            for name, at in (("o_mix", 0), ("o_stats", 1), ("o_norm", 3), ("o_add", 4), ("u_stats", 6),
                             ("u_norm", 9), ("u_turn0", 10), ("u_turn1", 11), ("u_route", 12)):
                timetable[38 + 4 * q + at].append((name, q))

        def o_bank(b, q):
            return 2 if isinstance(b, int) and b == 0 and q % 2 else 4

        LEAD = 8
        HT_STORED = 49

        def beside(steps, place, b):
            if place < LEAD:
                attend(steps, PLACES - LEAD + place, b - 1)
            else:
                attend(steps, place - LEAD, b)

        def beside_last(steps, route, place):
            if place < LEAD:
                attend(steps, PLACES - LEAD + place, B - 1)
            else:
                route(place - LEAD)

        shared_at = {9: 0, 13: 1, 17: 2, 20: 3, 24: 4, 28: 5}

        WEIGHTS_AT = (1, 3, 5, 7, 9, 11)

        def attend(steps, place, b):
            for name, q in timetable[place]:
                if name in steps:
                    steps[name](b, q)

        NR = 12
        NBLK = 2 * (NT // RB)
        R_IDX = NR + -(-NBLK // SR) + 1

        def blocks_at(place):
            n = SR * (place - NR)
            return range(n, min(n + SR, NBLK)) if n >= 0 else ()

        def last_add(v, eng, g, tiles, done):
            eng.wait_ge(t_x[g % TX], 16 * (g // TX + 1))
            eng.wait_ge(t_act, g + 1)
            x, y = flat4(last_x[g % TX][:, tiles, :]), flat4(last_y[g % TY][:, tiles, :])
            v.tensor_tensor(x, x, y, ALU.add).then_inc(done, 1)
        DVE_TILES, POOL_TILES = slice(0, 1), slice(1, GT)

        block = ctx.enter_context(nc.Block())

        @block.sync
        def _(sp):
            for opened in (xtlo_ok, hT_ok, g_done, o_ok, m_act, lno_ok, x2_ok, *x2_out, u_ok, u_out, ut_ps, lg_ps,
                           lg_ok, xhi_ok, xlo_ok, xt_ps, xn_ok, b_ps, ht_ps, h_out, act_ok, silu_ok, alo_ok, dn_done,
                           y_sb, *y_out):
                sp.sem_inc(opened, OPEN)

            def load_piece(w, j, up, dn, stage):
                if not (isinstance(w, int) and w == 0 and j < 3):
                    sp.wait_ge(w_lo, w * PIECES + (j - 2))
                    sp.sem_inc(sp_go, 1)
                if j < 4:
                    src = up[j // 2][(j % 2) * P:(j % 2 + 1) * P, :]
                    dst = stage[j % 3]
                else:
                    half = FM // 2
                    src = dn.rearrange("(m p) d -> p m d", p=P)[:, (j - 4) * half:(j - 3) * half, :]
                    dst = stage[j % 3].rearrange("p (m d) -> p m d", d=D)
                sp.dma_start(dst, src).then_inc(stage_in[j % 3], 16)

            def load_x(b, q):
                sp.dma_start(xin[:, q % 2, :, :], x_t[b * GB + q]).then_inc(x_in_s[q % 2], 16)

            def first_x(b, q):
                if q == 0:
                    for k in range(2):
                        sp.wait_ge(xn_ok, OPEN + b * GB + (k - 1 if k else 0))
                        sp.sem_inc(sp_go, 1)
                        load_x(b, k)

            def next_x(b, q):
                if q < 2:
                    sp.wait_ge(xn_ok, OPEN + b * GB + (q + 1))
                    sp.sem_inc(sp_go, 1)
                    load_x(b, q + 2)

            def load_res(b, q):
                sp.wait_ge(u_ok, OPEN + b * GB + (q - 1 if q >= 2 else 0))
                sp.sem_inc(sp_go, 1)
                sp.wait_ge(x2_out[q % 2], OPEN + b * (16 * (GB // 2)) + 16 * (q // 2))
                sp.sem_inc(sp_go, 1)
                sp.dma_start(x2[:, q % 2, :, :], x_t[b * GB + q]).then_inc(xres_in[q % 2], 16)

            def first_res(b, q):
                for k in range(2):
                    load_res(b, k)

            def store_x2(b, q):
                sp.wait_ge(x2_ok, OPEN + b * GB + (q + 1))
                sp.sem_inc(sp_go, 1)
                sp.dma_start(x2_t[b * GB + q], x2[:, q % 2, :, :]).then_inc(x2_out[q % 2], 16)

            def store_u(b, q):
                sp.wait_ge(u_ok, OPEN + b * GB + (q + 1))
                sp.sem_inc(sp_go, 1)
                sp.dma_start(u_t[b * GB + q], u[:, :, :]).then_inc(u_out, 16)
                if q < 2:
                    load_res(b, q + 2)

            def store_h(b, q):
                sp.wait_ge(hT_ok, OPEN + b * (2 * GB) + (2 * q + 2))
                sp.sem_inc(sp_go, 1)
                sp.dma_start(hT_d[b * GB + q], flat_h(hr)).then_inc(h_out, 16)

            steps = {"x_norm": next_x, "m_dots": first_res, "u_stats": store_x2, "u_turn0": store_u,
                     "u_turn1": store_h}

            def load_h(b, j):
                n = b * GB + j
                sp.wait_ge(h_out, OPEN + n * 16 + 16)
                sp.sem_inc(sp_go, 1)
                if not (isinstance(n, int) and n == 0):
                    sp.wait_ge(hlo_ok, n)
                    sp.sem_inc(sp_go, 1)
                sp.dma_start(flat_h(hfull), hT_d[n]).then_inc(h_in, 16)

            def store_y(b, j):
                sp.wait_ge(y_sb, OPEN + b * GB + (j + 1))
                sp.sem_inc(sp_go, 1)
                sp.dma_start(y_t[b * GB + j], ysb[:, j % 2, :, :]).then_inc(y_out[j % 2], 16)

            first_x(0, 0)
            for dst, src in ((wqk, Wqk), (tsb, Wv), (wo, Wo), (wr, Wr)):
                sp.dma_start(dst if dst is tsb else dst[:, :, :],
                             src.rearrange("(k p) n -> p k n", p=P)).then_inc(const_in, 16)
            with nc.allow_non_contiguous_dma(reason="vectors of 256 values"):
                for dst, src in ((gcol, ln_g), (bcol, ln_b)):
                    sp.dma_start(dst[:, :], src.rearrange("(k p) -> p k", p=P)).then_inc(const_in, 16)
                for h in range(HB):
                    src = tau.rearrange("(k h) a b -> (a b) h k", h=HB)[:, h, :]
                    sp.dma_start(taus[h * DH:(h + 1) * DH, :], src.broadcast_to([DH, KC])).then_inc(const_in, 16)
            for place in range(PLACES - LEAD):
                attend(steps, place, 0)
                if place in (2, 10):
                    for j in ((0, 1, 2) if place == 2 else (3, 4, 5)):
                        load_piece(0, j, [W1s, W3s], W2s, stage_first)
            sp.wait_ge(w_lo, PIECES)
            load_h(0, 0)

            with sp.Fori(1, B) as b:
                first_x(b, 0)
                for place in range(PLACES):
                    j, step = place // (2 * FM), place % (2 * FM)
                    if step == 2 and j < GB - 1:
                        load_h(b - 1, j + 1)
                    if step == 6 and j > 0:
                        store_y(b - 1, j - 1)
                    beside(steps, place, b)
                    if place == HT_STORED + LEAD + 1:
                        load_h(b, 0)
                store_y(b - 1, GB - 1)
            b = B - 1
            load_h(b, 1)
            for place in range(PLACES - LEAD, PLACES):
                attend(steps, place, b)
            for k in range(4):
                sp.wait_ge((xn_ok, xlo_ok, xt_ps, xt_ps)[k], OPEN + NG * (1, 1, 2, 2)[k])
                sp.sem_inc(sp_go, 1)
            for j in range(PIECES):
                load_piece(1, j, [W1[0], W3[0]], W2[0], stage_later)
            for j in range(GB - HELD):
                store_y(b, j)
            sp.wait_ge(const_ok, NCONST)
            for j in range(NZERO):
                sp.dma_start(y_zero[j], zrow[:, :]).then_inc(spare_out, 16)
            with sp.Fori(0, E - 1) as e:
                for j in range(PIECES):
                    load_piece(e + 2, j, [W1[e + 1], W3[e + 1]], W2[e + 1], stage_later)
            def load_held(h):
                sp.wait_ge(hlo_ok, held_chunk(h).n)
                sp.dma_start(flat_h(hfull), hT_d[FIRST + h]).then_inc(h_in, 16)
            load_held(0)
            for j in range(PIECES):
                load_piece(E + 1, j, [W1s, W3s], W2s, stage_later)
            load_held(1)
            sp.wait_ge(r_idx, 1)
            for k in range(2):
                sp.wait_ge(x2_out[k], OPEN + 16 * (NG // 2))
            sp.wait_ge(ht_ps, OPEN + 2 * 2 * E)
            for k in range(TX):
                sp.dma_start(last_x[k], last_view(x2_d, k)).then_inc(t_x[k], 16)
            sp.wait_ge(w_lo, PIECES * (E + 2))
            for k in range(2):
                sp.wait_ge(added[k], 16 * HALF * E)
            for k in range(TY):
                sp.dma_start(last_y[k], last_view(y_d[0:T, :], k)).then_inc(t_y[k], 16)
            for g in range(NG):
                sp.wait_ge(t_ok, g + 1)
                sp.wait_ge(t_okp, g + 1)
                if g + TY < NG:
                    sp.dma_start(last_y[g % TY], last_view(y_d[0:T, :], g + TY)).then_inc(t_y[g % TY], 16)
                sp.dma_start(last_view(out_d, g), last_x[g % TX]).then_inc(t_out[g % TX], 16)
                if 1 <= g and g - 1 + TX < NG:
                    k = (g - 1) % TX
                    sp.wait_ge(t_out[k], 16 * ((g - 1) // TX + 1))
                    sp.dma_start(last_x[k], last_view(x2_d, g - 1 + TX)).then_inc(t_x[k], 16)
            for k in range(TX):
                sp.wait_ge(t_out[k], 16 * (-(-(NG - k) // TX)))

        @block.gpsimd
        def _(pool):
            v = nc.gpsimd
            n_const = [0]

            def made(ins, settle=False):
                n_const[0] += 1
                ins.then_inc(const_ok, 1)
                if settle:
                    pool.wait_ge(const_ok, n_const[0])
            made(v.memset(mhalf[:, :], -0.5))
            made(v.memset(ones[:, :], 1.0))
            made(v.memset(onesb[:, :], 1.0))
            made(v.memset(zrow[:, :], 0.0))
            made(v.memset(headmask[:, :, :], 1.0))
            made(v.memset(carry[:, :, :], 1.0))
            made(v.iota(slot1[:, :], [[1, P]], base=1, channel_multiplier=0, allow_small_or_imprecise_dtypes=True))
            made(v.iota(colid[:, :], [[1, NC]], base=0, channel_multiplier=0, allow_small_or_imprecise_dtypes=True))
            made(v.iota(rank[:, :], [[-1, E]], base=E, channel_multiplier=0, allow_small_or_imprecise_dtypes=True))
            made(v.iota(estep[:, :], [[ST, E]], base=0, channel_multiplier=0, allow_small_or_imprecise_dtypes=True))
            made(v.iota(tokid[:, :], [[P, NT]], base=1, channel_multiplier=1, allow_small_or_imprecise_dtypes=True))
            made(v.iota(spare[:, :, :], [[0, E], [P, ST]], base=T + 1, channel_multiplier=1,
                        allow_small_or_imprecise_dtypes=True), True)
            made(v.memset(carry[:, :, 0:1], 0.0))
            made(v.affine_select(out=ident[:, :], in_=ones[:, :], compare_op=ALU.is_equal, fill=0.0, base=0,
                                 pattern=[[-1, P]], channel_multiplier=1))
            made(v.affine_select(out=earlier[:, :], in_=onesb[:, :], compare_op=ALU.is_ge, fill=0.0, base=-1,
                                 pattern=[[1, P]], channel_multiplier=-1))
            made(v.affine_select(out=headmask[:, :, :], in_=headmask[:, :, :], compare_op=ALU.is_ge, fill=0.0,
                                 base=0, pattern=[[-DH, HB], [0, DH]], channel_multiplier=1), True)
            made(v.affine_select(out=headmask[:, :, :], in_=headmask[:, :, :], compare_op=ALU.is_ge, fill=0.0,
                                 base=DH - 1, pattern=[[DH, HB], [0, DH]], channel_multiplier=-1))
            assert n_const[0] == NCONST

            def low_piece(w, j, wset, stage):
                hi, lo, src = piece(j, wset, stage)
                pool.wait_ge(w_hi, w * PIECES + (j + 1))
                v.tensor_tensor(lo, src, hi.bitcast(F32), ALU.subtract).then_inc(w_lo, 1)

            def x_rstd(b, q):
                pool.wait_ge(a_var, b * GB + (q + 1))
                v.tensor_tensor(rstd[:, :], veA[:, :], mhalf[:, :], ALU.pow).then_inc(a_rstd, 1)

            def x_part(b, q):
                pool.wait_ge(xhi_ok, OPEN + b * GB + (q + 1))
                v.tensor_tensor(xx[:, :, 1, :], xn[:, :, :], xx[:, :, 0, :].bitcast(F32),
                                ALU.subtract).then_inc(xlo_ok, 1)

            def o_rstd(b, q):
                pool.wait_ge(b_var, b * GB + (q + 1))
                v.tensor_tensor(rstdB[:, :], veB[:, :], mhalf[:, :], ALU.pow).then_inc(b_rstd, 1)

            def o_add(b, q):
                pool.wait_ge(lno_ok, OPEN + b * GB + (q + 1))
                pool.wait_ge(xres_in[q % 2], b * (16 * (GB // 2)) + 16 * (q // 2 + 1))
                v.tensor_tensor(x2[:, q % 2, :, :], ln_o[:, :, :], x2[:, q % 2, :, :], ALU.add).then_inc(x2_ok, 1)

            def u_rstd(b, q):
                pool.wait_ge(b_var2, b * GB + (q + 1))
                v.tensor_tensor(rstd2[:, :], ve2[:, :], mhalf[:, :], ALU.pow).then_inc(b_rstd2, 1)

            steps = {"x_stats": x_rstd, "x_low0": x_part, "o_stats": o_rstd, "o_add": o_add, "u_stats": u_rstd}

            for place in range(PLACES - LEAD):
                attend(steps, place, 0)
                if place in shared_at:
                    low_piece(0, shared_at[place], 0, stage_first)
            with pool.Fori(1, B) as b:
                for place in range(PLACES):
                    beside(steps, place, b)
            for place in range(PLACES - LEAD, PLACES):
                attend(steps, place, B - 1)
            for j in range(PIECES):
                low_piece(1, j, 1, stage_later)
            pool.wait_ge(r_slots, 1)
            for n in range(NBLK):
                r, c, cut = n % SR, n % 2, slice(n // 2 * RB, (n // 2 + 1) * RB)
                if n >= SR:
                    pool.wait_ge(r_mm, n - SR + 1)
                pool.wait_ge(r_selE, n + 1)
                v.tensor_tensor(selB[:, r, :, 0, :], selE[:, r, :, :], along(tokid[:, cut], NC), ALU.mult)
                v.tensor_tensor(selB[:, r, :, 1, :], selE[:, r, :, :], along(gates[:, c, cut], NC),
                                ALU.mult).then_inc(r_sel, 1)

            def gather(e, part):
                if not (isinstance(e, int) and e == 0):
                    pool.wait_ge(gathered[part], e * (16 * HALF))
                pool.sem_inc(pool_go, 1)
                v.tensor_copy(gcur[:, part, :], gidx[:, bass.ds(e * ST + part * HALF, HALF)]).then_inc(g_cur, 1)
                pool.wait_ge(g_cur, e * 2 + (part + 1))
                if not (isinstance(e, int) and e == 0):
                    x = e * 2 + part
                    pool.wait_ge(ht_ps, OPEN + x * 2 - 2)
                pool.sem_inc(pool_go, 1)
                for t in range(HALF):
                    w = LASTW if part * HALF + t == ST - 1 else P
                    pool.indirect_dma_start(rows[0:w, part, t, :], None, u_d,
                                            bass.IndirectOffsetOnAxis(ap=gcur[0:w, part, t:t + 1], axis=0)
                                            ).then_inc(gathered[part], 16)

            def release(e, part):
                if not (isinstance(e, int) and e == 0):
                    pool.wait_ge(added[part], e * (16 * HALF))
                pool.sem_inc(ysb_free[part], 1)

            def scatter(e, part):
                n = e * 2 + (FIRST + part)
                v.tensor_copy(scur[:, part, :], sidx[:, bass.ds(e * ST + part * HALF, HALF)]).then_inc(s_cur, 1)
                pool.wait_ge(s_cur, e * 2 + (part + 1))
                pool.wait_ge(y_sb, OPEN + n + 1)
                for s in range(2):
                    pool.wait_ge(y_out[s], OPEN + 16 * (FIRST // 2))
                    if not (isinstance(e, int) and e == 0):
                        pool.wait_ge(added[s], e * (16 * HALF))
                pool.wait_ge(spare_out, 16 * NZERO)
                pool.sem_inc(pool_go, 1)
                for t in range(HALF):
                    w = LASTW if part * HALF + t == ST - 1 else P
                    pool.indirect_dma_start(y_d, bass.IndirectOffsetOnAxis(ap=scur[0:w, part, t:t + 1], axis=0),
                                            ysb[0:w, part, t, :], None, compute_op=ALU.add
                                            ).then_inc(added[part], 16)

            pool.wait_ge(r_idx, 1)
            gather(0, 0)
            gather(0, 1)
            release(0, 0)
            release(0, 1)
            gather(1, 0)
            gather(1, 1)
            for j in range(PIECES):
                if j == 2:
                    scatter(0, 0)
                low_piece(2, j, 0, stage_later)

            def during(e, other):
                release(e, 0)
                gather(e + 1, 0)
                scatter(e - 1, 1)
                gather(e + 1, 1)
                release(e, 1)
                for j in range(PIECES):
                    if j == 2:
                        scatter(e, 0)
                    low_piece(e + 2, j, other, stage_later)

            during(1, 1)
            with pool.Fori(1, (E - 1) // 2) as i:
                for s in range(2):
                    during(i * 2 + s, s)
            release(E - 1, 0)
            scatter(E - 2, 1)
            release(E - 1, 1)
            for j in range(PIECES):
                if j == 2:
                    scatter(E - 1, 0)
                low_piece(E + 1, j, 0, stage_later)
            scatter(E - 1, 1)
            for g in range(NG):
                pool.wait_ge(t_var, g + 1)
                v.tensor_tensor(t_scale[g % 2], veA[:, :], mhalf[:, :], ALU.pow).then_inc(t_rstd, 1)
                if g > 0:
                    last_add(v, pool, g - 1, POOL_TILES, t_okp)
            last_add(v, pool, NG - 1, POOL_TILES, t_okp)

        @block.scalar
        def _(act_e):
            s = nc.scalar

            def x_high(b, q):
                act_e.wait_ge(xn_ok, OPEN + b * GB + (q + 1))
                act_e.wait_ge(g_done, OPEN + b * GB + q)
                s.activation(xx[:, :, 0, :], xn[:, :, :], ACT.Copy).then_inc(xhi_ok, 1)

            def x_keep(k):
                def step(b, q):
                    act_e.wait_ge(xt_ps, OPEN + b * (2 * GB) + (2 * q + k + 1))
                    if q == 0 and k == 0:
                        act_e.wait_ge(o_ok, OPEN + b * GB)
                    s.activation(xT_hi[:, k, q * GW:(q + 1) * GW], bank[6 + k][:, :], ACT.Copy).then_inc(xthi_ok, 1)
                return step

            def m_step(dst, src, ready, count, func=ACT.Copy):
                def step(b, q):
                    act_e.wait_ge(ready, b * (MP if ready is m_pe else MD) + count)
                    s.activation(dst, src, func).then_inc(m_act, 1)
                return step

            def m_gram(b, q):
                act_e.wait_ge(g_done, OPEN + b * GB + GB)
                act_e.wait_ge(x2_ok, OPEN + b * GB)
                for k in range(KC):
                    ins = s.activation(gs[:, k, :], bank[4 + k][:, :], ACT.Copy)
                ins.then_inc(m_act, 1)

            def keep_s(b, q):
                act_e.wait_ge(lg_ps, OPEN + b * GB)
                act_e.wait_ge(h_out, OPEN + b * (16 * GB))
                m_step(hr[:, 0, 0:KC * P], bank[6][:, 0:KC * P], m_pe, 3)(b, q)

            def o_norm(b, q):
                act_e.wait_ge(b_nb, b * GB + (q + 1))
                act_e.wait_ge(x2_ok, OPEN + b * GB + q)
                for t in range(GT):
                    ins = s.activation(ln_o[:, t, :], bank[o_bank(b, q) + t // 2][:, (t % 2) * D:(t % 2 + 1) * D],
                                       ACT.Identity, scale=rstdB[:, t:t + 1], bias=nbiasB[:, t:t + 1])
                ins.then_inc(lno_ok, 1)

            def u_keep(k):
                def step(b, q):
                    act_e.wait_ge(ut_ps, OPEN + b * (2 * GB) + (2 * q + k + 1))
                    act_e.wait_ge(lg_ps, OPEN + b * GB + q)
                    act_e.wait_ge(h_out, OPEN + b * (16 * GB) + 16 * q)
                    s.activation(hr[:, k, :], bank[6 + k][:, :], ACT.Identity,
                                 scale=gcol[:, k:k + 1], bias=bcol[:, k:k + 1]).then_inc(hT_ok, 1)
                return step

            tflat = flat4(tsb)
            steps = {"x_turn0": x_high, "x_low0": x_keep(0), "x_gram": x_keep(1), "m_gram": m_gram,
                     "m_keep_t": m_step(tflat, bank[4][:, :], m_pe, 2), "m_keep_s": keep_s,
                     "m_exp": m_step(lc[:, :, :], lc[:, :, :], m_dve, 3, ACT.Exp),
                     "m_keep_n": m_step(tflat, bank[6][:, :], m_pe, 5),
                     "m_high": m_step(m_hi[:, :, :].rearrange("p k d -> p (k d)"), bank[4][:, :], m_pe, 6),
                     "o_norm": o_norm, "u_turn0": u_keep(0), "u_turn1": u_keep(1)}

            def prep(c, k):
                if c.expert is not None:
                    act_e.wait_ge(ht_ps, OPEN + c.x * 2 + (k + 1))
                    act_e.wait_ge(hlo_ok, c.n)
                    s.activation(hfull[:, k, 0:c.w], bank[7][:, 0:c.w], ACT.Identity,
                                 scale=gcol[:, k:k + 1], bias=bcol[:, k:k + 1]).then_inc(hf_ok, 1)
                if k == KC - 1:
                    if c.expert is not None:
                        act_e.wait_ge(hf_ok, c.x * 2 + 2)
                    else:
                        act_e.wait_ge(h_in, c.landed)
                    if not (isinstance(c.n, int) and c.n == 0):
                        act_e.wait_ge(b_ps, OPEN + (c.n - 1) * FM)
                    s.activation(h_hi[:, c.slot, :, 0:c.w], hfull[:, :, 0:c.w], ACT.Copy).then_inc(hhi_ok, 1)

            def high_piece(w, j, wset, stage):
                if j == 0:
                    if isinstance(w, int) and w == 1:
                        act_e.wait_ge(o_ok, OPEN + NG)
                        act_e.wait_ge(g_done, OPEN + NG)
                    elif not (isinstance(w, int) and w == 0):
                        act_e.wait_ge(dn_done, OPEN + w * (2 * FM) + FM * (FIRST - 4))
                hi, lo, src = piece(j, wset, stage)
                act_e.wait_ge(stage_in[j % 3], w * 32 + 16 * (j // 3 + 1))
                s.activation(hi, src, ACT.Copy).then_inc(w_hi, 1)

            def high(c, m):
                act_e.wait_ge(act_ok, OPEN + c.n * FM + (m + 1))
                act_e.wait_ge(dn_done, OPEN + c.n * FM + (m - 3))
                s.activation(act_hi[:, m % 4, 0:c.w], act[:, m % 2, 0:c.w], ACT.Copy).then_inc(ahi_ok, 1)

            def take_y(c):
                act_e.wait_ge(dn_done, OPEN + c.n * FM + FM)
                if c.expert is None:
                    if isinstance(c.n, int) and c.n >= FIRST:
                        act_e.wait_ge(added[c.slot], 16 * HALF * E)
                    else:
                        act_e.wait_ge(y_out[c.slot], OPEN + c.stored)
                    for h in range(2):
                        ins = s.activation(flat4(ysb[:, c.slot, 2 * h:2 * h + 2, :]), bank[2 + h][:, :], ACT.Copy)
                else:
                    act_e.wait_ge(y_out[c.slot], OPEN + 16 * (FIRST // 2))
                    act_e.wait_ge(ysb_free[c.slot], c.expert + 1)
                    for t, w in enumerate(c.widths):
                        col = c.expert * ST + (c.slot * HALF + t + NC)
                        ins = s.activation(ysb[0:w, c.slot, t, :], bank[2 + t // 2][0:w, (t % 2) * D:(t % 2 + 1) * D],
                                           ACT.Copy, scale=table2[0:w, bass.ds(col, 1)])
                ins.then_inc(y_sb, 1)

            def body(prev, c, nxt, between=lambda place: None):
                for m in range(FM):
                    if m == 2 and prev is not None:
                        take_y(prev)
                    act_e.wait_ge(a_ps, c.n * FM + (m + 1))
                    act_e.wait_ge(alo_ok, OPEN + c.n * FM + (m - 1))
                    a = bank[4 if c.wide and m % 2 else 0]
                    s.activation(act[:, m % 2, 0:c.w], a[:, 0:c.w], ACT.Silu).then_inc(silu_ok, 1)
                    between(2 * m)
                    if m > 0:
                        high(c, m - 1)
                    elif prev is not None:
                        high(prev, FM - 1)
                    if m in (4, 5) and nxt is not None:
                        prep(nxt, m - 4)
                    between(2 * m + 1)

            act_e.wait_ge(wvT_ps, 1)
            s.activation(wvT[:, :, :].rearrange("p k d -> p (k d)"), bank[6][:, :], ACT.Copy).then_inc(wvT_ok, 1)
            act_e.wait_ge(const_in, 16 * NSMALL)
            for place in range(PLACES - LEAD):
                attend(steps, place, 0)
                if place in shared_at:
                    high_piece(0, shared_at[place], 0, stage_first)
            for k in range(KC):
                prep(shared_chunk(0, 0), k)
            with act_e.Fori(1, B) as b:
                cs = [shared_chunk(b - 1, j) for j in range(GB)] + [shared_chunk(b, 0)]
                for j in range(GB):
                    body(cs[j - 1] if j else None, cs[j], cs[j + 1] if j < GB - 1 else None,
                         lambda place: beside(steps, 2 * FM * j + place, b))
                high(cs[GB - 1], FM - 1)
                prep(cs[GB], KC - 1)
                take_y(cs[GB - 1])

            def route(place):
                if place == 5:
                    act_e.wait_ge(r_d, 1)
                    s.activation(rsmall[:, 1, 0:NT], rsmall[:, 0, 0:NT], ACT.Exp).then_inc(r_ex, 1)
                if place % 2 and 3 <= place < 3 + 2 * PIECES:
                    high_piece(1, (place - 3) // 2, 1, stage_later)

            cs = last_chunks()
            body(None, cs[0], cs[1], lambda place: beside_last(steps, route, place))
            body(cs[0], cs[1], None, lambda place: beside_last(steps, route, 2 * FM + place))
            high(cs[1], FM - 1)
            take_y(cs[1])
            for k in range(KC):
                prep(expert_chunk(0, 0, 1), k)

            def body_and_weights(prev, c, nxt):
                def weights(place):
                    if place in WEIGHTS_AT and c.slot == 1:
                        high_piece(c.expert + 2, WEIGHTS_AT.index(place), 1 - c.wset, stage_later)
                body(prev, c, nxt, weights)
            routed_chunks(act_e, body_and_weights)
            def last_norm(g):
                act_e.wait_ge(t_nb, g + 1)
                y = last_y[g % TY]
                for t in range(GT):
                    ins = s.activation(y[:, t, :], y[:, t, :], ACT.Identity,
                                       scale=t_scale[g % 2][:, t:t + 1], bias=nbias[:, t:t + 1])
                ins.then_inc(t_act, 1)

            def last_pass(place):
                if place > LAST0 and place % 2 == 0:
                    last_norm((place - LAST0) // 2 - 1)
            held_chunks(body, last_pass)
            high(held_chunk(1), FM - 1)
            take_y(held_chunk(1))
            for g in range(IN_HELD - 1, NG):
                last_norm(g)

        @block.tensor
        def _(pe):
            t_ = nc.tensor

            def three(o, a_hi, a_lo, b_hi, b_lo, start, stop):
                t_.matmul(o, a_lo, b_hi, start=start, stop=False, skip_group_check=True)
                t_.matmul(o, a_hi, b_lo, start=False, stop=False, skip_group_check=True)
                return t_.matmul(o, a_hi, b_hi, start=False, stop=stop, skip_group_check=True)

            def x_turn(k):
                def step(b, q):
                    if k == 0:
                        pe.wait_ge(xn_ok, OPEN + b * GB + (q + 1))
                        pe.wait_ge(xtlo_ok, OPEN + b * (2 * GB) + 2 * q)
                    if q == 0 and k == 0:
                        pe.wait_ge(lg_ok, OPEN + b * GB)
                    for t in range(GT):
                        ins = t_.transpose(bank[6 + k][:, t * P:(t + 1) * P], xn[:, t, k * P:(k + 1) * P], ident[:, :])
                    ins.then_inc(xt_ps, 1)
                return step

            def x_gram(b, q):
                pe.wait_ge(xlo_ok, OPEN + b * GB + (q + 1))
                if q == 0:
                    pe.wait_ge(lno_ok, OPEN + b * GB)
                for t in range(GT):
                    for k in range(KC):
                        ins = t_.matmul(bank[4 + k][:, :], xx[:, t, 0, k * P:(k + 1) * P],
                                        xx[:, t, :, :].rearrange("p h d -> p (h d)"),
                                        start=(q == 0 and t == 0), stop=(q == GB - 1 and t == GT - 1))
                ins.then_inc(g_done, 1)

            def m_turn(b, q):
                pe.wait_ge(m_act, OPEN + b * MA + 1)
                pe.wait_ge(xtlo_ok, OPEN + b * (2 * GB) + 2 * GB)
                for k in range(KC):
                    for c in range(KC):
                        ins = t_.transpose(bank[6][:, k * D + c * P:k * D + (c + 1) * P],
                                           gs[:, c, D + k * P:D + (k + 1) * P], ident[:, :])
                ins.then_inc(m_pe, 1)

            def m_times_wqk(b, q):
                pe.wait_ge(m_dve, b * MD + 1)
                for c in range(KC):
                    for k in range(KC):
                        ins = t_.matmul(bank[4][:, c * D:(c + 1) * D], gf[:, k, c * P:(c + 1) * P], wqk[:, k, :],
                                        start=(k == 0), stop=(k == KC - 1))
                ins.then_inc(m_pe, 1)

            def m_dots(b, q):
                pe.wait_ge(m_act, OPEN + b * MA + 2)
                for c in range(KC):
                    for k in range(KC):
                        ins = t_.matmul(bank[6][:, c * P:(c + 1) * P], wqk[:, k, c * P:(c + 1) * P],
                                        tsb[:, k, c * P:(c + 1) * P], start=(k == 0), stop=(k == KC - 1))
                ins.then_inc(m_pe, 1)

            def m_rowdiag(b, q):
                pe.wait_ge(m_dve, b * MD + 2)
                t_.matmul(bank[5][:, 0:KC * P], ones[:, :], hr[:, 0, KC * P:2 * KC * P],
                          start=True, stop=True).then_inc(m_pe, 1)

            def m_times_wo(b, q):
                pe.wait_ge(m_dve, b * MD + 4)
                for c in range(KC):
                    ins = t_.matmul(bank[6][:, c * D:(c + 1) * D], sD[:, c, :], wo[:, c, :], start=True, stop=True)
                ins.then_inc(m_pe, 1)

            def m_times_wv(b, q):
                pe.wait_ge(m_act, OPEN + b * MA + 5)
                pe.wait_ge(wvT_ok, 1)
                for c in range(KC):
                    for k in range(KC):
                        ins = t_.matmul(bank[4][:, c * D:(c + 1) * D], wvT[:, k, c * P:(c + 1) * P], tsb[:, k, :],
                                        start=(k == 0), stop=(k == KC - 1))
                ins.then_inc(m_pe, 1)

            def o_mix(b, q):
                if q == 0:
                    pe.wait_ge(m_dve, b * MD + MD)
                if not (isinstance(b, int) and b == 0):
                    pe.wait_ge(lno_ok, OPEN + b * GB + q)
                elif q > 1:
                    pe.wait_ge(lno_ok, OPEN + (q - 1))
                for t in range(GT):
                    o = bank[o_bank(b, q) + t // 2][:, (t % 2) * D:(t % 2 + 1) * D]
                    cols = slice(q * GW + t * P, q * GW + (t + 1) * P)
                    for k in range(KC):
                        ins = three(o, xT_hi[:, k, cols], xT_lo[:, k, cols], m_hi[:, k, :], m_lo[:, k, :],
                                    k == 0, k == KC - 1)
                ins.then_inc(o_ok, 1)

            def u_turn(k):
                def step(b, q):
                    if k == 0:
                        pe.wait_ge(u_ok, OPEN + b * GB + (q + 1))
                        pe.wait_ge(lg_ok, OPEN + b * GB + q)
                    for t in range(GT):
                        ins = t_.transpose(bank[6 + k][:, t * P:(t + 1) * P], u[:, t, k * P:(k + 1) * P], ident[:, :])
                    ins.then_inc(ut_ps, 1)
                return step

            def u_route(b, q):
                pe.wait_ge(hT_ok, OPEN + b * (2 * GB) + (2 * q + 2))
                for t in range(GT):
                    for k in range(KC):
                        ins = t_.matmul(bank[6][:, t * 8:t * 8 + E], hr[:, k, t * P:(t + 1) * P], wr[:, k, :],
                                        start=(k == 0), stop=(k == KC - 1))
                ins.then_inc(lg_ps, 1)

            steps = {"x_turn0": x_turn(0), "x_turn1": x_turn(1), "x_gram": x_gram, "m_turn": m_turn,
                     "m_times_wqk": m_times_wqk, "m_dots": m_dots, "m_rowdiag": m_rowdiag,
                     "m_times_wo": m_times_wo, "m_times_wv": m_times_wv, "o_mix": o_mix,
                     "u_turn0": u_turn(0), "u_turn1": u_turn(1), "u_route": u_route}

            def turn(c, k):
                if k == 0:
                    pe.wait_ge(gathered[c.slot], c.landed)
                if not (isinstance(c.x, int) and c.x == 0 and k == 0):
                    pe.wait_ge(hf_ok, c.x * 2 + k)
                for t, w in enumerate(c.widths):
                    ins = t_.transpose(bank[7][:, t * P:t * P + w], rows[0:w, c.slot, t, k * P:(k + 1) * P],
                                       ident[0:w, 0:w])
                ins.then_inc(ht_ps, 1)

            def up(c, m, first_wide):
                if m == 0:
                    pe.wait_ge(hlo_ok, c.n + 1)
                    pe.wait_ge(w_lo, c.opening)
                back = 1 if c.wide and not (first_wide and m == 0) else 0
                for which, freed, full in ((0, silu_ok, a_ps), (1, act_ok, b_ps)):
                    o = bank[(4 if c.wide and m % 2 else 0) + which][:, 0:c.w]
                    pe.wait_ge(freed, OPEN + c.n * FM + (m - back))
                    for k in range(KC):
                        wh = wup_hi[c.wset][:, which, k, m * P:(m + 1) * P]
                        wl = wup_lo[c.wset][:, which, k, m * P:(m + 1) * P]
                        ins = three(o, wh, wl, h_hi[:, c.slot, k, 0:c.w], h_lo[:, c.slot, k, 0:c.w],
                                    k == 0, k == KC - 1)
                    ins.then_inc(full, 1)

            def down(c, m):
                pe.wait_ge(alo_ok, OPEN + c.n * FM + (m + 1))
                if m == 0:
                    pe.wait_ge(y_sb, OPEN + c.n)
                for t, w in enumerate(c.widths):
                    cols = slice(t * P, t * P + w)
                    ins = three(bank[2 + t // 2][0:w, (t % 2) * D:(t % 2 + 1) * D],
                                act_hi[:, m % 4, cols], act_lo[:, m % 4, cols],
                                wdn_hi[c.wset][:, m, :], wdn_lo[c.wset][:, m, :],
                                m == 0 and t % 2 == 0, m == FM - 1)
                ins.then_inc(dn_done, 1)

            def body(prev, c, nxt, between=lambda place: None):
                first_wide = c.wide and prev is not None and not prev.wide
                for m in range(FM):
                    up(c, m, first_wide)
                    between(2 * m)
                    if m in (4, 5) and nxt is not None and nxt.expert is not None:
                        turn(nxt, m - 4)
                    if m >= 2:
                        down(c, m - 2)
                    elif prev is not None:
                        down(prev, m + FM - 2)
                    between(2 * m + 1)

            pe.wait_ge(const_ok, NCONST)
            pe.wait_ge(const_in, 16 * NSMALL)
            for k in range(KC):
                for c in range(KC):
                    ins = t_.transpose(bank[6][:, k * D + c * P:k * D + (c + 1) * P], tsb[:, c, k * P:(k + 1) * P],
                                       ident[:, :])
            ins.then_inc(wvT_ps, 1)
            pe.wait_ge(wvT_ok, 1)
            for place in range(PLACES - LEAD):
                attend(steps, place, 0)
            with pe.Fori(1, B) as b:
                cs = [shared_chunk(b - 1, j) for j in range(GB)] + [shared_chunk(b, 0)]
                for j in range(GB):
                    body(cs[j - 1] if j else None, cs[j], cs[j + 1] if j < GB - 1 else None,
                         lambda place: beside(steps, 2 * FM * j + place, b))
                for m in (FM - 2, FM - 1):
                    down(cs[GB - 1], m)

            def count(c, which, to):
                pe.wait_ge(r_oh, c + 1)
                t_.matmul(bank[to][:, 0:E * NT], (earlier, onesb)[which][:, :],
                          oh[:, c, :, :].rearrange("p e t -> p (e t)"), start=True, stop=True).then_inc(r_cnt, 1)

            def route(place):
                if place == 2:
                    count(0, 1, 4)
                    count(0, 0, 5)
                elif place == 4:
                    count(1, 0, 6)
                elif place == 6:
                    pe.wait_ge(r_scan, 1)
                    count(1, 1, 4)
                elif place == 9:
                    pe.wait_ge(r_scan, 3)
                for n in blocks_at(place - 1):
                    pe.wait_ge(r_selA, n + 1)
                    pe.wait_ge(r_sel, n + 1)
                    for t in range(RB):
                        ins = t_.matmul(bank[6][:, 0:2 * NC], selA[:, n % SR, t, :],
                                        selB[:, n % SR, t, :, :].rearrange("p a c -> p (a c)"),
                                        start=(n == 0 and t == 0), stop=(n == NBLK - 1 and t == RB - 1))
                    ins.then_inc(r_mm, 1)

            cs = last_chunks()
            body(None, cs[0], cs[1], lambda place: beside_last(steps, route, place))
            body(cs[0], cs[1], None, lambda place: beside_last(steps, route, 2 * FM + place))
            for m in (FM - 2, FM - 1):
                down(cs[1], m)
            for place in range(2 * FM * (GB - HELD) - LEAD, R_IDX + 1):
                route(place)
            for k in range(KC):
                turn(expert_chunk(0, 0, 1), k)
            routed_chunks(pe, body)
            held_chunks(body)
            for m in (FM - 2, FM - 1):
                down(held_chunk(1), m)

        @block.vector
        def _(dve):
            v = nc.vector
            SQ = float(np.sqrt(np.float32(N)))

            def stats(ch, src, st_, mv_):
                for t in range(GT):
                    ins = v.bn_stats(st_[:, t, :], src(t))
                ch.link(ins)
                dve.sem_inc(dve_go, 1)
                for t in range(GT):
                    ins = v.bn_aggr(mv_[:, t, :], st_[:, t, :])
                ch.link(ins)

            def x_stats(b, q):
                dve.wait_ge(x_in_s[q % 2], b * (8 * GB) + 16 * (q // 2 + 1))
                ch = Chain(dve, a_chain, (b * GB + q) * 2)
                stats(ch, lambda t: xin[:, q % 2, t, :], st, mv)
                v.tensor_scalar(veA[:, :], mv[:, :, 1], EPS, None, ALU.add).then_inc(a_var, 1)

            def x_norm(b, q):
                g = b * GB + q
                dve.wait_ge(a_rstd, g + 1)
                dve.wait_ge(xhi_ok, OPEN + g)
                dve.wait_ge(xlo_ok, OPEN + g)
                dve.wait_ge(xt_ps, OPEN + g * 2)
                for t in range(GT):
                    ins = v.tensor_scalar(xn[:, t, :], xin[:, q % 2, t, :], mv[:, t, 0:1], rstd[:, t:t + 1],
                                          ALU.subtract, ALU.mult)
                ins.then_inc(xn_ok, 1)

            def x_low(k):
                def step(b, q):
                    dve.wait_ge(xthi_ok, b * (2 * GB) + (2 * q + k + 1))
                    v.tensor_tensor(xT_lo[:, k, q * GW:(q + 1) * GW], bank[6 + k][:, :],
                                    xT_hi[:, k, q * GW:(q + 1) * GW].bitcast(F32), ALU.subtract).then_inc(xtlo_ok, 1)
                return step

            M_AT = {"turn": 0, "logits": 1, "softmax": 6}
            M_STEPS = 9
            gflat = flat4(gf)

            def m_sum(b, q):
                dve.wait_ge(m_act, OPEN + b * MA + 1)
                dve.wait_ge(u_out, OPEN + b * (16 * GB))
                dve.wait_ge(ut_ps, OPEN + b * (2 * GB))
                ch = Chain(dve, m_chain, b * M_STEPS + M_AT["turn"])
                ch.step(v.tensor_tensor(gf, gs[:, :, 0:D], gs[:, :, D:2 * D], ALU.add))

            def m_sym(b, q):
                dve.wait_ge(m_chain, b * M_STEPS + 1)
                dve.wait_ge(m_pe, b * MP + 1)
                v.tensor_tensor(gflat, gflat, bank[6][:, :], ALU.add).then_inc(m_dve, 1)

            def m_diag(b, q):
                dve.wait_ge(m_act, OPEN + b * MA + 3)
                v.tensor_tensor(sD, sS, ident[:, :].rearrange("p (a j) -> p a j", a=1).broadcast_to([P, KC, P]),
                                ALU.mult).then_inc(m_dve, 1)
                dve.wait_ge(m_dve, b * MD + 2)
                v.tensor_reduce(small[:, 0, :], sD, AX.X, ALU.add)

            def m_logits(b, q):
                ch = Chain(dve, m_chain, b * M_STEPS + M_AT["logits"])
                dve.wait_ge(m_pe, b * MP + 4)
                ch.link(v.scalar_tensor_tensor(out=hr[:, 0, 0:KC * P], in0=hr[:, 0, 0:KC * P], scalar=2.0,
                                               in1=bank[5][:, 0:KC * P], op0=ALU.mult, op1=ALU.subtract))
                hm = headmask[:, :, :].rearrange("p h e -> p (h e)").rearrange("p (a j) -> p a j", a=1)
                ch.link(v.tensor_tensor(sS, sS, hm.broadcast_to([P, KC, P]), ALU.mult))
                ch.link(v.tensor_reduce(lc[:, :, :], sS.rearrange("p k (h e) -> p k e h", e=DH), AX.X, ALU.add))
                for k in range(KC):
                    ins = v.tensor_scalar(lc[:, k, :], lc[:, k, :], small[:, 0, k:k + 1], taus[:, k:k + 1],
                                          ALU.subtract, ALU.mult)
                ch.link(ins)
                ch.link(v.tensor_reduce(small[:, 1, :], lc[:, :, :], AX.X, ALU.max))
                for k in range(KC):
                    ins = v.tensor_scalar(lc[:, k, :], lc[:, k, :], small[:, 1, k:k + 1], None, ALU.subtract)
                ins.then_inc(m_dve, 1)

            def m_softmax(b, q):
                ch = Chain(dve, m_chain, b * M_STEPS + M_AT["softmax"])
                dve.wait_ge(m_act, OPEN + b * MA + 4)
                ch.link(v.tensor_reduce(small[:, 2, :], lc[:, :, :], AX.X, ALU.add))
                ch.link(v.reciprocal(small[:, 3, :], small[:, 2, :]))
                for k in range(KC):
                    ins = v.tensor_scalar(lc[:, k, :], lc[:, k, :], small[:, 3, k:k + 1], None, ALU.mult)
                ch.link(ins)
                for k in range(KC):
                    own = lc[:, k, :].rearrange("p (a e) -> p a e", a=1).broadcast_to([P, HB, DH])
                    ins = v.tensor_tensor(sD[:, k, :].rearrange("p (h e) -> p h e", e=DH), headmask[:, :, :],
                                          own, ALU.mult)
                ins.then_inc(m_dve, 1)

            def m_low(b, q):
                flat = lambda t: t.rearrange("p k d -> p (k d)")
                dve.wait_ge(m_act, OPEN + b * MA + 6)
                v.tensor_tensor(flat(m_lo[:, :, :]), bank[4][:, :], flat(m_hi[:, :, :]).bitcast(F32),
                                ALU.subtract).then_inc(m_dve, 1)

            def o_stats(b, q):
                ch = Chain(dve, b_chain, (b * GB + q) * 2)
                dve.wait_ge(o_ok, OPEN + b * GB + (q + 1))
                stats(ch, lambda t: bank[o_bank(b, q) + t // 2][:, (t % 2) * D:(t % 2 + 1) * D], stB, mvB)
                v.tensor_scalar(veB[:, :], mvB[:, :, 1], EPS, None, ALU.add).then_inc(b_var, 1)

            def o_norm(b, q):
                dve.wait_ge(b_rstd, b * GB + (q + 1))
                v.scalar_tensor_tensor(out=nbiasB[:, :], in0=mvB[:, :, 0], scalar=-1.0, in1=rstdB[:, :],
                                       op0=ALU.mult, op1=ALU.mult).then_inc(b_nb, 1)

            def u_stats(b, q):
                ch = Chain(dve, u_chain, (b * GB + q) * 2)
                dve.wait_ge(x2_ok, OPEN + b * GB + (q + 1))
                stats(ch, lambda t: x2[:, q % 2, t, :], st2, mv2)
                v.tensor_scalar(ve2[:, :], mv2[:, :, 1], 1.0 + EPS, EPS * EPS, ALU.mult, ALU.add).then_inc(b_var2, 1)

            def u_norm(b, q):
                g = b * GB + q
                dve.wait_ge(b_rstd2, g + 1)
                dve.wait_ge(u_out, OPEN + g * 16)
                dve.wait_ge(ut_ps, OPEN + g * 2)
                for t in range(GT):
                    ins = v.tensor_scalar(u[:, t, :], x2[:, q % 2, t, :], mv2[:, t, 0:1], rstd2[:, t:t + 1],
                                          ALU.subtract, ALU.mult)
                ins.then_inc(u_ok, 1)

            def u_route(b, q):
                g = b * GB + q
                dve.wait_ge(lg_ps, OPEN + g + 1)
                v.tensor_copy(lg[:, :, bass.ds(g * GT, GT)],
                              bank[6][:, 0:GT * 8].rearrange("p (t e) -> p e t", e=8)[:, 0:E, :]).then_inc(lg_ok, 1)

            steps = {"x_stats": x_stats, "x_norm": x_norm, "x_low0": x_low(0), "x_gram": x_low(1),
                     "m_turn": m_sum, "m_sym": m_sym, "m_diag": m_diag, "m_logits": m_logits,
                     "m_softmax": m_softmax, "m_low": m_low, "o_stats": o_stats, "o_norm": o_norm,
                     "u_stats": u_stats, "u_norm": u_norm, "u_route": u_route}

            def prep(c):
                dve.wait_ge(hhi_ok, c.n + 1)
                if not (isinstance(c.n, int) and c.n == 0):
                    dve.wait_ge(b_ps, OPEN + (c.n - 1) * FM)
                v.tensor_tensor(h_lo[:, c.slot, :, 0:c.w], hfull[:, :, 0:c.w],
                                h_hi[:, c.slot, :, 0:c.w].bitcast(F32), ALU.subtract).then_inc(hlo_ok, 1)

            def low(c, m):
                dve.wait_ge(ahi_ok, c.n * FM + (m + 1))
                dve.wait_ge(dn_done, OPEN + c.n * FM + (m - 3))
                v.tensor_tensor(act_lo[:, m % 4, 0:c.w], act[:, m % 2, 0:c.w],
                                act_hi[:, m % 4, 0:c.w].bitcast(F32), ALU.subtract).then_inc(alo_ok, 1)

            def body(prev, c, nxt, between=lambda place: None):
                for m in range(FM):
                    dve.wait_ge(silu_ok, OPEN + c.n * FM + (m + 1))
                    dve.wait_ge(b_ps, OPEN + c.n * FM + (m + 1))
                    v.tensor_tensor(act[:, m % 2, 0:c.w], bank[(4 if c.wide and m % 2 else 0) + 1][:, 0:c.w],
                                    act[:, m % 2, 0:c.w], ALU.mult).then_inc(act_ok, 1)
                    between(2 * m)
                    if m > 0:
                        low(c, m - 1)
                    elif prev is not None:
                        low(prev, FM - 1)
                    if m == 6 and nxt is not None:
                        prep(nxt)
                    between(2 * m + 1)

            dve.wait_ge(const_in, 16 * NSMALL)
            v.tensor_scalar(taus[:, :], taus[:, :], 1.0 / SQ, None, ALU.mult).then_inc(tau_ok, 1)
            dve.wait_ge(tau_ok, 1)
            dve.wait_ge(const_ok, NCONST)
            for place in range(PLACES - LEAD):
                attend(steps, place, 0)
            prep(shared_chunk(0, 0))
            with dve.Fori(1, B) as b:
                cs = [shared_chunk(b - 1, j) for j in range(GB)] + [shared_chunk(b, 0)]
                for j in range(GB):
                    body(cs[j - 1] if j else None, cs[j], cs[j + 1] if j < GB - 1 else None,
                         lambda place: beside(steps, 2 * FM * j + place, b))
                low(cs[GB - 1], FM - 1)
                prep(cs[GB])

            ch = Chain(dve, r_chain, 0)
            over_e = lambda a: a.rearrange("p (a t) -> p a t", a=1).broadcast_to([P, E, NT])
            over_t = lambda a: a.rearrange("p (e a) -> p e a", a=1).broadcast_to([P, E, NT])
            by_t = lambda a: a.rearrange("p e t -> p t e")
            flat = lambda a: a.rearrange("p e t -> p (e t)")
            best = rsmall[:, 3, :].rearrange("p (c t) -> p c t", c=2)
            pos = rsmall[:, 0, :].rearrange("p (c t) -> p c t", c=2)
            first = rsmall[:, 2, :].rearrange("p (c t) -> p c t", c=2)

            def pick_best(c):
                if c == 0:
                    dve.wait_ge(lg_ok, OPEN + NG)
                    dve.wait_ge(u_out, OPEN + 16 * NG)
                    dve.wait_ge(h_out, OPEN + 16 * NG)
                ch.link(v.tensor_reduce(best[:, c, :], by_t(lg[:, :, :]), AX.X, ALU.max))
                ch.link(v.tensor_tensor(rt, lg[:, :, :], over_e(best[:, c, :]), ALU.is_equal))

            def pick_first(c):
                ch.link(v.tensor_tensor(rt, rt, over_t(rank[:, :]), ALU.mult))
                ch.link(v.tensor_reduce(rsmall[:, 2, 0:NT], by_t(rt), AX.X, ALU.max))

            def mark(c):
                v.tensor_tensor(oh[:, c, :, :], rt, over_e(rsmall[:, 2, 0:NT]), ALU.is_equal).then_inc(r_oh, 1)
                dve.wait_ge(r_oh, c + 1)
                if c == 0:
                    ch.link(v.scalar_tensor_tensor(out=lg[:, :, :], in0=oh[:, 0, :, :], scalar=-BIG,
                                                   in1=lg[:, :, :], op0=ALU.mult, op1=ALU.add))
                else:
                    v.tensor_tensor(rsmall[:, 0, 0:NT], best[:, 1, :], best[:, 0, :], ALU.subtract).then_inc(r_d, 1)

            def gates_of(c):
                dve.wait_ge(r_ex, 1)
                ch.link(v.tensor_scalar(rsmall[:, 0, 0:NT], rsmall[:, 1, 0:NT], 1.0, None, ALU.add))
                ch.link(v.reciprocal(gates[:, 0, :], rsmall[:, 0, 0:NT]))
                ch.link(v.tensor_tensor(gates[:, 1, :], gates[:, 0, :], rsmall[:, 1, 0:NT], ALU.mult))

            def scan(c):
                dve.wait_ge(r_cnt, (2, 4)[c])
                ch.link(v.tensor_tensor_scan(rincl, flat(carry[:, :, :]), bank[4][:, 0:E * NT], 0.0,
                                             ALU.mult, ALU.add))
                v.tensor_tensor(flat(rt), rincl, bank[4][:, 0:E * NT], ALU.subtract).then_inc(r_scan, 1)
                dve.wait_ge(r_scan, c + 1)

            def within(c):
                if c == 0:
                    ch.link(v.tensor_copy(total[:, :], rincl.rearrange("p (e t) -> p e t", e=E)[:, :, NT - 1]))
                    ch.link(v.tensor_tensor(flat(rt), flat(rt), bank[5][:, 0:E * NT], ALU.add))
                else:
                    ch.link(v.tensor_tensor(rt, rt, over_t(total[:, :]), ALU.add))
                    v.tensor_tensor(flat(rt), flat(rt), bank[6][:, 0:E * NT], ALU.add).then_inc(r_scan, 1)
                    dve.wait_ge(r_scan, 3)

            def queue(c):
                ch.link(v.tensor_tensor(rt, rt, oh[:, c, :, :], ALU.mult))
                ch.link(v.tensor_reduce(pos[:, c, :], by_t(rt), AX.X, ALU.add))

            def column(c):
                ch.link(v.tensor_tensor(rt, over_t(estep[:, :]), oh[:, c, :, :], ALU.mult))
                ch.link(v.tensor_reduce(first[:, c, :], by_t(rt), AX.X, ALU.add))

            def tile_of(_):
                ch.link(v.tensor_scalar(slotcol[:, :, :], pos, float(P), None, ALU.is_ge))
                for j in range(2, ST):
                    ch.link(v.scalar_tensor_tensor(out=slotcol[:, :, :], in0=pos, scalar=float(P * j),
                                                   in1=slotcol[:, :, :], op0=ALU.is_ge, op1=ALU.add))

            def slot_of(_):
                ch.link(v.scalar_tensor_tensor(out=slotm[:, :, :], in0=slotcol[:, :, :], scalar=-float(P), in1=pos,
                                               op0=ALU.mult, op1=ALU.add))
                ch.link(v.tensor_scalar(best, pos, float(CAP), None, ALU.is_lt))
                for s in range(2):
                    dve.wait_ge(x2_out[s], OPEN + 16 * (NG // 2))
                v.scalar_tensor_tensor(out=slotm[:, :, :], in0=slotm[:, :, :], scalar=1.0, in1=best,
                                       op0=ALU.add, op1=ALU.mult).then_inc(r_slots, 1)
                ch.link(v.tensor_tensor(slotcol[:, :, :], slotcol[:, :, :], first, ALU.add))

            routing = {0: ((pick_best, 0), (pick_first, 0)), 1: ((mark, 0),), 2: ((pick_best, 1), (pick_first, 1)),
                       3: ((mark, 1),), 4: ((scan, 0),), 5: ((within, 0),), 6: ((gates_of, 0), (queue, 0)),
                       7: ((column, 0),), 8: ((scan, 1), (within, 1)), 9: ((queue, 1), (column, 1)),
                       10: ((tile_of, 0),), 11: ((slot_of, 0),)}

            def select(n):
                r, c, cut = n % SR, n % 2, slice(n // 2 * RB, (n // 2 + 1) * RB)
                if n >= SR:
                    dve.wait_ge(r_mm, n - SR + 1)
                v.tensor_tensor(selE[:, r, :, :], across(colid[:, :], NC), along(slotcol[:, c, cut], NC),
                                ALU.is_equal).then_inc(r_selE, 1)
                v.tensor_tensor(selA[:, r, :, :], across(slot1[:, :], P), along(slotm[:, c, cut], P),
                                ALU.is_equal).then_inc(r_selA, 1)

            def indices():
                dve.wait_ge(r_mm, NBLK)
                ch.link(v.tensor_copy(table2[:, :], bank[6][:, 0:2 * NC]))
                v.tensor_scalar(gidx[:, :], table2[:, 0:NC], -1.0, 0.0, ALU.add, ALU.max)
                ch.link(v.tensor_scalar(tabe[:, :], table2[:, 0:NC], 0.0, None, ALU.is_equal))
                ch.link(v.tensor_tensor(tabe[:, :], tabe[:, :], spare[:, :, :].rearrange("p e s -> p (e s)"),
                                        ALU.mult))
                ch.link(v.tensor_tensor(tabe[:, :], tabe[:, :], table2[:, 0:NC], ALU.add))
                v.tensor_scalar(sidx[:, :], tabe[:, :], -1.0, None, ALU.add).then_inc(r_idx, 1)

            def route(place):
                for step, c in routing.get(place, ()):
                    step(c)
                for n in blocks_at(place):
                    select(n)
                if place == R_IDX:
                    indices()

            cs = last_chunks()
            body(None, cs[0], cs[1], lambda place: beside_last(steps, route, place))
            body(cs[0], cs[1], None, lambda place: beside_last(steps, route, 2 * FM + place))
            low(cs[1], FM - 1)
            for place in range(2 * FM * (GB - HELD) - LEAD, R_IDX + 1):
                route(place)
            prep(expert_chunk(0, 0, 1))
            routed_chunks(dve, body)

            def last_stats(g):
                y = last_y[g % TY]
                dve.wait_ge(t_y[g % TY], 16 * (g // TY + 1))
                if g >= FIRST:
                    dve.wait_ge(y_sb, OPEN + NCH - HELD + (g - FIRST) + 1)
                    v.tensor_tensor(flat4(y), flat4(y), flat4(ysb[:, g - FIRST, :, :]), ALU.add).then_inc(t_sum, 1)
                    dve.wait_ge(t_sum, g - FIRST + 1)
                stats(Chain(dve, t_chain, 2 * g), lambda t: y[:, t, :], st, mv)
                v.tensor_scalar(veA[:, :], mv[:, :, 1], EPS, None, ALU.add).then_inc(t_var, 1)

            def last_bias(g):
                dve.wait_ge(t_rstd, g + 1)
                v.scalar_tensor_tensor(out=nbias[:, :], in0=mv[:, :, 0], scalar=-1.0, in1=t_scale[g % 2],
                                       op0=ALU.mult, op1=ALU.mult).then_inc(t_nb, 1)

            def last_pass(place):
                if place >= LAST0:
                    g = (place - LAST0) // 2
                    if place % 2 == 0:
                        last_stats(g)
                    else:
                        if g > 0:
                            last_add(v, dve, g - 1, DVE_TILES, t_ok)
                        last_bias(g)
            held_chunks(body, last_pass)
            low(held_chunk(1), FM - 1)
            for g in range(IN_HELD, NG):
                last_stats(g)
                last_add(v, dve, g - 1, DVE_TILES, t_ok)
                last_bias(g)
            last_add(v, dve, NG - 1, DVE_TILES, t_ok)


_INS = ['L0_attn_x', 'L0_attn_Wqk', 'L0_attn_Wv', 'L0_attn_Wo', 'L0_attn_tau', 'L0_ffn_ln_g', 'L0_ffn_ln_b',
        'L0_ffn_Wr', 'L0_ffn_W1', 'L0_ffn_W3', 'L0_ffn_W2', 'L0_ffn_W1s', 'L0_ffn_W3s', 'L0_ffn_W2s']


def kernel(**inputs):
    import numpy as _np
    import concourse.bacc as _bacc
    from concourse import mybir as _mybir
    from concourse.bass_utils import run_bass_kernel_spmd as _run

    nc = _bacc.Bacc("TRN2", target_bir_lowering=False, num_devices=1)
    arrays, args = {}, []
    for name in _INS:
        a = _np.ascontiguousarray(inputs[name])
        arrays[f"in_{name}_dram"] = a
        args.append(nc.dram_tensor(f"in_{name}_dram", a.shape, _mybir.dt.from_np(a.dtype), kind="ExternalInput").ap())
    shape = arrays["in_L0_attn_x_dram"].shape
    args.append(nc.dram_tensor("out_0_dram", shape, _mybir.dt.float32, kind="ExternalOutput").ap())
    sandwich_kernel(nc, *args)
    r = _run(nc, [arrays], core_ids=[0])
    return r.results[0]["out_0_dram"]
```
